# Optimizing a Trainium2 kernel written in Bass

```python
import numpy as np
import jax
import jax.numpy as jnp

def _softmax(x, axis=-1):
    return jax.nn.softmax(x, axis=axis)

def _gelu(x):
    return jax.nn.gelu(x, approximate=True)

def _silu(x):
    return jax.nn.silu(x)

def _sigmoid(x):
    return jax.nn.sigmoid(x)

def _layernorm(x, axis=-1, eps=1e-05):
    m = jnp.mean(x, axis=axis, keepdims=True)
    v = jnp.var(x, axis=axis, keepdims=True)
    return (x - m) / jnp.sqrt(v + eps)

def _scatter_add(tgt, idx, src, axis=0):
    return tgt.at[idx].add(src)

def _segment_sum(src, seg, n):
    return jax.ops.segment_sum(src, seg, n)
kernel_name = 'mk_seq_preln_d2_jaxref_r4_4d40c8'

def setup_inputs(seed: int=0):
    np.random.seed(seed)
    _w = jnp.asarray

    def _L0_attn_setup():
        import jax, jax.numpy as jnp
        import numpy as np
        MODEL_DIM = 256
        NUM_HEADS = 16
        D_K = MODEL_DIM // NUM_HEADS
        MAX_SEQ_LEN = 800
        B, T = (2, 512)
        THETA_BASE = 10000.0
        key = jax.random.key(seed)
        ks = jax.random.split(key, 5)
        scale = 1.0 / np.sqrt(MODEL_DIM)
        x = jax.random.normal(ks[0], (B, T, MODEL_DIM), dtype=jnp.float32)
        wq = jax.random.normal(ks[1], (MODEL_DIM, MODEL_DIM), dtype=jnp.float32) * scale
        wk = jax.random.normal(ks[2], (MODEL_DIM, MODEL_DIM), dtype=jnp.float32) * scale
        wv = jax.random.normal(ks[3], (MODEL_DIM, MODEL_DIM), dtype=jnp.float32) * scale
        wo = jax.random.normal(ks[4], (MODEL_DIM, MODEL_DIM), dtype=jnp.float32) * scale
        bq = jnp.zeros((MODEL_DIM,), jnp.float32)
        bk = jnp.zeros((MODEL_DIM,), jnp.float32)
        bv = jnp.zeros((MODEL_DIM,), jnp.float32)
        bo = jnp.zeros((MODEL_DIM,), jnp.float32)
        theta = THETA_BASE ** (jnp.arange(D_K // 2, dtype=jnp.float32) * (-2.0 / D_K))
        ang = jnp.outer(jnp.arange(MAX_SEQ_LEN, dtype=jnp.float32), theta)
        ang = jnp.repeat(ang, 2, axis=-1)
        return {'x': x, 'wq': wq, 'bq': bq, 'wk': wk, 'bk': bk, 'wv': wv, 'bv': bv, 'wo': wo, 'bo': bo, 'cos': jnp.cos(ang), 'sin': jnp.sin(ang)}
    _L0_attn_in = _L0_attn_setup()

    def _L0_ffn_setup():
        import jax, jax.numpy as jnp
        import numpy as np
        S, B, H = (512, 1, 256)
        E, K, F = (8, 2, 352)
        key = jax.random.key(seed)
        k1, k2, k3, k4 = jax.random.split(key, 4)
        return {'hidden_states': jax.random.normal(k1, (S, B, H), jnp.float32), 'router_weight': jax.random.normal(k2, (H, E), jnp.float32) * 0.02, 'w1': jax.random.normal(k3, (E, H, 2 * F), jnp.float32) * 0.02, 'w2': jax.random.normal(k4, (E, F, H), jnp.float32) * 0.02}
    _L0_ffn_in = _L0_ffn_setup()

    def _L1_attn_setup():
        import jax, jax.numpy as jnp
        import numpy as np
        D_MODEL = 256
        D_INNER = 2 * D_MODEL
        D_STATE = 16
        D_CONV = 4
        DT_RANK = (D_MODEL + 15) // 16
        B_SZ, L_SEQ = (2, 512)
        LN_EPS = 1e-06

        def _mamba_block(x, ln_g, ln_b, W_in, conv_w, conv_b, W_x, W_dt, b_dt, A_log, Dp, W_out):
            B, L, D = x.shape
            mu = jnp.mean(x, axis=-1, keepdims=True)
            var = jnp.mean(jnp.square(x - mu), axis=-1, keepdims=True)
            h = (x - mu) * jax.lax.rsqrt(var + LN_EPS) * ln_g + ln_b
            xz = jnp.einsum('bld,ed->ble', h, W_in)
            xi, z = jnp.split(xz, 2, axis=-1)
            xc = jnp.transpose(xi, (0, 2, 1))
            xc = jax.lax.conv_general_dilated(xc, conv_w, window_strides=(1,), padding=[(D_CONV - 1, 0)], feature_group_count=D_INNER, dimension_numbers=('NCH', 'OIH', 'NCH'))
            xc = xc + conv_b[None, :, None]
            u = jax.nn.silu(jnp.transpose(xc, (0, 2, 1)))
            x_dbl = jnp.einsum('bld,ed->ble', u, W_x)
            dt = x_dbl[..., :DT_RANK]
            Bm = x_dbl[..., DT_RANK:DT_RANK + D_STATE]
            Cm = x_dbl[..., DT_RANK + D_STATE:]
            dt = jnp.einsum('blr,dr->bld', dt, W_dt)
            dt = jax.nn.softplus(dt + b_dt)
            A = -jnp.exp(A_log.astype(jnp.float32))
            dA = jnp.exp(jnp.einsum('bld,dn->bldn', dt, A))
            dBu = jnp.einsum('bld,bln->bldn', dt * u, Bm)

            def step(hst, inp):
                dA_t, dBu_t, C_t = inp
                hst = dA_t * hst + dBu_t
                y_t = jnp.einsum('bdn,bn->bd', hst, C_t)
                return (hst, y_t)
            h0 = jnp.zeros((B, D_INNER, D_STATE), dt.dtype)
            _, ys = jax.lax.scan(step, h0, (jnp.swapaxes(dA, 0, 1), jnp.swapaxes(dBu, 0, 1), jnp.swapaxes(Cm, 0, 1)))
            y = jnp.swapaxes(ys, 0, 1)
            y = y + u * Dp
            y = y * jax.nn.silu(z)
            out = jnp.einsum('bld,ed->ble', y, W_out)
            return x + out
        key = jax.random.key(seed)
        ks = jax.random.split(key, 12)
        s = 0.02
        x = jax.random.normal(ks[0], (B_SZ, L_SEQ, D_MODEL), jnp.float32)
        ln_g = jnp.ones((D_MODEL,), jnp.float32)
        ln_b = jnp.zeros((D_MODEL,), jnp.float32)
        W_in = jax.random.normal(ks[1], (2 * D_INNER, D_MODEL), jnp.float32) * s
        conv_w = jax.random.normal(ks[2], (D_INNER, 1, D_CONV), jnp.float32) * 0.2
        conv_b = jax.random.normal(ks[3], (D_INNER,), jnp.float32) * 0.02
        W_x = jax.random.normal(ks[4], (DT_RANK + 2 * D_STATE, D_INNER), jnp.float32) * s
        W_dt = jax.random.normal(ks[5], (D_INNER, DT_RANK), jnp.float32) * DT_RANK ** (-0.5)
        u = jax.random.uniform(ks[6], (D_INNER,), jnp.float32)
        dt0 = jnp.exp(u * (np.log(0.1) - np.log(0.001)) + np.log(0.001))
        b_dt = dt0 + jnp.log(-jnp.expm1(-dt0))
        A_log = jnp.log(jnp.tile(jnp.arange(1, D_STATE + 1, dtype=jnp.float32), (D_INNER, 1)))
        Dp = jnp.ones((D_INNER,), jnp.float32)
        W_out = jax.random.normal(ks[7], (D_MODEL, D_INNER), jnp.float32) * s
        return {'x': x, 'ln_g': ln_g, 'ln_b': ln_b, 'W_in': W_in, 'conv_w': conv_w, 'conv_b': conv_b, 'W_x': W_x, 'W_dt': W_dt, 'b_dt': b_dt, 'A_log': A_log, 'Dp': Dp, 'W_out': W_out}
    _L1_attn_in = _L1_attn_setup()

    def _L1_ffn_setup():
        import jax, jax.numpy as jnp
        import numpy as np
        B, S, D, E, K = (4, 512, 256, 8, 2)
        EPS, W_THRES, TEMP = (0.0001, 0.1, 1.0)
        key = jax.random.key(seed)
        k1, k2, k3, k4, k5 = jax.random.split(key, 5)
        x = jax.random.normal(k1, (B, S, D), dtype=jnp.float32)
        gate_W = jax.random.normal(k2, (D, E), dtype=jnp.float32) * 0.02
        gate_b = jnp.zeros((E,), dtype=jnp.float32)
        expert_W = jax.random.normal(k3, (E, D, D), dtype=jnp.float32) * 0.02
        expert_b = jnp.zeros((E, D), dtype=jnp.float32)
        return {'x': x, 'gate_W': gate_W, 'gate_b': gate_b, 'expert_W': expert_W, 'expert_b': expert_b}
    _L1_ffn_in = _L1_ffn_setup()
    _d = {'L0_attn_x': _L0_attn_in['x'], 'L0_attn_wq': _L0_attn_in['wq'], 'L0_attn_bq': _L0_attn_in['bq'], 'L0_attn_wk': _L0_attn_in['wk'], 'L0_attn_bk': _L0_attn_in['bk'], 'L0_attn_wv': _L0_attn_in['wv'], 'L0_attn_bv': _L0_attn_in['bv'], 'L0_attn_wo': _L0_attn_in['wo'], 'L0_attn_bo': _L0_attn_in['bo'], 'L0_attn_cos': _L0_attn_in['cos'], 'L0_attn_sin': _L0_attn_in['sin'], 'L0_ffn_router_weight': _L0_ffn_in['router_weight'], 'L0_ffn_w1': _L0_ffn_in['w1'], 'L0_ffn_w2': _L0_ffn_in['w2'], 'L1_attn_ln_g': _L1_attn_in['ln_g'], 'L1_attn_ln_b': _L1_attn_in['ln_b'], 'L1_attn_W_in': _L1_attn_in['W_in'], 'L1_attn_conv_w': _L1_attn_in['conv_w'], 'L1_attn_conv_b': _L1_attn_in['conv_b'], 'L1_attn_W_x': _L1_attn_in['W_x'], 'L1_attn_W_dt': _L1_attn_in['W_dt'], 'L1_attn_b_dt': _L1_attn_in['b_dt'], 'L1_attn_A_log': _L1_attn_in['A_log'], 'L1_attn_Dp': _L1_attn_in['Dp'], 'L1_attn_W_out': _L1_attn_in['W_out'], 'L1_ffn_gate_W': _L1_ffn_in['gate_W'], 'L1_ffn_gate_b': _L1_ffn_in['gate_b'], 'L1_ffn_expert_W': _L1_ffn_in['expert_W'], 'L1_ffn_expert_b': _L1_ffn_in['expert_b']}
    _x0 = _d['L0_attn_x']
    _d['L0_attn_x'] = jax.random.normal(jax.random.fold_in(jax.random.key(seed), 1), (8, 512, 256), dtype=_x0.dtype)
    del _x0
    return _d

def reference(L0_attn_x, L0_attn_wq, L0_attn_bq, L0_attn_wk, L0_attn_bk, L0_attn_wv, L0_attn_bv, L0_attn_wo, L0_attn_bo, L0_attn_cos, L0_attn_sin, L0_ffn_router_weight, L0_ffn_w1, L0_ffn_w2, L1_attn_ln_g, L1_attn_ln_b, L1_attn_W_in, L1_attn_conv_w, L1_attn_conv_b, L1_attn_W_x, L1_attn_W_dt, L1_attn_b_dt, L1_attn_A_log, L1_attn_Dp, L1_attn_W_out, L1_ffn_gate_W, L1_ffn_gate_b, L1_ffn_expert_W, L1_ffn_expert_b):

    def _L0_attn_ref(x, wq, bq, wk, bk, wv, bv, wo, bo, cos, sin):
        import jax, jax.numpy as jnp
        import numpy as np
        MODEL_DIM = 256
        NUM_HEADS = 16
        D_K = MODEL_DIM // NUM_HEADS
        MAX_SEQ_LEN = 800
        B, T = (2, 512)
        THETA_BASE = 10000.0
        b, t, dm = x.shape
        h, d = (NUM_HEADS, dm // NUM_HEADS)
        xq = (x @ wq.T + bq).reshape(b, h, t, d)
        xk = (x @ wk.T + bk).reshape(b, h, t, d)
        xv = (x @ wv.T + bv).reshape(b, h, t, d)

        def rot_half(q):
            q2 = q.reshape(b, h, t, d // 2, 2)
            return jnp.stack([-q2[..., 1], q2[..., 0]], axis=-1).reshape(b, h, t, d)
        c = cos[t]
        s = sin[t]
        xq = xq * c + rot_half(xq) * s
        xk = xk * c + rot_half(xk) * s
        scores = jnp.einsum('bhqd,bhkd->bhqk', xq, xk) / np.sqrt(d)
        p = jax.nn.softmax(scores, axis=-1)
        o = jnp.einsum('bhqk,bhkd->bhqd', p, xv)
        o = o.transpose(0, 2, 1, 3).reshape(b, t, dm)
        return o @ wo.T + bo

    def _L0_ffn_ref(hidden_states, router_weight, w1, w2):
        import jax, jax.numpy as jnp
        import numpy as np
        S, B, H = (512, 1, 256)
        E, K, F = (8, 2, 352)
        s, b, h = hidden_states.shape
        x = hidden_states.reshape(-1, h)
        logits = x @ router_weight
        probs = jax.nn.softmax(logits, axis=-1)
        _, topk_idx = jax.lax.top_k(probs, K)
        routing_map = jax.nn.one_hot(topk_idx, E, dtype=probs.dtype).sum(axis=1)
        local_probs = probs * routing_map
        y = jnp.einsum('th,ehf->tef', x, w1)
        y1, y2 = jnp.split(y, 2, axis=-1)
        g = jax.nn.silu(y1) * y2
        o = jnp.einsum('tef,efh->teh', g, w2)
        out = jnp.einsum('teh,te->th', o, local_probs)
        return out.reshape(s, b, h)

    def _L1_attn_ref(x, ln_g, ln_b, W_in, conv_w, conv_b, W_x, W_dt, b_dt, A_log, Dp, W_out):
        import jax, jax.numpy as jnp
        import numpy as np
        D_MODEL = 256
        D_INNER = 2 * D_MODEL
        D_STATE = 16
        D_CONV = 4
        DT_RANK = (D_MODEL + 15) // 16
        B_SZ, L_SEQ = (2, 512)
        LN_EPS = 1e-06

        def _mamba_block(x, ln_g, ln_b, W_in, conv_w, conv_b, W_x, W_dt, b_dt, A_log, Dp, W_out):
            B, L, D = x.shape
            mu = jnp.mean(x, axis=-1, keepdims=True)
            var = jnp.mean(jnp.square(x - mu), axis=-1, keepdims=True)
            h = (x - mu) * jax.lax.rsqrt(var + LN_EPS) * ln_g + ln_b
            xz = jnp.einsum('bld,ed->ble', h, W_in)
            xi, z = jnp.split(xz, 2, axis=-1)
            xc = jnp.transpose(xi, (0, 2, 1))
            xc = jax.lax.conv_general_dilated(xc, conv_w, window_strides=(1,), padding=[(D_CONV - 1, 0)], feature_group_count=D_INNER, dimension_numbers=('NCH', 'OIH', 'NCH'))
            xc = xc + conv_b[None, :, None]
            u = jax.nn.silu(jnp.transpose(xc, (0, 2, 1)))
            x_dbl = jnp.einsum('bld,ed->ble', u, W_x)
            dt = x_dbl[..., :DT_RANK]
            Bm = x_dbl[..., DT_RANK:DT_RANK + D_STATE]
            Cm = x_dbl[..., DT_RANK + D_STATE:]
            dt = jnp.einsum('blr,dr->bld', dt, W_dt)
            dt = jax.nn.softplus(dt + b_dt)
            A = -jnp.exp(A_log.astype(jnp.float32))
            dA = jnp.exp(jnp.einsum('bld,dn->bldn', dt, A))
            dBu = jnp.einsum('bld,bln->bldn', dt * u, Bm)

            def step(hst, inp):
                dA_t, dBu_t, C_t = inp
                hst = dA_t * hst + dBu_t
                y_t = jnp.einsum('bdn,bn->bd', hst, C_t)
                return (hst, y_t)
            h0 = jnp.zeros((B, D_INNER, D_STATE), dt.dtype)
            _, ys = jax.lax.scan(step, h0, (jnp.swapaxes(dA, 0, 1), jnp.swapaxes(dBu, 0, 1), jnp.swapaxes(Cm, 0, 1)))
            y = jnp.swapaxes(ys, 0, 1)
            y = y + u * Dp
            y = y * jax.nn.silu(z)
            out = jnp.einsum('bld,ed->ble', y, W_out)
            return x + out
        return _mamba_block(x, ln_g, ln_b, W_in, conv_w, conv_b, W_x, W_dt, b_dt, A_log, Dp, W_out)

    def _L1_ffn_ref(x, gate_W, gate_b, expert_W, expert_b):
        import jax, jax.numpy as jnp
        import numpy as np
        B, S, D, E, K = (4, 512, 256, 8, 2)
        EPS, W_THRES, TEMP = (0.0001, 0.1, 1.0)
        scores = jnp.maximum((x @ gate_W + gate_b) / TEMP, EPS)
        p = jax.nn.softmax(scores, axis=-1)
        _, topk_idx = jax.lax.top_k(p, K)
        topk_mask = jax.nn.one_hot(topk_idx, E, dtype=p.dtype).sum(-2) > 0
        w = jnp.maximum(p, W_THRES)
        w_gather = jnp.take_along_axis(w, topk_idx, axis=-1)
        total = jax.lax.stop_gradient(w_gather.sum(-1, keepdims=True))
        w = w / total
        comb = jnp.where(topk_mask, w, jnp.zeros_like(w))
        y = jnp.einsum('bsd,edf->bsef', x, expert_W) + expert_b
        out = jnp.einsum('bsef,bse->bsf', y, comb) / K
        return out
    x = L0_attn_x
    x = x + _L0_attn_ref(_layernorm(x, axis=-1), L0_attn_wq, L0_attn_bq, L0_attn_wk, L0_attn_bk, L0_attn_wv, L0_attn_bv, L0_attn_wo, L0_attn_bo, L0_attn_cos, L0_attn_sin)
    x = x + _L0_ffn_ref(_layernorm(x, axis=-1), L0_ffn_router_weight, L0_ffn_w1, L0_ffn_w2)
    x = x + _L1_attn_ref(_layernorm(x, axis=-1), L1_attn_ln_g, L1_attn_ln_b, L1_attn_W_in, L1_attn_conv_w, L1_attn_conv_b, L1_attn_W_x, L1_attn_W_dt, L1_attn_b_dt, L1_attn_A_log, L1_attn_Dp, L1_attn_W_out)
    x = x + _L1_ffn_ref(_layernorm(x, axis=-1), L1_ffn_gate_W, L1_ffn_gate_b, L1_ffn_expert_W, L1_ffn_expert_b)
    return x

_drawn_inputs = setup_inputs


def setup_inputs(seed=0):
    import zlib

    import numpy as np

    out = dict(_drawn_inputs(seed))
    spreads = {'L0_attn_bq': (0.0, 0.1),
     'L0_attn_bk': (0.0, 0.1),
     'L0_attn_bv': (0.0, 0.1),
     'L0_attn_bo': (0.0, 0.1),
     'L1_attn_ln_g': (1.0, 0.2),
     'L1_attn_ln_b': (0.0, 0.1),
     'L1_attn_Dp': (1.0, 0.2),
     'L1_ffn_gate_b': (0.0, 0.1),
     'L1_ffn_expert_b': (0.0, 0.1)}
    factors = {}
    for name, (base, spread) in spreads.items():
        noise = np.random.default_rng([zlib.crc32(name.encode()), seed]).standard_normal(out[name].shape)
        drawn = base * np.exp(spread * noise) if base else spread * noise
        out[name] = jnp.asarray(drawn.astype(out[name].dtype))
    for name, factor in factors.items():
        out[name] = (out[name] * factor).astype(out[name].dtype)
    return out
```

```python
from contextlib import ExitStack

import numpy as np

import concourse.bass as bass
from concourse import mybir

ALU = mybir.AluOpType
ACT = mybir.ActivationFunctionType
AX = mybir.AxisListType
F32 = mybir.dt.float32
F32R = mybir.dt.float32r

P = 128
D = 256
NB, T = 8, 512
NT = NB * T // P
NH = 16
DK = D // NH
NJ = D // DK
SCALE = DK ** -0.5


def wait(eng, sem, value):
    if not isinstance(value, int) or value > 0:
        eng.wait_ge(sem, value)

def attention_phase(nc, all_sems, A, x_out):
    with ExitStack() as ctx:
        sb = lambda name, shape, dt=F32: ctx.enter_context(nc.sbuf_tensor("at_" + name, shape, dt))
        sem = lambda name: all_sems("at_" + name)
        x_in = A["x"]

        ident = sb("ident", [P, P])
        cosb, sinb, signb = (sb(n, [P, D]) for n in ("cosb", "sinb", "signb"))
        cols = sb("cols", [P, 11])
        bqk = sb("bqk", [P, 4])
        wraw = sb("wraw", [P, 2, 2, D])
        wrot = sb("wrot", [P, 2, D])
        w_hi = sb("w_hi", [P, 2, 2, D], F32R)
        w_lo = sb("w_lo", [P, 2, 2, D], F32R)
        wv = sb("wv", [P, 2, D])
        bvt = sb("bvt", [P, 64])
        wo = sb("wo", [P, 4, D])
        bo = sb("bo", [P, D])
        eps = sb("eps", [P, 1])

        xin = sb("xin", [P, 4, D])
        stats = sb("stats", [P, 6])
        mv = sb("mv", [P, 2, 2])
        rs = sb("rs", [P, 2, 4])
        xn = sb("xn", [P, D])
        xT = sb("xT", [P, 2, P])
        xT_hi = sb("xT_hi", [P, 2, P], F32R)
        xT_lo = sb("xT_lo", [P, 2, P], F32R)
        qk = sb("qk", [P, 4, P])
        qk_hi = sb("qk_hi", [P, 4, P], F32R)
        qk_lo = sb("qk_lo", [P, 4, P], F32R)
        qst = sb("qst", [P, 4, NJ, P], F32R)
        kst = sb("kst", [P, 4, NJ, P], F32R)
        vau = sb("vau", [P, 4, 4, 4, 32])
        mx = sb("mx", [P, 2, 16])
        nm = sb("nm", [4, 4, 32, 4])
        nm_hi = sb("nm_hi", [4, 4, 32, 4], F32R)
        nm_lo = sb("nm_lo", [4, 4, 32, 4], F32R)
        probs = sb("probs", [P, 2, 16, 512])
        oc = sb("oc", [P, 512])
        sums = sb("sums", [P, 512])
        rsum = sb("rsum", [P, 2, 512])
        oT = sb("oT", [P, 4, 512])
        xo = sb("xo", [P, 4, D])
        scr = nc.dram_tensor("at_scr", (4, 2, 2 * D, P), F32, kind="Internal").ap()

        s_ps = ctx.enter_context(nc.psum_tensor("at_s_ps", [P, 2, 2, 512], F32))
        t_ps = ctx.enter_context(nc.psum_tensor("at_t_ps", [P, 2, 512], F32))
        o_ps = ctx.enter_context(nc.psum_tensor("at_o_ps", [P, 512], F32))
        f_ps = ctx.enter_context(nc.psum_tensor("at_f_ps", [P, 512], F32))

        w_in, wprep, const_set = sem("w_in"), sem("wprep"), sem("const_set")
        x_loaded = [sem(f"x_loaded{r}") for r in range(4)]
        stats_done, aggr_done = sem("stats_done"), sem("aggr_done")
        ln_done, rsq_done = sem("ln_done"), sem("rsq_done")
        pool_chain = sem("pool_chain")
        xn_ready = sem("xn_ready")
        xT_ps_ready, xT_ready, xT_hi_ready, xT_lo_ready = (sem(n) for n in ("xT_ps_ready", "xT_ready", "xT_hi_ready", "xT_lo_ready"))
        qk_ps_ready, qk_ready, qk_hi_ready, qk_lo_ready = (sem(n) for n in ("qk_ps_ready", "qk_ready", "qk_hi_ready", "qk_lo_ready"))
        scr_written = sem("scr_written")
        stack_ready = [sem(f"stack_ready{r}") for r in range(4)]
        v_ps_ready, v_ready = sem("v_ps_ready"), sem("v_ready")
        s_ready, max_done = sem("s_ready"), sem("max_done")
        mT_ready, nm_made, nm_hi_ready, nm_ready, nm_rows = (sem(n) for n in ("mT_ready", "nm_made", "nm_hi_ready", "nm_ready", "nm_rows"))
        t_ready, exp_done, pv_done = sem("t_ready"), sem("exp_done"), sem("pv_done")
        oc_ready, sums_ready, lsum_done, rsum_ready, oT_ready = (sem(n) for n in ("oc_ready", "sums_ready", "lsum_done", "rsum_ready", "oT_ready"))
        xo_loaded, xo_biased, wo_ready, xo_ready, x_stored = (sem(n) for n in ("xo_loaded", "xo_biased", "wo_ready", "xo_ready", "x_stored"))

        def slots(eng, slot):
            for t in range(-6, 4):
                slot(t // 4, t % 4)
            with eng.Fori(1, NB - 2) as i:
                for g in range(4):
                    slot(i, g)
            for t in range(4 * (NB - 2), NT + 2):
                slot(t // 4, t % 4)

        def tile(i, g, lag):
            q = g + lag
            n = i + q // 4 if q // 4 else i
            t = 4 * n + q % 4
            if isinstance(t, int) and not 0 <= t < NT:
                return None
            return t, q % 4, n

        passed = all_sems("passed")

        def pass_on(eng, t):
            if not isinstance(t, int):
                eng.sem_inc(passed, 1)

        with nc.Block() as block:

            @block.sync
            def _(sp):
                first = [(ident, A["ident"]), (cosb, A["cosb"]), (sinb, A["sinb"]), (signb, A["signb"]),
                         (cols, A["at_cols"]), (wv, A["wvT"].rearrange("(k c) e -> c k e", k=2)),
                         (bvt, A["bvt"]), (wo, A["wo_pad"]), (bo, A["bo_rep"])]
                for dst, src in first:
                    sp.dma_start(dst[tuple(slice(None) for _ in dst.shape)], src).then_inc(w_in, 16)
                for m in range(2):
                    if m:
                        sp.wait_ge(wprep, 5)
                    for v, n in enumerate((("wqT", "wqTs"), ("wkT", "wkTs"))[m]):
                        sp.dma_start(wraw[:, v, :, :], A[n].rearrange("(k c) e -> c k e", k=2)).then_inc(w_in, 16)

                def slot(i, g):
                    if w := tile(i, g, 6):
                        t, r, n = w
                        wait(sp, xn_ready, t - 3)
                        sp.dma_start(xin[:, r, :], x_in[bass.ds(t * P, P), :].rearrange("(h k) c -> k h c", h=4)).then_inc(x_loaded[r], 16)
                    if w := tile(i, g, 1):
                        t, r, n = w
                        sp.wait_ge(const_set, 6)
                        sp.wait_ge(nm_ready, t + 1)
                        for row, src in ((48, nm_hi), (49, nm_lo)):
                            sp.dma_start(qst[row:row + 1, r, :, :].bitcast(F32).rearrange("o (c j) k -> o c (j k)", c=4),
                                         src[:, :, :, :].bitcast(F32).rearrange("c j k h -> c (j k h)")).then_inc(nm_rows, 16)
                    if w := tile(i, g, 3):
                        t, r, n = w
                        wait(sp, stack_ready[r], 96 * n)
                        pass_on(sp, t)
                        wait(sp, t_ready, 16 * (t - 3))
                        pass_on(sp, t)
                        for kind, src, ready, rows_q, rows_k in ((0, qk_hi, qk_hi_ready, (0, 32), (0, 16)),
                                                                 (1, qk_lo, qk_lo_ready, (16,), (32,))):
                            sp.wait_ge(ready, t + 1)
                            sp.dma_start(scr[r, kind].rearrange("(a p) t -> p a t", p=P), src[:, :, :].bitcast(F32)).then_inc(scr_written, 16)
                            sp.wait_ge(scr_written, 32 * t + 16 * (kind + 1))
                            for st, rows, col in ((qst, rows_q, 0), (kst, rows_k, D)):
                                for row in rows:
                                    sp.dma_start(st[row:row + 16, r, :, :].bitcast(F32),
                                                 scr[r, kind, col:col + D].rearrange("(j d) t -> d j t", d=DK)).then_inc(stack_ready[r], 16)
                    if g == 1 and (w := tile(i, g, -5)):
                        n = w[2]
                        sp.wait_ge(xo_ready, 2 * (n + 1))
                        sp.dma_start(x_out[bass.ds(n * 4 * P, 4 * P), :].rearrange("(k p) c -> p k c", p=P), xo[:, :, :]).then_inc(x_stored, 16)
                    if g == 0 and (w := tile(i, g, -4)):
                        n = w[2]
                        wait(sp, x_stored, 16 * n)
                        sp.dma_start(xo[:, :, :], x_in[bass.ds(n * 4 * P, 4 * P), :].rearrange("(k p) c -> p k c", p=P)).then_inc(xo_loaded, 16)

                slots(sp, slot)
                sp.wait_ge(x_stored, 16 * NB)

            @block.gpsimd
            def _(pool):
                fills = [(eps[:, :], 1e-5), (vau[:, :, :, :, :], 1.0), (qst[:, :, :, :].bitcast(F32), 0.0)]
                fills += [(kst[a:b, :, :, :].bitcast(F32), v) for a, b, v in ((0, 32, 0.0), (32, 64, 1.0), (64, P, 0.0))]
                for n, (dst, value) in enumerate(fills):
                    wait(pool, const_set, n)
                    pool.memset(dst, value).then_inc(const_set, 1)

                def chain(ins, count):
                    ins.then_inc(pool_chain, 1)
                    pool.wait_ge(pool_chain, count)

                def slot(i, g):
                    if w := tile(i, g, 1):
                        t = w[0]
                        pool.wait_ge(nm_hi_ready, t + 1)
                        wait(pool, nm_rows, 32 * t)
                        pool.tensor_tensor(nm_lo[:, :, :, :], nm[:, :, :, :], nm_hi[:, :, :, :], ALU.subtract).then_inc(nm_ready, 1)
                    if w := tile(i, g, 3):
                        t = w[0]
                        pool.wait_ge(qk_hi_ready, t + 1)
                        wait(pool, scr_written, 32 * t)
                        pool.tensor_tensor(qk_lo[:, :, :], qk[:, :, :], qk_hi[:, :, :], ALU.subtract).then_inc(qk_lo_ready, 1)
                    if w := tile(i, g, -1):
                        t, r, n = w
                        pool.wait_ge(rsum_ready, t + 1)
                        if r == 0:
                            wait(pool, wo_ready, 2 * n)
                        pool.tensor_tensor(oT[:, r, :].rearrange("p (k j) -> p j k", j=NJ), oc[:, :].rearrange("p (j k) -> p j k", j=NJ),
                                           rsum[:, 1, :].rearrange("p (j k) -> p j k", j=NJ), ALU.mult).then_inc(oT_ready, 1)
                    if w := tile(i, g, 5):
                        t, r, n = w
                        p = r % 2
                        pool.wait_ge(rsq_done, t + 1)
                        y, v, a, b = rs[:, p, 1:2], mv[:, p, 1:2], rs[:, p, 2:3], rs[:, p, 3:4]
                        chain(pool.tensor_tensor(a, y, y, ALU.mult), 5 * t + 1)
                        chain(pool.tensor_tensor(b, v, eps[:, :], ALU.add), 5 * t + 2)
                        chain(pool.tensor_tensor(a, a, b, ALU.mult), 5 * t + 3)
                        pass_on(pool, t)
                        chain(pool.tensor_scalar(a, a, -0.5, 1.5, ALU.mult, ALU.add), 5 * t + 4)
                        chain(pool.tensor_tensor(y, y, a, ALU.mult), 5 * t + 5)
                    if w := tile(i, g, 4):
                        t = w[0]
                        pool.wait_ge(xT_hi_ready, t + 1)
                        wait(pool, qk_ps_ready, t)
                        pool.tensor_tensor(xT_lo[:, :, :], xT[:, :, :], xT_hi[:, :, :], ALU.subtract).then_inc(xT_lo_ready, 1)
                    if g == 0 and (w := tile(i, g, -4)):
                        n = w[2]
                        pool.wait_ge(xo_loaded, 16 * (n + 1))
                        bo_all = bo[:, :].unsqueeze(1).broadcast_to([P, 4, D])
                        pool.tensor_tensor(xo[:, :, :], xo[:, :, :], bo_all, ALU.add).then_inc(xo_biased, 1)

                slots(pool, slot)

            @block.scalar
            def _(act):
                act.preload_act_table_set("natural_log_exp_and_others")
                act.wait_ge(const_set, 6)

                def exp(t, r, k):
                    act.wait_ge(t_ready, 16 * t + k + 1)
                    wait(act, pv_done, 4 * (t - 1))
                    act.activation(probs[:, r % 2, k, :], t_ps[:, k % 2, :], ACT.Exp, scale=SCALE).then_inc(exp_done, 1)

                def slot(i, g):
                    for k in range(16):
                        if w := tile(i, g, 0):
                            exp(w[0], w[1], k)
                        if k == 1 and (w := tile(i, g, 1)):
                            t = w[0]
                            act.wait_ge(mT_ready, t + 1)
                            wait(act, nm_ready, t)
                            wait(act, nm_rows, 32 * t)
                            m_ps = f_ps[0:4, :].rearrange("c (h j k) -> c j k h", h=4, j=4)
                            act.activation(nm[:, :, :, :], m_ps, ACT.Copy, scale=-1.0).then_inc(nm_made, 1)
                            act.activation(nm_hi[:, :, :, :], m_ps, ACT.Copy, scale=-1.0).then_inc(nm_hi_ready, 1)
                        if k == 1 and (w := tile(i, g, -1)):
                            t = w[0]
                            act.wait_ge(pv_done, 4 * t + 4)
                            wait(act, oT_ready, t)
                            act.activation(oc[:, :], o_ps[:, :], ACT.Copy).then_inc(oc_ready, 1)
                        if k == 4 and (w := tile(i, g, -1)):
                            t = w[0]
                            act.wait_ge(sums_ready, t + 1)
                            act.activation(rsum[:, 0, :], sums[:, :], ACT.Ln).then_inc(lsum_done, 1)
                            act.wait_ge(lsum_done, t + 1)
                            act.activation(rsum[:, 1, :], rsum[:, 0, :], ACT.Exp, scale=-1.0).then_inc(rsum_ready, 1)
                        if k == 5 and (w := tile(i, g, 3)):
                            t = w[0]
                            act.wait_ge(qk_ready, t + 1)
                            wait(act, scr_written, 32 * t)
                            act.activation(qk_hi[:, :, :], qk[:, :, :], ACT.Copy).then_inc(qk_hi_ready, 1)
                        if k == 9 and (w := tile(i, g, 5)):
                            t, r, n = w
                            p = r % 2
                            act.wait_ge(aggr_done, t + 1)
                            wait(act, xn_ready, t - 1)
                            act.activation(rs[:, p, 0:1], mv[:, p, 1:2], ACT.Ln, bias=eps[:, :]).then_inc(ln_done, 1)
                            act.wait_ge(ln_done, t + 1)
                            act.activation(rs[:, p, 1:2], rs[:, p, 0:1], ACT.Exp, scale=-0.5).then_inc(rsq_done, 1)
                        if k == 11 and (w := tile(i, g, 4)):
                            t = w[0]
                            act.wait_ge(xT_ps_ready, t + 1)
                            wait(act, xT_lo_ready, t)
                            wait(act, v_ps_ready, t)
                            t_in = f_ps[:, 0:2 * P].rearrange("p (k t) -> p k t", k=2)
                            act.activation(xT[:, :, :], t_in, ACT.Copy).then_inc(xT_ready, 1)
                            act.activation(xT_hi[:, :, :], t_in, ACT.Copy).then_inc(xT_hi_ready, 1)

                slots(act, slot)

            @block.vector
            def _(dve):
                done = [0]

                def link(ins):
                    done[0] += 1
                    ins.then_inc(wprep, 1)
                    dve.wait_ge(wprep, done[0])

                dve.wait_ge(w_in, 16 * 11)
                link(dve.tensor_tensor(sinb[:, :], sinb[:, :], signb[:, :], ALU.mult))
                for m in range(2):
                    if m:
                        dve.wait_ge(w_in, 16 * 13)
                    for kt in range(2):
                        link(dve.tensor_tensor(wraw[:, 1, kt, :], wraw[:, 1, kt, :], sinb[:, :], ALU.mult)) if kt == 0 else \
                            dve.tensor_tensor(wraw[:, 1, kt, :], wraw[:, 1, kt, :], sinb[:, :], ALU.mult).then_inc(wprep, 1)
                    done[0] += 1
                    cos2 = cosb[:, :].unsqueeze(1).broadcast_to([P, 2, D])
                    dve.wait_ge(wprep, done[0])
                    if m == 0:
                        link(dve.tensor_tensor(wrot[:, :, :], wraw[:, 0, :, :], cos2, ALU.mult))
                        link(dve.tensor_tensor(wrot[:, :, :], wrot[:, :, :], wraw[:, 1, :, :], ALU.add))
                    else:
                        link(dve.tensor_tensor(wrot[:, :, :], wraw[:, 0, :, :], cos2, ALU.mult))
                        link(dve.tensor_tensor(wrot[:, :, :], wrot[:, :, :], wraw[:, 1, :, :], ALU.add))
                    link(dve.tensor_copy(w_hi[:, m, :, :], wrot[:, :, :]))
                    link(dve.tensor_tensor(w_lo[:, m, :, :], wrot[:, :, :], w_hi[:, m, :, :], ALU.subtract))
                link(dve.tensor_tensor(cols[:, 9:10], cols[:, 9:10], cols[:, 10:11], ALU.mult))
                link(dve.tensor_scalar(cols[:, 4:8], cols[:, 4:8], cols[:, 9:10], None, ALU.mult))
                link(dve.tensor_scalar(bqk[:, :], cols[:, 0:4], cols[:, 8:9], None, ALU.mult))
                link(dve.tensor_tensor(bqk[:, :], bqk[:, :], cols[:, 4:8], ALU.add))
                dve.wait_ge(const_set, 6)

                def max_pair(t, m):
                    dve.wait_ge(s_ready, 8 * t + m + 1)
                    if m == 0:
                        wait(dve, mT_ready, t - 1)
                    h, c = m // 2, 2 * (m % 2)
                    out = mx[:, parity[0], 4 * h + c:4 * h + c + 2]
                    dve.tensor_reduce(out, s_ps[:, m % 2, :, :], AX.X, ALU.max).then_inc(max_done, 1)

                parity = [0]

                def project_out(n, part):
                    dve.wait_ge(xo_biased, n + 1)
                    dve.wait_ge(wo_ready, 2 * n + part + 1)
                    dve.tensor_tensor(xo[:, 2 * part:2 * part + 2, :], f_ps[:, :].rearrange("p (a c) -> p a c", a=2),
                                      xo[:, 2 * part:2 * part + 2, :], ALU.add).then_inc(xo_ready, 1)

                def slot(i, g):
                    ahead = tile(i, g, 2)

                    def mp(m):
                        if ahead:
                            parity[0] = ahead[1] % 2
                            max_pair(ahead[0], m)

                    if g == 1 and (w := tile(i, g, -5)):
                        project_out(w[2], 1)
                    mp(0)
                    if w := tile(i, g, 3):
                        t, r, n = w
                        dve.wait_ge(v_ps_ready, t + 1)
                        wait(dve, pv_done, 4 * (t - 3))
                        v_in = f_ps[:, 0:256].rearrange("p (h c d) -> p h c d", h=4, d=DK)
                        v_b = bvt[:, :].rearrange("p (c d) -> p c d", d=DK).unsqueeze(1).broadcast_to([P, 4, 4, DK])
                        dve.tensor_tensor(vau[:, r, :, :, 0:DK], v_in, v_b, ALU.add).then_inc(v_ready, 1)
                    if w := tile(i, g, -1):
                        t = w[0]
                        dve.wait_ge(oc_ready, t + 1)
                        wait(dve, lsum_done, t)
                        pass_on(dve, t)
                        dve.stream_shuffle(sums[:, :], oc[:, :], [16 + q % 16 for q in range(32)]).then_inc(sums_ready, 1)
                    mp(1)
                    if w := tile(i, g, 3):
                        t = w[0]
                        dve.wait_ge(qk_ps_ready, t + 1)
                        wait(dve, qk_lo_ready, t)
                        b_all = bqk[:, :].unsqueeze(2).broadcast_to([P, 4, P])
                        dve.tensor_tensor(qk[:, :, :], f_ps[:, :].rearrange("p (a t) -> p a t", a=4), b_all, ALU.add).then_inc(qk_ready, 1)
                    if w := tile(i, g, 5):
                        t, r, n = w
                        dve.wait_ge(x_loaded[r], 16 * (n + 1))
                        wait(dve, xn_ready, t - 1)
                        wait(dve, aggr_done, t)
                        dve.bn_stats(stats[:, :], xin[:, r, :]).then_inc(stats_done, 1)
                    mp(2)
                    mp(3)
                    if w := tile(i, g, 5):
                        t, r, n = w
                        dve.wait_ge(stats_done, t + 1)
                        pass_on(dve, t)
                        dve.bn_aggr(mv[:, r % 2, :], stats[:, :]).then_inc(aggr_done, 1)
                    mp(4)
                    mp(5)
                    mp(6)
                    if w := tile(i, g, 5):
                        t, r, n = w
                        dve.wait_ge(pool_chain, 5 * t + 5)
                        wait(dve, xT_ps_ready, t)
                        dve.tensor_scalar(xn[:, :], xin[:, r, :], mv[:, r % 2, 0:1], rs[:, r % 2, 1:2],
                                          ALU.subtract, ALU.mult).then_inc(xn_ready, 1)
                    mp(7)
                    if g == 0 and (w := tile(i, g, -4)):
                        project_out(w[2], 0)

                slots(dve, slot)

            @block.tensor
            def _(pe):
                pe.wait_ge(w_in, 16 * 13)
                pe.wait_ge(wprep, 17)
                pe.wait_ge(const_set, 6)

                def of_head(stack, r, h, chunk=None):
                    seq = stack[:, r, :, :].rearrange("r j (k h) -> r (j k) h", h=4)
                    return seq[:, :, h] if chunk is None else seq[:, chunk * P:(chunk + 1) * P, h]

                def scores_T(t, r, k):
                    c, h = k // 4, k % 4
                    wait(pe, exp_done, 16 * t + k - 1)
                    pe.matmul(t_ps[:, k % 2, :], of_head(kst, r, h, c), of_head(qst, r, h), start=True, stop=True).then_inc(t_ready, 1)

                def scores(t, r, m):
                    wait(pe, max_done, 8 * t + m - 1)
                    h, c = m // 2, 2 * (m % 2)
                    for a in range(2):
                        last = pe.matmul(s_ps[:, m % 2, a, :], of_head(qst, r, h, c + a), of_head(kst, r, h), start=True, stop=True)
                    last.then_inc(s_ready, 1)

                def values(t, r, c):
                    pe.wait_ge(exp_done, 16 * t + 4 * c + 4)
                    if c == 0:
                        wait(pe, oc_ready, t)
                        pe.wait_ge(v_ready, t + 1)
                    for h in range(4):
                        last = pe.matmul(o_ps[32 * h:32 * h + 32, :], vau[:, r, h, c, :], probs[:, r % 2, 4 * c + h, :],
                                         start=(c == 0), stop=(c == 3))
                    last.then_inc(pv_done, 1)

                def slot(i, g):
                    now, ahead, front, batch = tile(i, g, 0), tile(i, g, 2), tile(i, g, 3), tile(i, g, -4)
                    for k in range(16):
                        if now:
                            if k == 0:
                                pe.wait_ge(nm_rows, 32 * (now[0] + 1))
                            scores_T(now[0], now[1], k)
                        if ahead and k % 2 == 0:
                            if k == 0:
                                pe.wait_ge(stack_ready[ahead[1]], 96 * (ahead[2] + 1))
                            scores(ahead[0], ahead[1], k // 2)
                        if k == 1 and (w := tile(i, g, 1)):
                            t, r, n = w
                            wait(pe, xT_hi_ready, t + 3) if tile(i, g, 3) else None
                            if g == 1 and (b := tile(i, g, -5)):
                                pe.wait_ge(xo_ready, 2 * (b[2] + 1))
                            pe.wait_ge(max_done, 8 * t + 8)
                            for h in range(4):
                                last = pe.transpose(f_ps[0:4, h * P:(h + 1) * P], mx[:, r % 2, 4 * h:4 * h + 4], ident[:, :])
                            last.then_inc(mT_ready, 1)
                        if k == 1 and (w := tile(i, g, -1)):
                            for c in range(4):
                                values(w[0], w[1], c)
                        if k == 1 and front:
                            t = front[0]
                            wait(pe, nm_hi_ready, t - 1)
                            pe.wait_ge(xT_hi_ready, t + 1)
                            for h in range(4):
                                for kt in range(2):
                                    for jj in range(4):
                                        wv_j = wv[:, kt, :].rearrange("p (c j d) -> p j c d", c=4, j=4)[:, jj, :, :]
                                        last = pe.matmul(f_ps[32 * jj:32 * jj + 32, 64 * h:64 * h + 64],
                                                         xT[:, kt, :].rearrange("c (k h) -> c k h", h=4)[:, :, h],
                                                         wv_j, start=(kt == 0), stop=(kt == 1), skip_group_check=True)
                            last.then_inc(v_ps_ready, 1)
                        if k == 3 and front:
                            t = front[0]
                            pe.wait_ge(xT_lo_ready, t + 1)
                            pe.wait_ge(v_ready, t + 1)
                            for a in range(4):
                                m, et = a // 2, a % 2
                                parts = [(wt, xt, kt) for kt in range(2) for wt, xt in ((w_hi, xT_hi), (w_lo, xT_hi), (w_hi, xT_lo))]
                                for n3, (wt, xt, kt) in enumerate(parts):
                                    last = pe.matmul(f_ps[:, a * P:(a + 1) * P], wt[:, m, kt, et * P:(et + 1) * P], xt[:, kt, :],
                                                     start=(n3 == 0), stop=(n3 == 5))
                            last.then_inc(qk_ps_ready, 1)
                        if k == 10 and (w := tile(i, g, 4)):
                            t = w[0]
                            pe.wait_ge(xn_ready, t + 1)
                            wait(pe, qk_ready, t)
                            wait(pe, nm_hi_ready, t - 2)
                            for kt in range(2):
                                last = pe.transpose(f_ps[:, kt * P:(kt + 1) * P], xn[:, kt * P:(kt + 1) * P], ident[:, :])
                            last.then_inc(xT_ps_ready, 1)
                        if (g, k) in ((0, 14), (1, 0)) and (w := tile(i, g, -4 - g)):
                            n, part = w[2], g
                            if part == 0:
                                pe.wait_ge(oT_ready, 4 * n + 4)
                                if w := tile(i, g, 4):
                                    pe.wait_ge(xT_hi_ready, w[0] + 1)
                                else:
                                    pe.wait_ge(qk_ready, NT)
                            else:
                                pe.wait_ge(xo_ready, 2 * n + 1)
                            for a in range(2):
                                tok = slice((2 * part + a) * P, (2 * part + a + 1) * P)
                                for gg in range(4):
                                    last = pe.matmul(f_ps[:, a * D:(a + 1) * D], oT[:, gg, tok], wo[:, gg, :], start=(gg == 0), stop=(gg == 3))
                            last.then_inc(wo_ready, 1)

                slots(pe, slot)


class Steps:
    def __init__(self, eng, sem, per_batch):
        self.eng, self.sem, self.per_batch = eng, sem, per_batch

    def begin(self, n):
        self.base, self.count = n * self.per_batch, 0

    def mark(self, ins):
        ins.then_inc(self.sem, 1)
        self.count += 1

    def settle(self):
        self.eng.wait_ge(self.sem, self.base + self.count)

    def __call__(self, ins):
        self.mark(ins)
        self.settle()


def batch_slots(eng, slot):
    slot(-1, 1, (0, 0))
    slot(0, 0, (1, 1))
    with eng.Fori(0, (NB - 2) // 2) as i:
        slot(2 * i + 1, 1, (2 * i + 2, 0))
        slot(2 * i + 2, 0, (2 * i + 3, 1))
    slot(NB - 1, 1, None)


def dve_normalise(dve, steps, passed, x, xn, stats, mv, rs, eps, var_ready, rs_ready, xn_ready, n, part):
    if part == 0:
        for k in range(4):
            steps.mark(dve.bn_stats(stats[:, k, :], x[:, k, :]))
        for k in range(4):
            if k == 0:
                steps.settle()
                dve.sem_inc(passed, 1)
            ins = dve.bn_aggr(mv[:, k, :], stats[:, k, :])
            steps.mark(ins) if k < 3 else ins.then_inc(var_ready, 1)
    else:
        dve.wait_ge(rs_ready, n + 1)
        y, v, a, b = rs[:, 0, :], mv[:, :, 1], rs[:, 1, :], rs[:, 2, :]
        steps(dve.tensor_tensor(a, y, y, ALU.mult))
        steps(dve.tensor_scalar(b, v, eps, None, ALU.add))
        steps(dve.tensor_tensor(a, a, b, ALU.mult))
        steps(dve.tensor_scalar(a, a, -0.5, 1.5, ALU.mult, ALU.add))
        steps(dve.tensor_tensor(rs[:, 3, :], y, a, ALU.mult))
        for k in range(4):
            last = dve.tensor_scalar(xn[:, k, :], x[:, k, :], mv[:, k, 0:1], rs[:, 3, k:k + 1], ALU.subtract, ALU.mult)
        last.then_inc(xn_ready, 1)


def dve_top2(dve, steps, p, order, work, small):
    bc = lambda s: s.unsqueeze(2).broadcast_to([P, 4, 8])
    m, m1, c = work[:, 0], work[:, 1], work[:, 2]
    steps(dve.tensor_reduce(small[:, 0, :], p, AX.X, ALU.add))
    steps(dve.reciprocal(small[:, 1, :], small[:, 0, :]))
    steps(dve.tensor_tensor(p, p, bc(small[:, 1, :]), ALU.mult))
    left = p
    for r, mask in enumerate((m, m1)):
        steps(dve.tensor_reduce(small[:, 2, :], left, AX.X, ALU.max))
        steps(dve.tensor_tensor(c, left, bc(small[:, 2, :]), ALU.is_equal))
        steps(dve.tensor_tensor(c, c, order, ALU.mult))
        steps(dve.tensor_reduce(small[:, 3, :], c, AX.X, ALU.max))
        steps(dve.tensor_tensor(mask, c, bc(small[:, 3, :]), ALU.is_equal))
        if r == 0:
            left = work[:, 3]
            steps(dve.scalar_tensor_tensor(left, mask, -2.0, p, ALU.mult, ALU.add))
    steps(dve.tensor_tensor(m, m, m1, ALU.add))
    return m


def moe_swiglu_phase(nc, sem, A, x_in, x_out):
    E, F = 8, 352
    FT = [(0, 128), (128, 128), (256, 96)]
    N_STEPS = 4 + 3 + 5 + 1 + 15
    with ExitStack() as ctx:
        sb = lambda name, shape, dt=F32: ctx.enter_context(nc.sbuf_tensor("m0_" + name, shape, dt))
        ident = sb("ident", [P, P])
        w1_hi, w1_lo = (sb(f"w1_{s}", [P, E, 2, 2 * F], F32R) for s in ("hi", "lo"))
        w2_hi, w2_lo = (sb(f"w2_{s}", [P, E, 3, D], F32R) for s in ("hi", "lo"))
        rw = sb("rw", [P, 2, E])
        order = sb("order", [P, 4, E])
        eps = sb("eps", [P, 1])
        x = sb("x", [P, 2, 4, D])
        xn = sb("xn", [P, 4, D])
        stats, mv, rs = sb("stats", [P, 4, 6]), sb("mv", [P, 4, 2]), sb("rs", [P, 4, 4])
        xT = sb("xT", [P, 2, T])
        xT_hi, xT_lo = (sb(f"xT_{s}", [P, 2, 2, T], F32R) for s in ("hi", "lo"))
        p = sb("p", [P, 4, E])
        work, small = sb("work", [P, 4, 4, E]), sb("small", [P, 4, 4])
        prob = sb("prob", [P, 2, 4, E])
        raw = sb("raw", [P, 2, 3 * D])
        g = sb("g", [P, 2, T])
        g_hi, g_lo = (sb(f"g_{s_}", [P, 2, 3, T], F32R) for s_ in ("hi", "lo"))
        y_ps = ctx.enter_context(nc.psum_tensor("m0_y_ps", [P, 2, 2, T], F32))
        o_ps = ctx.enter_context(nc.psum_tensor("m0_o_ps", [P, 2, 2, D], F32))
        f_ps = ctx.enter_context(nc.psum_tensor("m0_f_ps", [P, 2, T], F32))

        names = """const_in w_hi w_ready x_stored steps var_ready ln_ready rs_ready xn_ready xT_ps xT_ready xT_hi_ready xT_lo_ready
                   logits z_ready exp_ready prob_ready y_ready silu_ready g_ready g_hi_ready g_lo_ready o_ready acc_done const_set"""
        (const_in, w_hi_s, w_ready, x_stored, steps_s, var_ready, ln_ready, rs_ready, xn_ready, xT_ps, xT_ready, xT_hi_ready, xT_lo_ready,
         logits, z_ready, exp_ready, prob_ready, y_ready, silu_ready, g_ready, g_hi_ready, g_lo_ready, o_ready, acc_done,
         const_set) = (sem("m0_" + q) for q in names.split())
        w_in = [sem(f"m0_w_in{r}") for r in range(2)]
        passed = sem("passed")
        x_loaded = [sem(f"m0_x_loaded{r}") for r in range(2)]

        def pieces(e):
            r3, f3 = F - 2 * P, lambda t, a, b: t[:, e, a:b, :]
            for j in range(3):
                r = (3 * e + j) % 2
                if j < 2:
                    yield r, [(raw[:, r, 0:2 * F], A["m0_w1"][e, j * P:(j + 1) * P], w1_hi[:, e, j, :], w1_lo[:, e, j, :])]
                else:
                    raw_3 = raw[:, r, :].rearrange("p (f c) -> p f c", f=3)
                    yield r, [(raw_3[:, 0:2, :], A["m0_w2"][e, 0:2 * P].rearrange("(k c) f -> c k f", k=2), f3(w2_hi, 0, 2), f3(w2_lo, 0, 2)),
                              (raw_3[0:r3, 2, :], A["m0_w2"][e, 2 * P:F], w2_hi[0:r3, e, 2, :], w2_lo[0:r3, e, 2, :])]

        def low(pool, n, b):
            pool.wait_ge(xT_ready, n + 1)
            pool.wait_ge(xT_hi_ready, n + 1)
            if not isinstance(n, int) or n > 1:
                pool.wait_ge(y_ready, 3 * E * (n - 1))
            pool.tensor_tensor(xT_lo[:, b, :, :], xT[:, :, :], xT_hi[:, b, :, :], ALU.subtract).then_inc(xT_lo_ready, 1)

        def f_ring(e, f):
            return (3 * e + f) % 2

        with nc.Block() as block:

            @block.sync
            def _(sp):
                sp.dma_start(x[:, 0, :, :], x_in[0:T, :].rearrange("(k p) c -> p k c", p=P)).then_inc(x_loaded[0], 16)
                for dst, src in ((ident[:, :], A["ident"]), (rw[:, :, :], A["m0_rw"]), (order[:, :, :], A["order"])):
                    sp.dma_start(dst, src).then_inc(const_in, 16)
                sp.dma_start(x[:, 1, :, :], x_in[T:2 * T, :].rearrange("(k p) c -> p k c", p=P)).then_inc(x_loaded[1], 16)
                for e in range(E):
                    for j, (r, parts) in enumerate(pieces(e)):
                        wait(sp, w_ready, 3 * e + j - 1)
                        for dst, src, _, _ in parts:
                            sp.dma_start(dst, src).then_inc(w_in[r], 16)

                def store(n, b):
                    sp.wait_ge(acc_done, 2 * E * (n + 1))
                    sp.dma_start(x_out[bass.ds(n * T, T), :].rearrange("(k p) c -> p k c", p=P), x[:, b, :, :]).then_inc(x_stored, 16)

                def slot(n, b, following):
                    if isinstance(n, int) and n < 1:
                        return
                    store(n - 1, 1 - b)
                    sp.wait_ge(x_stored, 16 * n)
                    if following:
                        n1, b1 = following
                        sp.dma_start(x[:, b1, :, :], x_in[bass.ds(n1 * T, T), :].rearrange("(k p) c -> p k c", p=P)).then_inc(x_loaded[b1], 16)

                batch_slots(sp, slot)
                store(NB - 1, 1)
                sp.wait_ge(x_stored, 16 * NB)

            @block.gpsimd
            def _(pool):
                pool.memset(eps[:, :], 1e-5).then_inc(const_set, 1)
                low(pool, 0, 0)
                for e in range(E):
                    for j, (r, parts) in enumerate(pieces(e)):
                        pool.wait_ge(w_hi_s, 3 * e + j + 1)
                        for src, _, hi, lo in parts:
                            last = pool.tensor_tensor(lo, src, hi, ALU.subtract)
                        last.then_inc(w_ready, 1)

                def slot(n, b, following):
                    if following and not (isinstance(n, int) and n < 0):
                        low(pool, *following)

                batch_slots(pool, slot)

            @block.scalar
            def _(act):
                def before(n, part):
                    if part == 0:
                        act.wait_ge(const_set, 1)
                        act.wait_ge(var_ready, n + 1)
                        wait(act, xn_ready, n)
                        act.activation(rs[:, 0, :], mv[:, :, 1], ACT.Ln, bias=eps[:, :]).then_inc(ln_ready, 1)
                        act.wait_ge(ln_ready, n + 1)
                        act.activation(rs[:, 0, :], rs[:, 0, :], ACT.Exp, scale=-0.5).then_inc(rs_ready, 1)
                    if part == 2:
                        act.wait_ge(z_ready, n + 1)
                        act.activation(p[:, :, :], p[:, :, :], ACT.Exp).then_inc(exp_ready, 1)

                def transposed(n, b):
                    act.wait_ge(xT_ps, n + 1)
                    wait(act, xT_lo_ready, n)
                    wait(act, logits, n)
                    if not isinstance(n, int) or n > 1:
                        act.wait_ge(y_ready, 3 * E * (n - 1))
                    act.activation(xT[:, :, :], f_ps[:, :, :], ACT.Copy).then_inc(xT_ready, 1)
                    act.activation(xT_hi[:, b, :, :], f_ps[:, :, :], ACT.Copy).then_inc(xT_hi_ready, 1)

                def upper(q, r, b2, f):
                    rows = FT[f][1]
                    act.wait_ge(g_ready, q + 1)
                    act.activation(g_hi[0:rows, b2, f, :], g[0:rows, r, :], ACT.Copy).then_inc(g_hi_ready, 1)

                def slot(n, b, following):
                    if isinstance(n, int) and n < 0:
                        before(0, 0)
                        transposed(0, 0)
                        before(0, 2)
                        return
                    for e in range(E):
                        if isinstance(n, int) and n == 0:
                            split_hi(e)
                        for f in range(3):
                            q = 3 * E * n + 3 * e + f
                            rows = FT[f][1]
                            act.wait_ge(y_ready, q + 1)
                            wait(act, g_lo_ready, q - 1)
                            act.activation(g[0:rows, f_ring(e, f), :], y_ps[0:rows, f_ring(e, f), 0, :], ACT.Silu).then_inc(silu_ready, 1)
                            if f == 0 and not (isinstance(n, int) and n == 0 and e < 2):
                                act.wait_ge(o_ready, 2 * (E * n + e - 1))
                            if f:
                                upper(q - 1, f_ring(e, f - 1), e % 2, f - 1)
                        upper(q, f_ring(e, 2), e % 2, 2)
                        if following:
                            if e == 2:
                                before(following[0], 0)
                            if e == 4:
                                transposed(*following)
                            if e == 6:
                                before(following[0], 2)

                def split_hi(e):
                    for j, (r, parts) in enumerate(pieces(e)):
                        before = sum(len(list(pieces(0))[q % 3][1]) for q in range(3 * e + j + 1) if q % 2 == r)
                        act.wait_ge(w_in[r], 16 * before)
                        for src, _, hi, _ in parts:
                            last = act.activation(hi, src, ACT.Copy)
                        last.then_inc(w_hi_s, 1)

                batch_slots(act, slot)

            @block.vector
            def _(dve):
                steps = Steps(dve, steps_s, N_STEPS)
                dve.wait_ge(const_in, 48)

                def before(n, b, part):
                    if part == 0:
                        steps.begin(n)
                        dve.wait_ge(x_loaded[b], 16 * ((n - b) // 2 + 1) if isinstance(n, int) else 8 * (n - b) + 16)
                        wait(dve, var_ready, n)
                        dve_normalise(dve, steps, passed, x[:, b], xn, stats, mv, rs, 1e-5, var_ready, rs_ready, xn_ready, n, 0)
                    if part == 1:
                        wait(dve, xT_ps, n)
                        dve_normalise(dve, steps, passed, x[:, b], xn, stats, mv, rs, 1e-5, var_ready, rs_ready, xn_ready, n, 1)
                    if part == 2:
                        z_in = f_ps[:, 0, 0:4 * E].rearrange("p (k e) -> p k e", k=4)
                        dve.wait_ge(logits, n + 1)
                        steps(dve.tensor_reduce(small[:, 0, :], z_in, AX.X, ALU.max))
                        dve.tensor_tensor(p[:, :, :], z_in, small[:, 0, :].unsqueeze(2).broadcast_to([P, 4, E]), ALU.subtract).then_inc(z_ready, 1)
                    if part == 3:
                        dve.wait_ge(exp_ready, n + 1)
                        mask = dve_top2(dve, steps, p[:, :, :], order[:, :, :], work, small)
                        dve.tensor_tensor(prob[:, b, :, :], p[:, :, :], mask, ALU.mult).then_inc(prob_ready, 1)
                        assert steps.count == N_STEPS, steps.count

                def accumulate(n, b, e):
                    if e == 0:
                        dve.wait_ge(prob_ready, n + 1)
                    for half in range(2):
                        q = 2 * (E * n + e) + half
                        dve.wait_ge(o_ready, q + 1)
                        wait(dve, acc_done, q - 1)
                        for a in range(2):
                            k = 2 * half + a
                            last = dve.scalar_tensor_tensor(x[:, b, k, :], o_ps[:, half, a, :], prob[:, b, k, e:e + 1], x[:, b, k, :], ALU.mult, ALU.add)
                        last.then_inc(acc_done, 1)

                def slot(n, b, following):
                    if isinstance(n, int) and n < 0:
                        for part in range(4):
                            before(0, 0, part)
                        return
                    for e in range(E):
                        for f in range(3):
                            q = 3 * E * n + 3 * e + f
                            rows, r = FT[f][1], f_ring(e, f)
                            dve.wait_ge(silu_ready, q + 1)
                            dve.tensor_tensor(g[0:rows, r, :], g[0:rows, r, :], y_ps[0:rows, r, 1, :], ALU.mult).then_inc(g_ready, 1)
                            if f == 0:
                                if e:
                                    accumulate(n, b, e - 1)
                                elif not (isinstance(n, int) and n == 0):
                                    accumulate(n - 1, 1 - b, E - 1)
                            dve.wait_ge(g_hi_ready, q + 1)
                            dve.tensor_tensor(g_lo[0:rows, e % 2, f, :], g[0:rows, r, :], g_hi[0:rows, e % 2, f, :], ALU.subtract).then_inc(g_lo_ready, 1)
                        if following and e in (2, 3, 5, 6):
                            before(*following, (2, 3, 5, 6).index(e))

                batch_slots(dve, slot)
                accumulate(NB - 1, 1, E - 1)

            @block.tensor
            def _(pe):
                pe.wait_ge(const_in, 48)

                def transposes(n):
                    pe.wait_ge(xn_ready, n + 1)
                    wait(pe, z_ready, n)
                    for kt in range(2):
                        for k in range(4):
                            last = pe.transpose(f_ps[:, kt, k * P:(k + 1) * P], xn[:, k, kt * P:(kt + 1) * P], ident[:, :])
                    last.then_inc(xT_ps, 1)

                def router(n):
                    pe.wait_ge(xT_hi_ready, n + 1)
                    for k in range(4):
                        for kt in range(2):
                            last = pe.matmul(f_ps[:, 0, k * E:(k + 1) * E], xT[:, kt, k * P:(k + 1) * P], rw[:, kt, :], start=(kt == 0), stop=(kt == 1))
                    last.then_inc(logits, 1)

                def up(n, b, e):
                    for f, (f0, rows) in enumerate(FT):
                        q = 3 * E * n + 3 * e + f
                        wait(pe, g_ready, q - 1)
                        for half in range(2):
                            cols = slice(half * F + f0, half * F + f0 + rows)
                            parts = [(w, xt, kt) for kt in range(2) for w, xt in ((w1_hi, xT_hi), (w1_lo, xT_hi), (w1_hi, xT_lo))]
                            for m, (w, xt, kt) in enumerate(parts):
                                last = pe.matmul(y_ps[0:rows, f_ring(e, f), half, :], w[:, e, kt, cols], xt[:, b, kt, :], start=(m == 0), stop=(m == 5))
                        last.then_inc(y_ready, 1)

                def down(n, e):
                    pe.wait_ge(g_lo_ready, 3 * E * n + 3 * e + 3)
                    for half in range(2):
                        wait(pe, acc_done, 2 * (E * n + e - 1) + half + 1)
                        for a in range(2):
                            tok = slice((2 * half + a) * P, (2 * half + a + 1) * P)
                            parts = [(gg, w, f) for f in range(3) for gg, w in ((g_hi, w2_hi), (g_lo, w2_hi), (g_hi, w2_lo))]
                            for m, (gg, w, f) in enumerate(parts):
                                rows = FT[f][1]
                                last = pe.matmul(o_ps[:, half, a, :], gg[0:rows, e % 2, f, tok], w[0:rows, e, f, :], start=(m == 0), stop=(m == 8))
                        last.then_inc(o_ready, 1)

                def slot(n, b, following):
                    if isinstance(n, int) and n < 0:
                        transposes(0)
                        router(0)
                        return
                    pe.wait_ge(xT_lo_ready, n + 1)
                    for e in range(E):
                        if isinstance(n, int) and n == 0:
                            pe.wait_ge(w_ready, 3 * (e + 1))
                        up(n, b, e)
                        if e:
                            down(n, e - 1)
                        elif not (isinstance(n, int) and n == 0):
                            down(n - 1, E - 1)
                        if following and e == 4:
                            transposes(following[0])
                        if following and e == 5:
                            router(following[0])

                batch_slots(pe, slot)
                down(NB - 1, E - 1)


def moe_linear_phase(nc, sem, A, x_in, x_out):
    E, PAIRS = 8, 4
    N_STEPS = 4 + 3 + 5 + 3 + 15 + 4
    with ExitStack() as ctx:
        sb = lambda name, shape, dt=F32: ctx.enter_context(nc.sbuf_tensor("m1_" + name, shape, dt))
        ident = sb("ident", [P, P])
        w_hi, w_lo = (sb(f"w_{s}", [P, PAIRS, 2, 2 * D], F32R) for s in ("hi", "lo"))
        raw = sb("raw", [P, PAIRS, 2, 2 * D])
        gw = sb("gw", [P, 2, E])
        gb = sb("gb", [P, E])
        eb = sb("eb", [E, D])
        order = sb("order", [P, 4, E])
        eps = sb("eps", [P, 1])
        x = sb("x", [P, 2, 4, D])
        xn = sb("xn", [P, 4, D])
        stats, mv, rs = sb("stats", [P, 4, 6]), sb("mv", [P, 4, 2]), sb("rs", [P, 4, 4])
        xT = sb("xT", [P, 2, T])
        xT_hi, xT_lo = (sb(f"xT_{s}", [P, 2, 2, T], F32R) for s in ("hi", "lo"))
        p = sb("p", [P, 4, E])
        work, small = sb("work", [P, 4, 4, E]), sb("small", [P, 4, 4])
        comb = sb("comb", [P, 2, 4, E])
        combT = sb("combT", [E, 2, T])
        f_ps = ctx.enter_context(nc.psum_tensor("m1_f_ps", [P, 2, T], F32))
        o_ps = ctx.enter_context(nc.psum_tensor("m1_o_ps", [P, 4, 2 * D], F32))
        b_ps = ctx.enter_context(nc.psum_tensor("m1_b_ps", [P, 2, 2 * D], F32))

        names = """const_in w_in w_hi w_ready x_stored steps var_ready ln_ready rs_ready xn_ready xT_ps xT_ready xT_hi_ready xT_lo_ready
                   logits z_ready exp_ready comb_ready combT_ps combT_ready b_ready b_added o_ready acc_done const_set"""
        (const_in, w_in, w_hi_s, w_ready, x_stored, steps_s, var_ready, ln_ready, rs_ready, xn_ready, xT_ps, xT_ready, xT_hi_ready, xT_lo_ready,
         logits, z_ready, exp_ready, comb_ready, combT_ps, combT_ready, b_ready, b_added, o_ready, acc_done, const_set) = (sem("m1_" + q) for q in names.split())
        passed = sem("passed")
        x_loaded = [sem(f"m1_x_loaded{r}") for r in range(2)]
        UNITS = 4 * PAIRS

        def low(pool, n, b):
            pool.wait_ge(xT_ready, n + 1)
            pool.wait_ge(xT_hi_ready, n + 1)
            if not isinstance(n, int) or n > 1:
                pool.wait_ge(o_ready, UNITS * (n - 1))
            pool.tensor_tensor(xT_lo[:, b, :, :], xT[:, :, :], xT_hi[:, b, :, :], ALU.subtract).then_inc(xT_lo_ready, 1)

        with nc.Block() as block:

            @block.sync
            def _(sp):
                sp.dma_start(x[:, 0, :, :], x_in[0:T, :].rearrange("(k p) c -> p k c", p=P)).then_inc(x_loaded[0], 16)
                for dst, src in ((ident[:, :], A["ident"]), (gw[:, :, :], A["m1_gw"]), (gb[:, :], A["m1_gb"]), (eb[:, :], A["m1_eb"]),
                                 (order[:, :, :], A["order"])):
                    sp.dma_start(dst, src).then_inc(const_in, 16)
                for e in range(PAIRS):
                    sp.dma_start(raw[:, e, :, :], A["m1_w"][e].rearrange("(k c) f -> c k f", k=2)).then_inc(w_in, 16)

                def store(n, b):
                    sp.wait_ge(acc_done, UNITS * (n + 1))
                    sp.dma_start(x_out[bass.ds(n * T, T), :].rearrange("(k p) c -> p k c", p=P), x[:, b, :, :]).then_inc(x_stored, 16)

                def slot(n, b, following):
                    if isinstance(n, int) and n < 0:
                        return
                    if not (isinstance(n, int) and n == 0):
                        store(n - 1, 1 - b)
                        sp.wait_ge(x_stored, 16 * n)
                    if following:
                        n1, b1 = following
                        sp.dma_start(x[:, b1, :, :], x_in[bass.ds(n1 * T, T), :].rearrange("(k p) c -> p k c", p=P)).then_inc(x_loaded[b1], 16)

                batch_slots(sp, slot)
                store(NB - 1, 1)
                sp.wait_ge(x_stored, 16 * NB)

            @block.gpsimd
            def _(pool):
                pool.memset(eps[:, :], 1e-5).then_inc(const_set, 1)
                low(pool, 0, 0)
                for e in range(PAIRS):
                    pool.wait_ge(w_hi_s, e + 1)
                    pool.tensor_tensor(w_lo[:, e, :, :], raw[:, e, :, :], w_hi[:, e, :, :], ALU.subtract).then_inc(w_ready, 1)

                def slot(n, b, following):
                    if following and not (isinstance(n, int) and n < 0):
                        low(pool, *following)

                batch_slots(pool, slot)

            @block.scalar
            def _(act):
                act.preload_act_table_set("natural_log_exp_and_others")
                act.wait_ge(const_set, 1)

                def before(n, b, part):
                    if part == 0:
                        act.wait_ge(var_ready, n + 1)
                        wait(act, xn_ready, n)
                        act.activation(rs[:, 0, :], mv[:, :, 1], ACT.Ln, bias=eps[:, :]).then_inc(ln_ready, 1)
                        act.wait_ge(ln_ready, n + 1)
                        act.activation(rs[:, 0, :], rs[:, 0, :], ACT.Exp, scale=-0.5).then_inc(rs_ready, 1)
                    if part == 1:
                        act.wait_ge(xT_ps, n + 1)
                        wait(act, xT_lo_ready, n)
                        wait(act, logits, n)
                        if not isinstance(n, int) or n > 1:
                            act.wait_ge(o_ready, UNITS * (n - 1))
                        act.activation(xT[:, :, :], f_ps[:, :, :], ACT.Copy).then_inc(xT_ready, 1)
                        act.activation(xT_hi[:, b, :, :], f_ps[:, :, :], ACT.Copy).then_inc(xT_hi_ready, 1)
                    if part == 2:
                        act.wait_ge(z_ready, n + 1)
                        act.activation(p[:, :, :], p[:, :, :], ACT.Exp).then_inc(exp_ready, 1)
                    if part == 3:
                        act.wait_ge(combT_ps, n + 1)
                        if not isinstance(n, int) or n > 1:
                            act.wait_ge(b_ready, 2 * (n - 1))
                        act.activation(combT[:, b, :], f_ps[0:E, 0, :], ACT.Copy).then_inc(combT_ready, 1)

                def slot(n, b, following):
                    if isinstance(n, int) and n < 0:
                        for part in range(3):
                            before(0, 0, part)
                        for e in range(PAIRS):
                            if e == 0:
                                act.wait_ge(w_in, 16 * PAIRS)
                            act.activation(w_hi[:, e, :, :], raw[:, e, :, :], ACT.Copy).then_inc(w_hi_s, 1)
                        before(0, 0, 3)
                    elif following:
                        for part in range(4):
                            before(*following, part)

                batch_slots(act, slot)

            @block.vector
            def _(dve):
                steps = Steps(dve, steps_s, N_STEPS)
                dve.wait_ge(const_in, 80)

                def before(n, b, part):
                    if part == 0:
                        steps.begin(n)
                        dve.wait_ge(x_loaded[b], 16 * ((n - b) // 2 + 1) if isinstance(n, int) else 8 * (n - b) + 16)
                        wait(dve, var_ready, n)
                        dve_normalise(dve, steps, passed, x[:, b], xn, stats, mv, rs, 1e-5, var_ready, rs_ready, xn_ready, n, 0)
                    if part == 1:
                        wait(dve, xT_ps, n)
                        dve_normalise(dve, steps, passed, x[:, b], xn, stats, mv, rs, 1e-5, var_ready, rs_ready, xn_ready, n, 1)
                    if part == 2:
                        z_in = f_ps[:, 0, 0:4 * E].rearrange("p (k e) -> p k e", k=4)
                        bc = lambda s: s.unsqueeze(2).broadcast_to([P, 4, E])
                        dve.wait_ge(logits, n + 1)
                        steps(dve.tensor_tensor(p[:, :, :], z_in, gb[:, :].unsqueeze(1).broadcast_to([P, 4, E]), ALU.add))
                        steps(dve.tensor_scalar(p[:, :, :], p[:, :, :], 1e-4, None, ALU.max))
                        steps(dve.tensor_reduce(small[:, 0, :], p[:, :, :], AX.X, ALU.max))
                        dve.tensor_tensor(p[:, :, :], p[:, :, :], bc(small[:, 0, :]), ALU.subtract).then_inc(z_ready, 1)
                    if part == 3:
                        bc = lambda s: s.unsqueeze(2).broadcast_to([P, 4, E])
                        dve.wait_ge(exp_ready, n + 1)
                        mask = dve_top2(dve, steps, p[:, :, :], order[:, :, :], work, small)
                        steps(dve.scalar_tensor_tensor(work[:, 1], p[:, :, :], 0.1, mask, ALU.max, ALU.mult))
                        steps(dve.tensor_reduce(small[:, 0, :], work[:, 1], AX.X, ALU.add))
                        steps(dve.reciprocal(small[:, 1, :], small[:, 0, :]))
                        steps(dve.tensor_tensor(work[:, 1], work[:, 1], bc(small[:, 1, :]), ALU.mult))
                        dve.tensor_scalar(comb[:, b, :, :], work[:, 1], 0.5, None, ALU.mult).then_inc(comb_ready, 1)
                        assert steps.count == N_STEPS, steps.count

                def accumulate(n, b, u):
                    k, e = u // PAIRS, 2 * (u % PAIRS)
                    dve.wait_ge(o_ready, UNITS * n + u + 1)
                    if u % PAIRS == 0 and k % 2 == 0:
                        dve.wait_ge(b_ready, 2 * n + k // 2 + 1)
                        dve.tensor_tensor(x[:, b, k:k + 2, :], b_ps[:, k // 2, :].rearrange("p (a c) -> p a c", a=2), x[:, b, k:k + 2, :],
                                          ALU.add).then_inc(b_added, 1)
                        dve.wait_ge(b_added, 2 * n + k // 2 + 1)
                    else:
                        dve.wait_ge(acc_done, UNITS * n + u)
                    for a in range(2):
                        ins = dve.scalar_tensor_tensor(x[:, b, k, :], o_ps[:, u % 4, a * D:(a + 1) * D], comb[:, b, k, e + a:e + a + 1], x[:, b, k, :],
                                                       ALU.mult, ALU.add)
                        if a == 0:
                            ins.then_inc(half_s, 1)
                            dve.wait_ge(half_s, UNITS * n + u + 1)
                        else:
                            ins.then_inc(acc_done, 1)

                half_s = sem("m1_half_done")

                def slot(n, b, following):
                    if isinstance(n, int) and n < 0:
                        for part in range(4):
                            before(0, 0, part)
                        return
                    dve.wait_ge(comb_ready, n + 1)
                    for u in range(UNITS):
                        accumulate(n, b, u)
                        if following and u in (3, 5, 9, 11):
                            before(*following, (3, 5, 9, 11).index(u))

                batch_slots(dve, slot)

            @block.tensor
            def _(pe):
                pe.wait_ge(const_in, 80)

                def before(n, b, part):
                    if part == 0:
                        pe.wait_ge(xn_ready, n + 1)
                        wait(pe, combT_ready, n)
                        for kt in range(2):
                            for k in range(4):
                                last = pe.transpose(f_ps[:, kt, k * P:(k + 1) * P], xn[:, k, kt * P:(kt + 1) * P], ident[:, :])
                        last.then_inc(xT_ps, 1)
                    if part == 1:
                        pe.wait_ge(xT_hi_ready, n + 1)
                        for k in range(4):
                            for kt in range(2):
                                last = pe.matmul(f_ps[:, 0, k * E:(k + 1) * E], xT[:, kt, k * P:(k + 1) * P], gw[:, kt, :], start=(kt == 0), stop=(kt == 1))
                        last.then_inc(logits, 1)
                    if part == 2:
                        pe.wait_ge(comb_ready, n + 1)
                        for k in range(4):
                            last = pe.transpose(f_ps[0:E, 0, k * P:(k + 1) * P], comb[:, b, k, :], ident[:, :])
                        last.then_inc(combT_ps, 1)

                def slot(n, b, following):
                    if isinstance(n, int) and n < 0:
                        for part in range(3):
                            before(0, 0, part)
                        return
                    pe.wait_ge(xT_lo_ready, n + 1)
                    pe.wait_ge(combT_ready, n + 1)
                    for u in range(UNITS):
                        k, e = u // PAIRS, u % PAIRS
                        tok = slice(k * P, (k + 1) * P)
                        if u % PAIRS == 0 and k % 2 == 0:
                            wait(pe, b_added, 2 * n + k // 2 - 1)
                            for a in range(2):
                                last = pe.matmul(b_ps[:, k // 2, a * D:(a + 1) * D], combT[:, b, (k + a) * P:(k + a + 1) * P], eb[:, :], start=True, stop=True)
                            last.then_inc(b_ready, 1)
                        if isinstance(n, int) and n == 0 and k == 0:
                            pe.wait_ge(w_ready, e + 1)
                        wait(pe, acc_done, UNITS * n + u - 3)
                        parts = [(xt, w, kt) for kt in range(2) for xt, w in ((xT_hi, w_hi), (xT_lo, w_hi), (xT_hi, w_lo))]
                        for m, (xt, w, kt) in enumerate(parts):
                            last = pe.matmul(o_ps[:, u % 4, :], xt[:, b, kt, tok], w[:, e, kt, :], start=(m == 0), stop=(m == 5))
                        last.then_inc(o_ready, 1)
                        if following and u in (8, 10, 14):
                            before(*following, (8, 10, 14).index(u))

                batch_slots(pe, slot)


DI = 2 * D
DS, DTR = 16, 16
ND = DI // P
NP = DS // 2

SCHEDULE = {
    (0, 0): [("final", 3)], (0, 2): [("out", 0), ("out", 1)], (0, 3): [("z", 0), ("z", 1)], (0, 4): [("z", 2), ("z", 3)],
    (0, 5): [("silu_z", 0)], (0, 6): [("dt", 1)],
    (1, 0): [("final", 0)], (1, 1): [("ln", 0)], (1, 2): [("ln", 1)], (1, 3): [("ln", 2)], (1, 4): [("dt", 2)],
    (1, 5): [("tr", 0), ("tr", 1)], (1, 6): [("xi", 0), ("xi", 1)], (1, 7): [("conv", 0), ("conv", 1)],
    (2, 0): [("final", 1), ("xi", 2), ("xi", 3)], (2, 1): [("conv", 2), ("conv", 3)], (2, 2): [("silu_u", 0), ("split", 0)],
    (2, 3): [("ux", 0), ("split", 1)], (2, 4): [("ux", 1), ("split", 2), ("dt", 3)], (2, 5): [("ux", 2), ("split", 3)], (2, 6): [("ux", 3), ("stack", 0)],
    (3, 0): [("final", 2), ("bc", 0)], (3, 1): [("dt0", 0)], (3, 2): [("bc", 1)], (3, 3): [("bc", 2)], (3, 4): [("bc", 3)],
    (3, 5): [("bc", 4)], (3, 6): [("bc", 5)], (3, 7): [("bc", 6), ("bc", 7)],
}
NEXT = ("ln", "tr", "xi", "conv", "silu_u", "split", "ux", "stack", "dt0", "bc")
LAST = ("out",)
FILLS = [(kind, i, k) for key in sorted(SCHEDULE) for kind, i in SCHEDULE[key] if kind in ("out", "z", "dt", "dt0", "tr", "xi", "conv", "bc")
         for k in range(4 if kind == "bc" else 1)]


def mamba_phase(nc, sem, A, x_in, x_out):
    with ExitStack() as ctx:
        sb = lambda name, shape, dt=F32: ctx.enter_context(nc.sbuf_tensor("mb_" + name, shape, dt))
        ident = sb("ident", [P, P])
        cols = sb("cols", [P, 4, 9])
        lnc = sb("lnc", [P, 2, 2])
        a_neg = sb("a_neg", [P, ND, DS])
        fix = sb("fix", [P, 3])
        diag = sb("diag", [P, ND, 4, P])
        wi_hi, wi_lo = (sb(f"wi_{s}", [P, 2, 2 * DI], F32R) for s in ("hi", "lo"))
        wo_hi, wo_lo = (sb(f"wo_{s}", [P, ND, D], F32R) for s in ("hi", "lo"))
        wx_hi, wx_lo = (sb(f"wx_{s}", [P, ND, 48], F32R) for s in ("hi", "lo"))
        wdt = sb("wdt", [DTR, DI])
        sel_f, sel = sb("sel_f", [64, 32]), sb("sel", [64, 32], F32R)
        res = sb("res", [P, 2, 4, D])
        xn = sb("xn", [P, 4, D])
        stats, mv, rs = sb("stats", [P, 2, 4, 6]), sb("mv", [P, 2, 4, 2]), sb("rs", [P, 2, 4, 4])
        hT_hi, hT_lo = (sb(f"hT_{s}", [P, 2, T], F32R) for s in ("hi", "lo"))
        xi = sb("xi", [P, 2, T + 3])
        u = sb("u", [P, 2, ND, T])
        u_hi, u_lo = (sb(f"u_{s}", [P, T], F32R) for s in ("hi", "lo"))
        z = sb("z", [P, ND, T])
        stack = sb("stack", [64, T], F32R)
        dtr = sb("dtr", [DTR, T])
        ex, w1, lg = (sb(n, [P, T]) for n in ("ex", "w1", "lg"))
        dt, dtu = sb("dt", [P, 2, T]), sb("dtu", [P, 2, T])
        bbc, cbc = sb("bbc", [P, DS, T]), sb("cbc", [P, DS, T])
        yt = sb("yt", [P, T])
        raw_wi, raw_wo = bbc[:, 0:4, :].rearrange("p (k a) t -> p k (a t)", k=2), bbc[:, 4:6, :].rearrange("p a (b e) -> p (a b) e", b=2)
        raw_wx = bbc[:, 6, 0:ND * 48].rearrange("p (d e) -> p d e", d=ND)
        dbu = sb("dbu", [P, 2, 2, T])
        hc = sb("hc", [P, 2, 2, T])
        y_hi, y_lo = (sb(f"y_{s}", [P, ND, T], F32R) for s in ("hi", "lo"))
        da_ps = ctx.enter_context(nc.psum_tensor("mb_da_ps", [P, 2, 2, T], F32))
        y_ps = ctx.enter_context(nc.psum_tensor("mb_y_ps", [P, T], F32))
        g_ps = ctx.enter_context(nc.psum_tensor("mb_g_ps", [P, T], F32))
        f_ps = ctx.enter_context(nc.psum_tensor("mb_f_ps", [P, 2, T], F32))

        names = """const_in prep p_bias a_exp x_stored passed_pool ln_done ln_steps var1 rs1 xn1 var2 rs2 xn2 res_sum
                   f_ready hT_hi_ready z_ready u_ready u_hi_ready u_lo_ready stack_hi_ready dtr_ready stack_ready
                   act_steps ex_ready dt_steps dt_ready dtu_ready da_ready dbu_ready scan_done hc_ready y_ready
                   y_used yg_ready y_hi_ready y_lo_ready ux_done"""
        S = {q: sem("mb_" + q) for q in names.split()}
        S["passed"] = sem("passed")
        f_used = [sem(f"mb_f_used{r}") for r in range(2)]
        x_loaded = [sem(f"mb_x_loaded{r}") for r in range(2)]
        PREP = 4 * ND + 2 + 2 + 6 + 1

        def present(n, kind, i):
            if n == -1:
                return kind in NEXT
            if n == NB:
                return kind in LAST or (kind, i) == ("final", 3)
            if n == 0 and (kind in LAST or (kind, i) == ("final", 3)):
                return False
            return not (n == NB - 1 and kind in NEXT)

        def fill(n, kind, i, k=0):
            at = FILLS.index((kind, i, k))
            bank = at % 2

            def before(m, upto=None):
                here = [(j, f) for j, f in enumerate(FILLS[:upto]) if present(m, f[0], f[1])]
                return sum(j % 2 == bank for j, f in here), len(here)
            if isinstance(n, int):
                parts = [before(m) for m in range(-1, n)] + [before(n, at)]
                return bank, sum(p[0] for p in parts), sum(p[1] for p in parts) + 1
            parts = [before(-1), before(0), before(1, at)]
            same, every = before(1)
            return bank, n * same + sum(p[0] for p in parts) - same, n * every + sum(p[1] for p in parts) + 1 - every

        def tasks(run, n, b, key):
            for kind, i in SCHEDULE.get(key, []):
                if present(n if isinstance(n, int) else 1, kind, i):
                    back = kind in LAST or (kind, i) == ("final", 3)
                    m, mb = (n + 1, 1 - b) if kind in NEXT else (n - 1, 1 - b) if back else (n, b)
                    run(kind, i, n, m, mb)

        def slots(eng, unit, run, lag=0):
            keys = [(d, p) for d in range(ND) for p in range(NP)]

            def slot(n, b, _):
                if isinstance(n, int) and n < 0:
                    for key in keys:
                        tasks(run, n, b, key)
                    unit(n, b, ND, 0)
                    return
                for at, (d, p) in enumerate(keys):
                    unit(n, b, d, p)
                    if not lag:
                        tasks(run, n, b, (d, p))
                    elif at:
                        tasks(run, n, b, keys[at - 1])
                if lag:
                    tasks(run, n, b, keys[-1])
                    unit(n, b, ND, 0)

            batch_slots(eng, slot)
            for key in keys:
                tasks(run, NB, 0, key)

        def count(n, d, p):
            return ND * NP * n + NP * d + p

        def q_ring(p):
            return p % 2

        def used_up(eng, n, kind, i, k=0):
            bank, used, _ = fill(n, kind, i, k)
            eng.wait_ge(f_used[bank], used + 1)

        def load_count(n, b):
            return 16 * ((n - b) // 2 + 1) if isinstance(n, int) else 8 * (n - b) + 16

        with nc.Block() as block:

            @block.sync
            def _(sp):
                def load(n, b):
                    wait(sp, S["x_stored"], 16 * (n - 1) if not isinstance(n, int) or n > 1 else 0)
                    sp.dma_start(res[:, b, :, :], x_in[bass.ds(n * T, T), :].rearrange("(k p) c -> p k c", p=P)).then_inc(x_loaded[b], 16)

                load(0, 0)
                for dst, src in ((ident[:, :], A["ident"]), (cols[:, :, 0:7], A["mb_cols"]), (lnc[:, :, :], A["mb_ln"]), (a_neg[:, :, :], A["mb_alog"]),
                                 (wdt[:, :], A["mb_wdt"]), (sel_f[:, :], A["mb_sel"]), (raw_wi, A["mb_wi"].rearrange("(k c) e -> c k e", c=P)),
                                 (raw_wo, A["mb_wo"].rearrange("(k c) e -> c k e", c=P)),
                                 (raw_wx, A["mb_wx"].rearrange("(k c) e -> c k e", c=P))):
                    sp.dma_start(dst, src).then_inc(S["const_in"], 16)
                load(1, 1)

                def run(kind, i, n, m, b):
                    if (kind, i) == ("out", 1):
                        used_up(sp, n, "out", 1)
                        sp.dma_start(x_out[bass.ds(m * T, T), :].rearrange("(k p) c -> p k c", p=P), res[:, b, :, :]).then_inc(S["x_stored"], 16)
                    if (kind, i) == ("ln", 0) and not (isinstance(n, int) and n < 1):
                        load(m, b)

                slots(sp, lambda *a: None, run)
                sp.wait_ge(S["x_stored"], 16 * NB)

            @block.gpsimd
            def _(pool):
                for q, (dst, value) in enumerate(((fix[:, 0:1], 1e-5), (fix[:, 1:2], 1e-6), (fix[:, 2:3], 1.0), (xi[:, :, 0:3], 0.0))):
                    pool.memset(dst, value).then_inc(S["passed_pool"], 1)

                def unit(n, b, d, p):
                    if d == ND:
                        return
                    q = count(n, d, p)
                    if p == 0:
                        pool.wait_ge(S["dtu_ready"], ND * n + d + 1)
                    if d == 0:
                        used_up(pool, n - 1, "bc", p, 1)
                    wait(pool, S["scan_done"], q - 1)
                    dtu_2 = dtu[:, d % 2, :].unsqueeze(1).broadcast_to([P, 2, T])
                    pool.tensor_tensor(dbu[:, q_ring(p), :, :], dtu_2, bbc[:, 2 * p:2 * p + 2, :], ALU.mult).then_inc(S["dbu_ready"], 1)

                def run(kind, i, n, m, b):
                    if (kind, i) == ("ln", 1):
                        pool.wait_ge(S["xn1"], m + 1)
                        pool.tensor_tensor(res[:, b, :, :], res[:, b, :, :], xn[:, :, :], ALU.add).then_inc(S["res_sum"], 1)

                slots(pool, unit, run, lag=1)

            @block.scalar
            def _(act):
                act.preload_act_table_set("natural_log_exp_and_others")
                act.wait_ge(S["const_in"], 16 * 9)
                act.activation(a_neg[:, :, :], a_neg[:, :, :], ACT.Exp).then_inc(S["a_exp"], 1)
                act.wait_ge(S["prep"], PREP)
                act.wait_ge(S["passed_pool"], 4)

                def exps(n, d, p):
                    q = count(n, d, p)
                    if p == 0:
                        act.wait_ge(S["dt_ready"], ND * n + d + 1)
                    wait(act, S["hc_ready"], q - 1)
                    for j in range(2):
                        last = act.activation(da_ps[:, q_ring(p), j, :], dt[:, d % 2, :], ACT.Exp, scale=a_neg[:, d, 2 * p + j:2 * p + j + 1])
                    last.then_inc(S["da_ready"], 1)

                def unit(n, b, d, p):
                    if d == ND:
                        exps(0, 0, 0)
                    elif (d, p) != (ND - 1, NP - 1):
                        exps(n, d + (p + 1) // NP, (p + 1) % NP)
                    elif not (isinstance(n, int) and n == NB - 1):
                        exps(n + 1, 0, 0)

                def run(kind, i, n, m, b):
                    if kind in ("z", "tr", "xi", "conv", "dt", "dt0", "bc"):
                        bank, used, ready = fill(n, kind, i)
                    if kind == "ln" and i < 2:
                        var, rsq, xnr = (S["var1"], S["rs1"], S["xn1"]) if i == 0 else (S["var2"], S["rs2"], S["xn2"])
                        act.wait_ge(var, m + 1)
                        wait(act, xnr, m)
                        act.activation(rs[:, i, 0, :], mv[:, i, :, 1], ACT.Ln, bias=fix[:, i:i + 1]).then_inc(S["ln_done"], 1)
                        act.wait_ge(S["ln_done"], 2 * m + i + 1)
                        act.activation(rs[:, i, 0, :], rs[:, i, 0, :], ACT.Exp, scale=-0.5).then_inc(rsq, 1)
                    elif kind == "z":
                        act.wait_ge(S["f_ready"], ready)
                        wait(act, S["y_lo_ready"], ND * (m - 1) + i + 1)
                        act.activation(z[:, i, :], f_ps[:, bank, :], ACT.Identity, bias=cols[:, i, 8:9]).then_inc(f_used[bank], 1)
                    elif kind == "tr":
                        act.wait_ge(S["f_ready"], ready)
                        act.activation(hT_hi[:, i, :], f_ps[:, bank, :], ACT.Copy).then_inc(S["hT_hi_ready"], 1)
                    elif kind == "xi":
                        act.wait_ge(S["f_ready"], ready)
                        act.activation(xi[:, i % 2, 3:], f_ps[:, bank, :], ACT.Identity, bias=cols[:, i, 7:8]).then_inc(f_used[bank], 1)
                    elif kind == "conv":
                        act.wait_ge(S["f_ready"], ready)
                        act.activation(u[:, b, i, :], f_ps[:, bank, :], ACT.Identity, bias=cols[:, i, 4:5]).then_inc(f_used[bank], 1)
                    elif kind == "silu_z":
                        used_up(act, n, "z", 2)
                        used_up(act, n, "z", 3)
                        act.activation(z[:, :, :], z[:, :, :], ACT.Silu).then_inc(S["z_ready"], 1)
                        act.preload_act_table_set("natural_log_exp_and_others")
                    elif kind == "silu_u":
                        used_up(act, n, "conv", 2)
                        used_up(act, n, "conv", 3)
                        act.activation(u[:, b, :, :], u[:, b, :, :], ACT.Silu).then_inc(S["u_ready"], 1)
                        act.preload_act_table_set("natural_log_exp_and_others")
                        act.wait_ge(S["u_ready"], m + 1)
                    elif kind == "split":
                        wait(act, S["ux_done"], ND * m + i)
                        act.activation(u_hi[:, :], u[:, b, i, :], ACT.Copy).then_inc(S["u_hi_ready"], 1)
                    elif kind == "stack":
                        act.wait_ge(S["ux_done"], ND * m + ND)
                        act.activation(stack[0:32, :], g_ps[0:32, :], ACT.Copy).then_inc(S["stack_hi_ready"], 1)
                        act.activation(dtr[:, :], g_ps[32:48, :], ACT.Copy).then_inc(S["dtr_ready"], 1)
                    elif kind in ("dt", "dt0"):
                        q = ND * m + i
                        act.wait_ge(S["f_ready"], ready)
                        wait(act, S["dt_ready"], q)
                        act.activation(ex[:, :], f_ps[:, bank, :], ACT.Abs, bias=cols[:, i, 5:6]).then_inc(S["act_steps"], 1)
                        wait(act, S["da_ready"], NP * (q - 1))
                        act.activation(dt[:, i % 2, :], f_ps[:, bank, :], ACT.Relu, bias=cols[:, i, 5:6]).then_inc(f_used[bank], 1)
                        act.wait_ge(S["act_steps"], 2 * q + 1)
                        act.activation(ex[:, :], ex[:, :], ACT.Exp, scale=-1.0).then_inc(S["act_steps"], 1)
                        act.wait_ge(S["act_steps"], 2 * q + 2)
                        act.activation(w1[:, :], ex[:, :], ACT.Identity, bias=fix[:, 2:3])
                        act.activation(lg[:, :], ex[:, :], ACT.Ln, bias=fix[:, 2:3]).then_inc(S["ex_ready"], 1)
                    elif kind == "bc":
                        for k in range(4):
                            bank, used, ready = fill(n, kind, i, k)
                            act.wait_ge(S["f_ready"], ready)
                            if k == 0:
                                wait(act, S["dbu_ready"], count(m, -1, i) + 1)
                            if k == 2:
                                wait(act, S["hc_ready"], count(m, -1, i) + 1)
                            dst = (bbc, cbc)[k // 2][:, 2 * i + k % 2, :]
                            act.activation(dst, f_ps[:, bank, :], ACT.Copy).then_inc(f_used[bank], 1)
                    elif kind == "final":
                        act.wait_ge(S["yg_ready"], ND * m + i + 1)
                        if i == 0 and present(n if isinstance(n, int) else 1, "out", 1):
                            act.wait_ge(S["f_ready"], fill(n, "out", 1)[2])
                        act.activation(y_hi[:, i, :], z[:, i, :], ACT.Copy).then_inc(S["y_hi_ready"], 1)

                slots(act, unit, run)

            @block.vector
            def _(dve):
                done = [0]

                def mark(ins):
                    done[0] += 1
                    ins.then_inc(S["prep"], 1)

                def settle():
                    dve.wait_ge(S["prep"], done[0])

                dve.wait_ge(S["const_in"], 16 * 9)
                for d in range(ND):
                    for k in range(4):
                        mark(dve.tensor_scalar(diag[:, d, k, :], ident[:, :], cols[:, d, k:k + 1], None, ALU.mult))
                mark(dve.tensor_copy(sel[:, :], sel_f[:, :]))
                dve.wait_ge(S["p_bias"], 1)
                mark(dve.tensor_copy(cols[:, :, 7:9], g_ps[:, 0:8].rearrange("p (a d) -> p d a", a=2)))
                for kt in range(2):
                    mark(dve.tensor_scalar(raw_wi[:, kt, :], raw_wi[:, kt, :], lnc[:, kt, 0:1], None, ALU.mult))
                settle()
                for raw, hi, lo in ((raw_wi, wi_hi, wi_lo), (raw_wo, wo_hi, wo_lo), (raw_wx, wx_hi, wx_lo)):
                    mark(dve.tensor_copy(hi[:, :, :], raw))
                    settle()
                    mark(dve.tensor_tensor(lo[:, :, :], raw, hi[:, :, :], ALU.subtract))
                dve.wait_ge(S["a_exp"], 1)
                mark(dve.tensor_scalar(a_neg[:, :, :], a_neg[:, :, :], -1.0, None, ALU.mult))
                settle()
                assert done[0] == PREP, done[0]
                ln_steps = Steps(dve, S["ln_steps"], 2 * 12)

                def unit(n, b, d, p):
                    if d == ND:
                        return
                    q = count(n, d, p)
                    r = q_ring(p)
                    dve.wait_ge(S["da_ready"], q + 1)
                    dve.wait_ge(S["dbu_ready"], q + 1)
                    for j in range(2):
                        last = dve.tensor_tensor_scan(da_ps[:, r, j, :], da_ps[:, r, j, :], dbu[:, r, j, :], 0.0, ALU.mult, ALU.add)
                    last.then_inc(S["scan_done"], 1)
                    if d == 0:
                        used_up(dve, n - 1, "bc", p, 3)
                    wait(dve, S["y_ready"], q - 1)
                    dve.wait_ge(S["scan_done"], q + 1)
                    dve.tensor_tensor(hc[:, r, :, :], da_ps[:, r, :, :], cbc[:, 2 * p:2 * p + 2, :], ALU.mult).then_inc(S["hc_ready"], 1)
                    if p == 0:
                        if d:
                            final(n, b, d - 1)
                        elif not (isinstance(n, int) and n == 0):
                            final(n - 1, 1 - b, ND - 1)

                def final(n, b, d):
                    q = ND * n + d
                    dve.wait_ge(S["y_ready"], NP * (q + 1))
                    dve.wait_ge(S["z_ready"], n + 1)
                    wait(dve, S["yg_ready"], q)
                    dve.scalar_tensor_tensor(yt[:, :], u[:, b, d, :], cols[:, d, 6:7], y_ps[:, :], ALU.mult, ALU.add).then_inc(S["y_used"], 1)
                    dve.wait_ge(S["y_used"], q + 1)
                    dve.tensor_tensor(z[:, d, :], yt[:, :], z[:, d, :], ALU.mult).then_inc(S["yg_ready"], 1)

                def run(kind, i, n, m, b):
                    if kind in ("out", "tr"):
                        bank, used, ready = fill(n, kind, i)
                    if kind == "final":
                        if isinstance(n, int) and n == NB:
                            final(m, b, i)
                        dve.wait_ge(S["y_hi_ready"], ND * m + i + 1)
                        dve.tensor_tensor(y_lo[:, i, :], z[:, i, :], y_hi[:, i, :], ALU.subtract).then_inc(S["y_lo_ready"], 1)
                    elif kind == "out":
                        dve.wait_ge(S["f_ready"], ready)
                        r_2 = res[:, b, 2 * i:2 * i + 2, :]
                        dve.wait_ge(S["res_sum"], m + 1)
                        dve.tensor_tensor(r_2, f_ps[:, bank, :].rearrange("p (a c) -> p a c", a=2), r_2, ALU.add).then_inc(f_used[bank], 1)
                    elif kind == "ln":
                        if i == 0:
                            ln_steps.begin(m)
                            dve.wait_ge(x_loaded[b], load_count(m, b))
                            wait(dve, S["var1"], m)
                            wait(dve, S["xn1"], m)
                            dve_normalise(dve, ln_steps, S["passed"], res[:, b], xn, stats[:, 0], mv[:, 0], rs[:, 0], 1e-5, S["var1"], S["rs1"], S["xn1"], m, 0)
                        if i == 1:
                            if not (isinstance(n, int) and n < 0):
                                dve.wait_ge(S["f_ready"], fill(n - 1, "tr", 1)[2])
                            dve_normalise(dve, ln_steps, S["passed"], res[:, b], xn, stats[:, 0], mv[:, 0], rs[:, 0], 1e-5, S["var1"], S["rs1"], S["xn1"], m, 1)
                            wait(dve, S["var2"], m)
                            wait(dve, S["xn2"], m)
                            dve.wait_ge(S["xn1"], m + 1)
                            dve_normalise(dve, ln_steps, S["passed"], xn, xn, stats[:, 1], mv[:, 1], rs[:, 1], 1e-6, S["var2"], S["rs2"], S["xn2"], m, 0)
                        if i == 2:
                            dve.wait_ge(S["res_sum"], m + 1)
                            dve_normalise(dve, ln_steps, S["passed"], xn, xn, stats[:, 1], mv[:, 1], rs[:, 1], 1e-6, S["var2"], S["rs2"], S["xn2"], m, 1)
                            assert ln_steps.count == 24, ln_steps.count
                    elif kind == "tr":
                        dve.wait_ge(S["hT_hi_ready"], 2 * m + i + 1)
                        dve.tensor_tensor(hT_lo[:, i, :], f_ps[:, bank, :], hT_hi[:, i, :], ALU.subtract).then_inc(f_used[bank], 1)
                    elif kind == "split":
                        dve.wait_ge(S["u_hi_ready"], ND * m + i + 1)
                        dve.tensor_tensor(u_lo[:, :], u[:, b, i, :], u_hi[:, :], ALU.subtract).then_inc(S["u_lo_ready"], 1)
                    elif kind == "stack":
                        dve.wait_ge(S["stack_hi_ready"], m + 1)
                        if not (isinstance(n, int) and n < 0):
                            dve.wait_ge(S["f_ready"], fill(n - 1, "bc", NP - 1, 3)[2])
                        dve.tensor_tensor(stack[32:64, :], g_ps[0:32, :], stack[0:32, :], ALU.subtract).then_inc(S["stack_ready"], 1)
                    elif kind in ("dt", "dt0"):
                        q = ND * m + i
                        dve.wait_ge(S["ex_ready"], q + 1)
                        dve.scalar_tensor_tensor(w1[:, :], w1[:, :], -1.0, ex[:, :], ALU.add, ALU.subtract).then_inc(S["dt_steps"], 1)
                        dve.wait_ge(S["dt_steps"], 2 * q + 1)
                        dve.tensor_tensor(lg[:, :], lg[:, :], w1[:, :], ALU.subtract).then_inc(S["dt_steps"], 1)
                        dve.wait_ge(S["dt_steps"], 2 * q + 2)
                        dve.tensor_tensor(dt[:, i % 2, :], dt[:, i % 2, :], lg[:, :], ALU.add).then_inc(S["dt_ready"], 1)
                        dve.wait_ge(S["dt_ready"], q + 1)
                        dve.tensor_tensor(dtu[:, i % 2, :], dt[:, i % 2, :], u[:, b, i, :], ALU.mult).then_inc(S["dtu_ready"], 1)

                slots(dve, unit, run, lag=1)

            @block.tensor
            def _(pe):
                pe.wait_ge(S["const_in"], 16 * 9)
                for j in range(8):
                    for kt in range(2):
                        last = pe.matmul(g_ps[:, j:j + 1], raw_wi[:, kt, j * P:(j + 1) * P], lnc[:, kt, 1:2], start=(kt == 0), stop=(kt == 1))
                last.then_inc(S["p_bias"], 1)
                pe.wait_ge(S["prep"], PREP)

                def unit(n, b, d, p):
                    if d == ND:
                        return
                    q = count(n, d, p)
                    if p == 0:
                        wait(pe, S["y_used"], ND * n + d)
                    pe.wait_ge(S["hc_ready"], q + 1)
                    for j in range(2):
                        last = pe.matmul(y_ps[:, :], ident[:, :], hc[:, q_ring(p), j, :], start=(p == 0 and j == 0), stop=(p == NP - 1 and j == 1))
                    last.then_inc(S["y_ready"], 1)

                def run(kind, i, n, m, b):
                    if kind == "ux":
                        q = ND * m + i
                        pe.wait_ge(S["u_lo_ready"], q + 1)
                        if i == 0:
                            wait(pe, S["stack_ready"], m)
                            wait(pe, S["dtr_ready"], m)
                        for k, (w, ux) in enumerate(((wx_hi, u_hi), (wx_lo, u_hi), (wx_hi, u_lo))):
                            last = pe.matmul(g_ps[0:48, :], w[:, i, :], ux[:, :], start=(i == 0 and k == 0), stop=(i == ND - 1 and k == 2))
                        last.then_inc(S["ux_done"], 1)
                        return
                    if kind not in ("out", "z", "dt", "dt0", "tr", "xi", "conv", "bc"):
                        return
                    for k in range(4 if kind == "bc" else 1):
                        bank, used, ready = fill(n, kind, i, k)
                        out = f_ps[:, bank, :]
                        wait(pe, f_used[bank], used)
                        if kind == "out":
                            pe.wait_ge(S["y_lo_ready"], ND * m + ND)
                            for a in range(2):
                                tok = slice((2 * i + a) * P, (2 * i + a + 1) * P)
                                parts = [(yy, w, d) for d in range(ND) for yy, w in ((y_hi, wo_hi), (y_lo, wo_hi), (y_hi, wo_lo))]
                                for c, (yy, w, d) in enumerate(parts):
                                    last = pe.matmul(out[:, a * D:(a + 1) * D], yy[:, d, tok], w[:, d, :], start=(c == 0), stop=(c == 3 * ND - 1))
                        elif kind in ("xi", "z"):
                            if (kind, i) == ("xi", 0):
                                used_up(pe, n, "tr", 0)
                                used_up(pe, n, "tr", 1)
                            e = slice(((kind == "z") * ND + i) * P, ((kind == "z") * ND + i + 1) * P)
                            parts = [(w, h, kt) for kt in range(2) for w, h in ((wi_hi, hT_hi), (wi_lo, hT_hi), (wi_hi, hT_lo))]
                            for c, (w, h, kt) in enumerate(parts):
                                last = pe.matmul(out, w[:, kt, e], h[:, kt, :], start=(c == 0), stop=(c == 5))
                        elif kind == "tr":
                            pe.wait_ge(S["xn2"], m + 1)
                            for a in range(4):
                                last = pe.transpose(out[:, a * P:(a + 1) * P], xn[:, a, i * P:(i + 1) * P], ident[:, :])
                        elif kind == "conv":
                            used_up(pe, n, "xi", i)
                            for c in range(4):
                                last = pe.matmul(out, diag[:, i, c, :], xi[:, i % 2, c:c + T], start=(c == 0), stop=(c == 3))
                        elif kind in ("dt", "dt0"):
                            pe.wait_ge(S["dtr_ready"], m + 1)
                            last = pe.matmul(out, wdt[:, i * P:(i + 1) * P], dtr[:, :], start=True, stop=True)
                        elif kind == "bc":
                            row = (k // 2) * DS + 2 * i + k % 2
                            pe.wait_ge(S["stack_ready"], m + 1)
                            last = pe.matmul(out, sel[:, row:row + 1].broadcast_to([64, P]), stack[:, :], start=True, stop=True)
                        last.then_inc(S["f_ready"], 1)

                slots(pe, unit, run)


def four_phases(nc, A, x4):
    x1, x2, x3 = (nc.dram_tensor(f"x{i}", (NB * T, D), F32, kind="Internal").ap() for i in (1, 2, 3))
    with ExitStack() as sems:
        passed = sems.enter_context(nc.semaphore("passed"))
        sem = lambda name: passed if name == "passed" else sems.enter_context(nc.semaphore(name))
        attention_phase(nc, sem, A, x1)
        moe_swiglu_phase(nc, sem, A, x1, x2)
        mamba_phase(nc, sem, A, x2, x3)
        moe_linear_phase(nc, sem, A, x3, x4)


def host_layout(a):
    c = {k: np.ascontiguousarray(np.asarray(v)) for k, v in a.items()}
    rep = lambda row: np.ascontiguousarray(np.broadcast_to(row, (P, row.size)))
    swap = np.arange(D) ^ 1
    col2 = lambda v: v.reshape(2, P).T
    cos, sin = (c[f"L0_attn_{n}"][T] for n in ("cos", "sin"))
    sign = np.where(np.arange(D) % 2 == 0, -1.0, 1.0).astype(np.float32)
    out = {"x": c["L0_attn_x"].reshape(NB * T, D), "ident": np.eye(P, dtype=np.float32)}
    for n in "qk":
        w = c[f"L0_attn_w{n}"].T
        out[f"w{n}T"], out[f"w{n}Ts"] = np.ascontiguousarray(w), np.ascontiguousarray(w[:, swap])
    out["cosb"], out["sinb"], out["signb"] = rep(np.tile(cos, NJ)), rep(np.tile(sin, NJ)), rep(sign)
    bq, bk, bv = (c[f"L0_attn_b{n}"] for n in "qkv")
    out["at_cols"] = np.ascontiguousarray(np.concatenate(
        [col2(bq), col2(bk), col2(bq[swap]), col2(bk[swap])] + [np.tile(v, P // v.size)[:, None] for v in (cos, sin, sign[:P])], axis=1))
    out["wvT"] = np.ascontiguousarray(c["L0_attn_wv"].T)
    out["bvt"] = np.ascontiguousarray(np.repeat(bv.reshape(4, 4, DK).transpose(1, 0, 2).reshape(4, 4 * DK), 32, axis=0))
    wo = np.zeros((4, 32, 4, D), np.float32)
    wo[:, :DK] = c["L0_attn_wo"].T.reshape(4, 4, DK, D).transpose(1, 2, 0, 3)
    out["wo_pad"] = wo.reshape(P, 4, D)
    out["bo_rep"] = rep(c["L0_attn_bo"])
    out["order"] = np.ascontiguousarray(np.broadcast_to(np.arange(8, 0, -1, dtype=np.float32), (P, 4, 8)))
    out["m0_rw"] = np.ascontiguousarray(c["L0_ffn_router_weight"].reshape(2, P, 8).transpose(1, 0, 2))
    out["m1_gw"] = np.ascontiguousarray(c["L1_ffn_gate_W"].reshape(2, P, 8).transpose(1, 0, 2))
    out["m1_gb"], out["m1_eb"] = rep(c["L1_ffn_gate_b"]), c["L1_ffn_expert_b"]
    out["m1_w"] = np.ascontiguousarray(c["L1_ffn_expert_W"].reshape(4, 2, D, D).transpose(0, 2, 1, 3).reshape(4, D, 2 * D))
    m = {k[8:]: v for k, v in c.items() if k.startswith("L1_attn_")}
    inner = [*m["conv_w"][:, 0, :].T, m["conv_b"], m["b_dt"], m["Dp"]]
    out["mb_cols"] = np.ascontiguousarray(np.stack([v.reshape(4, P) for v in inner], 2).transpose(1, 0, 2))
    out["mb_ln"] = np.ascontiguousarray(np.stack([v.reshape(2, P) for v in (m["ln_g"], m["ln_b"])], 2).transpose(1, 0, 2))
    out["mb_alog"] = np.ascontiguousarray(m["A_log"].reshape(4, P, 16).transpose(1, 0, 2))
    out["mb_wdt"], out["mb_wi"], out["mb_wo"] = (np.ascontiguousarray(m[k].T) for k in ("W_dt", "W_in", "W_out"))
    out["mb_wx"] = np.ascontiguousarray(np.concatenate([m["W_x"][16:], m["W_x"][:16]]).T)
    out["mb_sel"] = np.ascontiguousarray(np.tile(np.eye(32, dtype=np.float32), (2, 1)))
    out["m0_w1"], out["m0_w2"] = c["L0_ffn_w1"], c["L0_ffn_w2"]
    return out


def kernel(**inputs):
    import concourse.bacc as _bacc
    from concourse.bass_utils import run_bass_kernel_spmd as _run

    arrays = host_layout(inputs)
    nc = _bacc.Bacc("TRN2", target_bir_lowering=False, num_devices=1)
    args = {name: nc.dram_tensor("in_" + name, a.shape, F32, kind="ExternalInput").ap() for name, a in arrays.items()}
    x4 = nc.dram_tensor("x4", (NB * T, D), F32, kind="ExternalOutput").ap()
    four_phases(nc, args, x4)
    r = _run(nc, [{"in_" + name: a for name, a in arrays.items()}], core_ids=[0])
    return r.results[0]["x4"].reshape(NB, T, D)
```

```python
from contextlib import ExitStack

import numpy as np

import concourse.bass as bass
from concourse import mybir

ALU = mybir.AluOpType
ACT = mybir.ActivationFunctionType
AX = mybir.AxisListType
F32 = mybir.dt.float32
F32R = mybir.dt.float32r

P = 128
D = 256
NB, T = 8, 512
NT = NB * T // P
NH = 16
DK = D // NH
NJ = D // DK
SCALE = DK ** -0.5


def wait(eng, sem, value):
    if not isinstance(value, int) or value > 0:
        eng.wait_ge(sem, value)

def attention_phase(nc, all_sems, A, x_out):
    with ExitStack() as ctx:
        sb = lambda name, shape, dt=F32: ctx.enter_context(nc.sbuf_tensor("at_" + name, shape, dt))
        sem = lambda name: all_sems("at_" + name)
        x_in = A["x"]

        ident = sb("ident", [P, P])
        cosb, sinb, signb = (sb(n, [P, D]) for n in ("cosb", "sinb", "signb"))
        cols = sb("cols", [P, 11])
        bqk = sb("bqk", [P, 4])
        wraw = sb("wraw", [P, 2, 2, D])
        wrot = sb("wrot", [P, 2, D])
        w_hi = sb("w_hi", [P, 2, 2, D], F32R)
        w_lo = sb("w_lo", [P, 2, 2, D], F32R)
        wv = sb("wv", [P, 2, D])
        bvt = sb("bvt", [P, 64])
        wo = sb("wo", [P, 4, D])
        bo = sb("bo", [P, D])
        eps = sb("eps", [P, 1])

        xin = sb("xin", [P, 4, D])
        stats = sb("stats", [P, 6])
        mv = sb("mv", [P, 2, 2])
        rs = sb("rs", [P, 2, 4])
        xn = sb("xn", [P, D])
        xT = sb("xT", [P, 2, 2, P])
        xT_hi = sb("xT_hi", [P, 2, P], F32R)
        xT_lo = sb("xT_lo", [P, 2, P], F32R)
        qk = sb("qk", [P, 4, P])
        qk_hi = sb("qk_hi", [P, 4, P], F32R)
        qk_lo = sb("qk_lo", [P, 4, P], F32R)
        qst = sb("qst", [P, 4, NJ, P], F32R)
        kst = sb("kst", [P, 4, NJ, P], F32R)
        vau = sb("vau", [P, 4, 4, 4, 32])
        mx = sb("mx", [P, 2, 16])
        nm = sb("nm", [4, 4, 32, 4])
        nm_hi = sb("nm_hi", [4, 4, 32, 4], F32R)
        nm_lo = sb("nm_lo", [4, 4, 32, 4], F32R)
        probs = sb("probs", [P, 2, 16, 512])
        oc = sb("oc", [P, 512])
        sums = sb("sums", [P, 512])
        rsum = sb("rsum", [P, 2, 512])
        oT = sb("oT", [P, 4, 512])
        xo = sb("xo", [P, 4, D])
        scr = nc.dram_tensor("at_scr", (4, 2, 2 * D, P), F32, kind="Internal").ap()

        s_ps = ctx.enter_context(nc.psum_tensor("at_s_ps", [P, 2, 2, 512], F32))
        t_ps = ctx.enter_context(nc.psum_tensor("at_t_ps", [P, 2, 512], F32))
        o_ps = ctx.enter_context(nc.psum_tensor("at_o_ps", [P, 512], F32))
        f_ps = ctx.enter_context(nc.psum_tensor("at_f_ps", [P, 512], F32))

        w_in, wprep, const_set = sem("w_in"), sem("wprep"), sem("const_set")
        x_loaded = [sem(f"x_loaded{r}") for r in range(4)]
        stats_done, aggr_done = sem("stats_done"), sem("aggr_done")
        ln_done, rsq_done = sem("ln_done"), sem("rsq_done")
        pool_chain = sem("pool_chain")
        xn_ready = sem("xn_ready")
        xT_ps_ready, xT_ready, xT_hi_ready, xT_lo_ready = (sem(n) for n in ("xT_ps_ready", "xT_ready", "xT_hi_ready", "xT_lo_ready"))
        qk_ps_ready, qk_ready, qk_hi_ready, qk_lo_ready = (sem(n) for n in ("qk_ps_ready", "qk_ready", "qk_hi_ready", "qk_lo_ready"))
        scr_written = sem("scr_written")
        stack_ready = [sem(f"stack_ready{r}") for r in range(4)]
        v_ps_ready, v_ready = sem("v_ps_ready"), sem("v_ready")
        s_ready, max_done = sem("s_ready"), sem("max_done")
        mT_ready, nm_made, nm_hi_ready, nm_ready, nm_rows = (sem(n) for n in ("mT_ready", "nm_made", "nm_hi_ready", "nm_ready", "nm_rows"))
        t_ready, exp_done, pv_done = sem("t_ready"), sem("exp_done"), sem("pv_done")
        oc_ready, sums_ready, lsum_done, rsum_ready, oT_ready = (sem(n) for n in ("oc_ready", "sums_ready", "lsum_done", "rsum_ready", "oT_ready"))
        xo_loaded, xo_biased, wo_ready, xo_ready, x_stored = (sem(n) for n in ("xo_loaded", "xo_biased", "wo_ready", "xo_ready", "x_stored"))

        def slots(eng, slot):
            for t in range(-6, 4):
                slot(t // 4, t % 4)
            with eng.Fori(1, NB - 2) as i:
                for g in range(4):
                    slot(i, g)
            for t in range(4 * (NB - 2), NT + 3):
                slot(t // 4, t % 4)

        def tile(i, g, lag):
            q = g + lag
            n = i + q // 4 if q // 4 else i
            t = 4 * n + q % 4
            if isinstance(t, int) and not 0 <= t < NT:
                return None
            return t, q % 4, n

        passed = all_sems("passed")

        def pass_on(eng, t):
            if not isinstance(t, int):
                eng.sem_inc(passed, 1)

        with nc.Block() as block:

            @block.sync
            def _(sp):
                first = [(ident, A["ident"]), (cosb, A["cosb"]), (sinb, A["sinb"]), (signb, A["signb"]),
                         (cols, A["at_cols"]), (wv, A["wvT"].rearrange("(k c) e -> c k e", k=2)),
                         (bvt, A["bvt"]), (wo, A["wo_pad"]), (bo, A["bo_rep"])]
                for dst, src in first:
                    sp.dma_start(dst[tuple(slice(None) for _ in dst.shape)], src).then_inc(w_in, 16)
                for m in range(2):
                    if m:
                        sp.wait_ge(wprep, 5)
                    for v, n in enumerate((("wqT", "wqTs"), ("wkT", "wkTs"))[m]):
                        sp.dma_start(wraw[:, v, :, :], A[n].rearrange("(k c) e -> c k e", k=2)).then_inc(w_in, 16)

                sp.sem_inc(x_stored, 16)

                def slot(i, g):
                    if w := tile(i, g, 6):
                        t, r, n = w
                        wait(sp, xn_ready, t - 3)
                        sp.dma_start(xin[:, r, :], x_in[bass.ds(t * P, P), :].rearrange("(h k) c -> k h c", h=4)).then_inc(x_loaded[r], 16)
                    if w := tile(i, g, 3):
                        t, r, n = w
                        sp.wait_ge(const_set, 6)
                        wait(sp, stack_ready[r], 96 * n)
                        pass_on(sp, t)
                        wait(sp, t_ready, 16 * (t - 3))
                        pass_on(sp, t)
                        for kind, src, ready, rows_q, rows_k in ((0, qk_hi, qk_hi_ready, (0, 32), (0, 16)),
                                                                 (1, qk_lo, qk_lo_ready, (16,), (32,))):
                            sp.wait_ge(ready, t + 1)
                            sp.dma_start(scr[r, kind].rearrange("(a p) t -> p a t", p=P), src[:, :, :].bitcast(F32)).then_inc(scr_written, 16)
                            sp.wait_ge(scr_written, 32 * t + 16 * (kind + 1))
                            for st, rows, col in ((qst, rows_q, 0), (kst, rows_k, D)):
                                for row in rows:
                                    sp.dma_start(st[row:row + 16, r, :, :].bitcast(F32),
                                                 scr[r, kind, col:col + D].rearrange("(j d) t -> d j t", d=DK)).then_inc(stack_ready[r], 16)
                    if w := tile(i, g, 1):
                        t, r, n = w
                        sp.wait_ge(const_set, 6)
                        sp.wait_ge(nm_ready, t + 1)
                        for row, src in ((48, nm_hi), (49, nm_lo)):
                            sp.dma_start(qst[row:row + 1, r, :, :].bitcast(F32).rearrange("o (c j) k -> o c (j k)", c=4),
                                         src[:, :, :, :].bitcast(F32).rearrange("c j k h -> c (j k h)")).then_inc(nm_rows, 16)
                    if g == 2 and (w := tile(i, g, -6)):
                        n = w[2]
                        sp.wait_ge(xo_ready, 2 * (n + 1))
                        sp.dma_start(x_out[bass.ds(n * 4 * P, 4 * P), :].rearrange("(k p) c -> p k c", p=P), xo[:, :, :]).then_inc(x_stored, 16)
                    if g == 1 and (w := tile(i, g, -5)):
                        n = w[2]
                        sp.wait_ge(x_stored, 16 * (n + 1))
                        sp.dma_start(xo[:, :, :], x_in[bass.ds(n * 4 * P, 4 * P), :].rearrange("(k p) c -> p k c", p=P)).then_inc(xo_loaded, 16)

                slots(sp, slot)
                sp.wait_ge(x_stored, 16 * (NB + 1))

            @block.gpsimd
            def _(pool):
                fills = [(eps[:, :], 1e-5), (vau[:, :, :, :, :], 1.0), (qst[:, :, :, :].bitcast(F32), 0.0)]
                fills += [(kst[a:b, :, :, :].bitcast(F32), v) for a, b, v in ((0, 32, 0.0), (32, 64, 1.0), (64, P, 0.0))]
                for n, (dst, value) in enumerate(fills):
                    wait(pool, const_set, n)
                    pool.memset(dst, value).then_inc(const_set, 1)

                def chain(ins, count):
                    ins.then_inc(pool_chain, 1)
                    pool.wait_ge(pool_chain, count)

                def slot(i, g):
                    if w := tile(i, g, 3):
                        t = w[0]
                        pool.wait_ge(qk_hi_ready, t + 1)
                        wait(pool, scr_written, 32 * t)
                        pool.tensor_tensor(qk_lo[:, :, :], qk[:, :, :], qk_hi[:, :, :], ALU.subtract).then_inc(qk_lo_ready, 1)
                    if w := tile(i, g, 1):
                        t = w[0]
                        pool.wait_ge(nm_hi_ready, t + 1)
                        wait(pool, nm_rows, 32 * t)
                        pool.tensor_tensor(nm_lo[:, :, :, :], nm[:, :, :, :], nm_hi[:, :, :, :], ALU.subtract).then_inc(nm_ready, 1)
                    if w := tile(i, g, -2):
                        t, r, n = w
                        pool.wait_ge(rsum_ready, t + 1)
                        if r == 0:
                            wait(pool, wo_ready, 2 * n)
                        pool.tensor_tensor(oT[:, r, :].rearrange("p (k j) -> p j k", j=NJ), oc[:, :].rearrange("p (j k) -> p j k", j=NJ),
                                           rsum[:, 1, :].rearrange("p (j k) -> p j k", j=NJ), ALU.mult).then_inc(oT_ready, 1)
                    if w := tile(i, g, 5):
                        t, r, n = w
                        p = r % 2
                        pool.wait_ge(rsq_done, t + 1)
                        y, v, a, b = rs[:, p, 1:2], mv[:, p, 1:2], rs[:, p, 2:3], rs[:, p, 3:4]
                        chain(pool.tensor_tensor(a, y, y, ALU.mult), 5 * t + 1)
                        chain(pool.tensor_tensor(b, v, eps[:, :], ALU.add), 5 * t + 2)
                        chain(pool.tensor_tensor(a, a, b, ALU.mult), 5 * t + 3)
                        pass_on(pool, t)
                        chain(pool.tensor_scalar(a, a, -0.5, 1.5, ALU.mult, ALU.add), 5 * t + 4)
                        chain(pool.tensor_tensor(y, y, a, ALU.mult), 5 * t + 5)
                    if w := tile(i, g, 4):
                        t = w[0]
                        pool.wait_ge(xT_hi_ready, t + 1)
                        wait(pool, qk_ps_ready, t)
                        pool.tensor_tensor(xT_lo[:, :, :], xT[:, w[1] % 2, :, :], xT_hi[:, :, :], ALU.subtract).then_inc(xT_lo_ready, 1)
                    if g == 1 and (w := tile(i, g, -5)):
                        n = w[2]
                        pool.wait_ge(xo_loaded, 16 * (n + 1))
                        bo_all = bo[:, :].unsqueeze(1).broadcast_to([P, 4, D])
                        pool.tensor_tensor(xo[:, :, :], xo[:, :, :], bo_all, ALU.add).then_inc(xo_biased, 1)

                slots(pool, slot)

            @block.scalar
            def _(act):
                act.preload_act_table_set("natural_log_exp_and_others")
                act.wait_ge(const_set, 6)

                def exp(t, r, k):
                    act.wait_ge(t_ready, 16 * t + k + 1)
                    wait(act, pv_done, 4 * (t - 1))
                    act.activation(probs[:, r % 2, k, :], t_ps[:, k % 2, :], ACT.Exp, scale=SCALE).then_inc(exp_done, 1)

                def slot(i, g):
                    for k in range(16):
                        if w := tile(i, g, 0):
                            exp(w[0], w[1], k)
                        if k == 9 and (w := tile(i, g, 1)):
                            t = w[0]
                            act.wait_ge(mT_ready, t + 1)
                            wait(act, nm_ready, t)
                            wait(act, nm_rows, 32 * t)
                            m_ps = f_ps[0:4, :].rearrange("c (h j k) -> c j k h", h=4, j=4)
                            act.activation(nm[:, :, :, :], m_ps, ACT.Copy, scale=-1.0).then_inc(nm_made, 1)
                            act.activation(nm_hi[:, :, :, :], m_ps, ACT.Copy, scale=-1.0).then_inc(nm_hi_ready, 1)
                        if k == 15 and (w := tile(i, g, -1)):
                            t = w[0]
                            act.wait_ge(pv_done, 4 * t + 4)
                            wait(act, oT_ready, t)
                            act.activation(oc[:, :], o_ps[:, :], ACT.Copy).then_inc(oc_ready, 1)
                        if k == 3 and (w := tile(i, g, -2)):
                            t = w[0]
                            act.wait_ge(sums_ready, t + 1)
                            act.activation(rsum[:, 0, :], sums[:, :], ACT.Ln).then_inc(lsum_done, 1)
                            act.wait_ge(lsum_done, t + 1)
                            act.activation(rsum[:, 1, :], rsum[:, 0, :], ACT.Exp, scale=-1.0).then_inc(rsum_ready, 1)
                        if k == 3 and (w := tile(i, g, 3)):
                            t = w[0]
                            act.wait_ge(qk_ready, t + 1)
                            wait(act, scr_written, 32 * t)
                            act.activation(qk_hi[:, :, :], qk[:, :, :], ACT.Copy).then_inc(qk_hi_ready, 1)
                        if k == 12 and (w := tile(i, g, 5)):
                            t, r, n = w
                            p = r % 2
                            act.wait_ge(aggr_done, t + 1)
                            wait(act, xn_ready, t - 1)
                            act.activation(rs[:, p, 0:1], mv[:, p, 1:2], ACT.Ln, bias=eps[:, :]).then_inc(ln_done, 1)
                            act.wait_ge(ln_done, t + 1)
                            act.activation(rs[:, p, 1:2], rs[:, p, 0:1], ACT.Exp, scale=-0.5).then_inc(rsq_done, 1)
                        if k == 13 and (w := tile(i, g, 4)):
                            t = w[0]
                            act.wait_ge(xT_ps_ready, t + 1)
                            wait(act, xT_lo_ready, t)
                            wait(act, v_ps_ready, t - 1)
                            t_in = f_ps[:, 0:2 * P].rearrange("p (k t) -> p k t", k=2)
                            act.activation(xT[:, w[1] % 2, :, :], t_in, ACT.Copy).then_inc(xT_ready, 1)
                            act.activation(xT_hi[:, :, :], t_in, ACT.Copy).then_inc(xT_hi_ready, 1)

                slots(act, slot)

            @block.vector
            def _(dve):
                done = [0]

                def link(ins):
                    done[0] += 1
                    ins.then_inc(wprep, 1)
                    dve.wait_ge(wprep, done[0])

                dve.wait_ge(w_in, 16 * 11)
                link(dve.tensor_tensor(sinb[:, :], sinb[:, :], signb[:, :], ALU.mult))
                for m in range(2):
                    if m:
                        dve.wait_ge(w_in, 16 * 13)
                    for kt in range(2):
                        link(dve.tensor_tensor(wraw[:, 1, kt, :], wraw[:, 1, kt, :], sinb[:, :], ALU.mult)) if kt == 0 else \
                            dve.tensor_tensor(wraw[:, 1, kt, :], wraw[:, 1, kt, :], sinb[:, :], ALU.mult).then_inc(wprep, 1)
                    done[0] += 1
                    cos2 = cosb[:, :].unsqueeze(1).broadcast_to([P, 2, D])
                    dve.wait_ge(wprep, done[0])
                    if m == 0:
                        link(dve.tensor_tensor(wrot[:, :, :], wraw[:, 0, :, :], cos2, ALU.mult))
                        link(dve.tensor_tensor(wrot[:, :, :], wrot[:, :, :], wraw[:, 1, :, :], ALU.add))
                    else:
                        link(dve.tensor_tensor(wrot[:, :, :], wraw[:, 0, :, :], cos2, ALU.mult))
                        link(dve.tensor_tensor(wrot[:, :, :], wrot[:, :, :], wraw[:, 1, :, :], ALU.add))
                    link(dve.tensor_copy(w_hi[:, m, :, :], wrot[:, :, :]))
                    link(dve.tensor_tensor(w_lo[:, m, :, :], wrot[:, :, :], w_hi[:, m, :, :], ALU.subtract))
                link(dve.tensor_tensor(cols[:, 9:10], cols[:, 9:10], cols[:, 10:11], ALU.mult))
                link(dve.tensor_scalar(cols[:, 4:8], cols[:, 4:8], cols[:, 9:10], None, ALU.mult))
                link(dve.tensor_scalar(bqk[:, :], cols[:, 0:4], cols[:, 8:9], None, ALU.mult))
                link(dve.tensor_tensor(bqk[:, :], bqk[:, :], cols[:, 4:8], ALU.add))
                dve.wait_ge(const_set, 6)

                def max_pair(t, m):
                    dve.wait_ge(s_ready, 8 * t + m + 1)
                    if m == 0:
                        wait(dve, mT_ready, t - 1)
                    h, c = m // 2, 2 * (m % 2)
                    out = mx[:, parity[0], 4 * h + c:4 * h + c + 2]
                    dve.tensor_reduce(out, s_ps[:, m % 2, :, :], AX.X, ALU.max).then_inc(max_done, 1)

                parity = [0]

                def project_out(n, part):
                    dve.wait_ge(xo_biased, n + 1)
                    dve.wait_ge(wo_ready, 2 * n + part + 1)
                    dve.tensor_tensor(xo[:, 2 * part:2 * part + 2, :], f_ps[:, :].rearrange("p (a c) -> p a c", a=2),
                                      xo[:, 2 * part:2 * part + 2, :], ALU.add).then_inc(xo_ready, 1)

                def slot(i, g):
                    ahead = tile(i, g, 2)

                    def mp(m):
                        if ahead:
                            parity[0] = ahead[1] % 2
                            max_pair(ahead[0], m)

                    if w := tile(i, g, -2):
                        t = w[0]
                        dve.wait_ge(oc_ready, t + 1)
                        wait(dve, lsum_done, t)
                        pass_on(dve, t)
                        dve.stream_shuffle(sums[:, :], oc[:, :], [16 + q % 16 for q in range(32)]).then_inc(sums_ready, 1)
                    if g == 2 and (w := tile(i, g, -6)):
                        project_out(w[2], 1)
                    mp(0)
                    if w := tile(i, g, 3):
                        t = w[0]
                        dve.wait_ge(qk_ps_ready, t + 1)
                        wait(dve, qk_lo_ready, t)
                        b_all = bqk[:, :].unsqueeze(2).broadcast_to([P, 4, P])
                        dve.tensor_tensor(qk[:, :, :], f_ps[:, :].rearrange("p (a t) -> p a t", a=4), b_all, ALU.add).then_inc(qk_ready, 1)
                    mp(1)
                    if w := tile(i, g, 2):
                        t, r, n = w
                        dve.wait_ge(v_ps_ready, t + 1)
                        wait(dve, pv_done, 4 * (t - 3))
                        v_in = f_ps[:, 0:256].rearrange("p (h c d) -> p h c d", h=4, d=DK)
                        v_b = bvt[:, :].rearrange("p (c d) -> p c d", d=DK).unsqueeze(1).broadcast_to([P, 4, 4, DK])
                        dve.tensor_tensor(vau[:, r, :, :, 0:DK], v_in, v_b, ALU.add).then_inc(v_ready, 1)
                    mp(2)
                    if w := tile(i, g, 5):
                        t, r, n = w
                        dve.wait_ge(x_loaded[r], 16 * (n + 1))
                        wait(dve, xn_ready, t - 1)
                        wait(dve, aggr_done, t)
                        dve.bn_stats(stats[:, :], xin[:, r, :]).then_inc(stats_done, 1)
                    mp(3)
                    if w := tile(i, g, 5):
                        t, r, n = w
                        dve.wait_ge(stats_done, t + 1)
                        pass_on(dve, t)
                        dve.bn_aggr(mv[:, r % 2, :], stats[:, :]).then_inc(aggr_done, 1)
                    mp(4)
                    mp(5)
                    mp(6)
                    mp(7)
                    if w := tile(i, g, 5):
                        t, r, n = w
                        dve.wait_ge(pool_chain, 5 * t + 5)
                        wait(dve, xT_ps_ready, t)
                        dve.tensor_scalar(xn[:, :], xin[:, r, :], mv[:, r % 2, 0:1], rs[:, r % 2, 1:2],
                                          ALU.subtract, ALU.mult).then_inc(xn_ready, 1)
                    if g == 1 and (w := tile(i, g, -5)):
                        project_out(w[2], 0)

                slots(dve, slot)

            @block.tensor
            def _(pe):
                S_AT = (1, 3, 5, 7, 9, 11, 13, 15)
                PV_AT, QK_AT, V_AT, MT_AT, XT_AT = 15, 2, 4, 8, 11
                pe.wait_ge(w_in, 16 * 13)
                pe.wait_ge(wprep, 17)
                pe.wait_ge(const_set, 6)

                def of_head(stack, r, h, rows, chunk=None):
                    seq = stack[0:rows, r, :, :].rearrange("r j (k h) -> r (j k) h", h=4)
                    return seq[:, :, h] if chunk is None else seq[:, chunk * P:(chunk + 1) * P, h]

                def scores_T(t, r, k):
                    c, h = k // 4, k % 4
                    wait(pe, exp_done, 16 * t + k - 1)
                    pe.matmul(t_ps[:, k % 2, :], of_head(kst, r, h, 64, c), of_head(qst, r, h, 64), start=True, stop=True).then_inc(t_ready, 1)

                def scores(t, r, m):
                    wait(pe, max_done, 8 * t + m - 1)
                    h, c = m // 2, 2 * (m % 2)
                    for a in range(2):
                        last = pe.matmul(s_ps[:, m % 2, a, :], of_head(qst, r, h, 48, c + a), of_head(kst, r, h, 48), start=True, stop=True)
                    last.then_inc(s_ready, 1)

                def values(t, r, c):
                    pe.wait_ge(exp_done, 16 * t + 4 * c + 4)
                    if c == 0:
                        wait(pe, oc_ready, t)
                        pe.wait_ge(v_ready, t + 1)
                    for h in range(4):
                        last = pe.matmul(o_ps[32 * h:32 * h + 32, :], vau[:, r, h, c, :], probs[:, r % 2, 4 * c + h, :],
                                         start=(c == 0), stop=(c == 3))
                    last.then_inc(pv_done, 1)

                def slot(i, g):
                    now, ahead, front = tile(i, g, 0), tile(i, g, 2), tile(i, g, 3)
                    batch = tile(i, g, -4 - g) if g in (1, 2) else None
                    for k in range(16):
                        if now:
                            if k == 0:
                                pe.wait_ge(nm_rows, 32 * (now[0] + 1))
                            scores_T(now[0], now[1], k)
                        if ahead and k in S_AT:
                            if k == S_AT[0]:
                                pe.wait_ge(stack_ready[ahead[1]], 96 * (ahead[2] + 1))
                            scores(ahead[0], ahead[1], S_AT.index(k))
                        if (g, k) in ((1, 14), (2, 0)) and batch:
                            project(i, g - 1, batch[2])
                        if k == QK_AT and front:
                            t = front[0]
                            pe.wait_ge(xT_lo_ready, t + 1)
                            if g == 2 and batch:
                                pe.wait_ge(xo_ready, 2 * (batch[2] + 1))
                            for a in range(4):
                                m, et = a // 2, a % 2
                                parts = [(wt, xt, kt) for kt in range(2) for wt, xt in ((w_hi, xT_hi), (w_lo, xT_hi), (w_hi, xT_lo))]
                                for n3, (wt, xt, kt) in enumerate(parts):
                                    last = pe.matmul(f_ps[:, a * P:(a + 1) * P], wt[:, m, kt, et * P:(et + 1) * P], xt[:, kt, :],
                                                     start=(n3 == 0), stop=(n3 == 5))
                            last.then_inc(qk_ps_ready, 1)
                        if k == PV_AT and (w := tile(i, g, -1)):
                            for c in range(4):
                                values(w[0], w[1], c)
                        if k == V_AT and ahead:
                            t = ahead[0]
                            if front:
                                pe.wait_ge(qk_ready, t + 2)
                            else:
                                pe.wait_ge(xT_hi_ready, NT)
                                pe.wait_ge(nm_hi_ready, t - 1)
                                if batch:
                                    wait(pe, xo_ready, 2 * (batch[2] + g - 1))
                            for h in range(4):
                                for kt in range(2):
                                    for jj in range(4):
                                        wv_j = wv[:, kt, :].rearrange("p (c j d) -> p j c d", c=4, j=4)[:, jj, :, :]
                                        last = pe.matmul(f_ps[32 * jj:32 * jj + 32, 64 * h:64 * h + 64],
                                                         xT[:, ahead[1] % 2, kt, :].rearrange("c (k h) -> c k h", h=4)[:, :, h],
                                                         wv_j, start=(kt == 0), stop=(kt == 1), skip_group_check=True)
                            last.then_inc(v_ps_ready, 1)
                        if k == MT_AT and (w := tile(i, g, 1)):
                            t, r, n = w
                            if ahead:
                                pe.wait_ge(v_ready, ahead[0] + 1)
                            else:
                                pe.wait_ge(v_ready, NT)
                                pe.wait_ge(xT_hi_ready, NT)
                                pe.wait_ge(nm_hi_ready, t)
                                if batch:
                                    wait(pe, xo_ready, 2 * (batch[2] + g - 1))
                            pe.wait_ge(max_done, 8 * t + 8)
                            for h in range(4):
                                last = pe.transpose(f_ps[0:4, h * P:(h + 1) * P], mx[:, r % 2, 4 * h:4 * h + 4], ident[:, :])
                            last.then_inc(mT_ready, 1)
                        if k == XT_AT and (w := tile(i, g, 4)):
                            t = w[0]
                            pe.wait_ge(xn_ready, t + 1)
                            wait(pe, qk_ready, t)
                            wait(pe, v_ready, t - 1)
                            wait(pe, nm_hi_ready, t - 2)
                            for kt in range(2):
                                last = pe.transpose(f_ps[:, kt * P:(kt + 1) * P], xn[:, kt * P:(kt + 1) * P], ident[:, :])
                            last.then_inc(xT_ps_ready, 1)

                def project(i, part, n):
                    if part == 0:
                        pe.wait_ge(oT_ready, 4 * n + 4)
                        if w := tile(i, 1, 4):
                            pe.wait_ge(xT_hi_ready, w[0] + 1)
                        else:
                            pe.wait_ge(xT_hi_ready, NT)
                            pe.wait_ge(nm_hi_ready, min(4 * i + 3, NT))
                    else:
                        pe.wait_ge(xo_ready, 2 * n + 1)
                    for a in range(2):
                        tok = slice((2 * part + a) * P, (2 * part + a + 1) * P)
                        for gg in range(4):
                            last = pe.matmul(f_ps[:, a * D:(a + 1) * D], oT[:, gg, tok], wo[:, gg, :], start=(gg == 0), stop=(gg == 3))
                    last.then_inc(wo_ready, 1)

                slots(pe, slot)


class Steps:
    def __init__(self, eng, sem, per_batch):
        self.eng, self.sem, self.per_batch = eng, sem, per_batch

    def begin(self, n):
        self.base, self.count = n * self.per_batch, 0

    def mark(self, ins):
        ins.then_inc(self.sem, 1)
        self.count += 1

    def settle(self):
        self.eng.wait_ge(self.sem, self.base + self.count)

    def __call__(self, ins):
        self.mark(ins)
        self.settle()


def batch_slots(eng, slot):
    slot(-1, 1, (0, 0))
    slot(0, 0, (1, 1))
    with eng.Fori(0, (NB - 2) // 2) as i:
        slot(2 * i + 1, 1, (2 * i + 2, 0))
        slot(2 * i + 2, 0, (2 * i + 3, 1))
    slot(NB - 1, 1, None)


def dve_normalise(dve, steps, passed, x, xn, stats, mv, rs, eps, var_ready, rs_ready, xn_ready, n, part):
    if part == 0:
        for k in range(4):
            steps.mark(dve.bn_stats(stats[:, k, :], x[:, k, :]))
        for k in range(4):
            if k == 0:
                steps.settle()
                dve.sem_inc(passed, 1)
            ins = dve.bn_aggr(mv[:, k, :], stats[:, k, :])
            steps.mark(ins) if k < 3 else ins.then_inc(var_ready, 1)
    else:
        dve.wait_ge(rs_ready, n + 1)
        y, v, a, b = rs[:, 0, :], mv[:, :, 1], rs[:, 1, :], rs[:, 2, :]
        steps(dve.tensor_tensor(a, y, y, ALU.mult))
        steps(dve.tensor_scalar(b, v, eps, None, ALU.add))
        steps(dve.tensor_tensor(a, a, b, ALU.mult))
        steps(dve.tensor_scalar(a, a, -0.5, 1.5, ALU.mult, ALU.add))
        steps(dve.tensor_tensor(rs[:, 3, :], y, a, ALU.mult))
        for k in range(4):
            last = dve.tensor_scalar(xn[:, k, :], x[:, k, :], mv[:, k, 0:1], rs[:, 3, k:k + 1], ALU.subtract, ALU.mult)
        last.then_inc(xn_ready, 1)


def dve_top2(dve, steps, p, order, work, small):
    bc = lambda s: s.unsqueeze(2).broadcast_to([P, 4, 8])
    m, m1, c = work[:, 0], work[:, 1], work[:, 2]
    steps(dve.tensor_reduce(small[:, 0, :], p, AX.X, ALU.add))
    steps(dve.reciprocal(small[:, 1, :], small[:, 0, :]))
    steps(dve.tensor_tensor(p, p, bc(small[:, 1, :]), ALU.mult))
    left = p
    for r, mask in enumerate((m, m1)):
        steps(dve.tensor_reduce(small[:, 2, :], left, AX.X, ALU.max))
        steps(dve.tensor_tensor(c, left, bc(small[:, 2, :]), ALU.is_equal))
        steps(dve.tensor_tensor(c, c, order, ALU.mult))
        steps(dve.tensor_reduce(small[:, 3, :], c, AX.X, ALU.max))
        steps(dve.tensor_tensor(mask, c, bc(small[:, 3, :]), ALU.is_equal))
        if r == 0:
            left = work[:, 3]
            steps(dve.scalar_tensor_tensor(left, mask, -2.0, p, ALU.mult, ALU.add))
    steps(dve.tensor_tensor(m, m, m1, ALU.add))
    return m


def moe_swiglu_phase(nc, sem, A, x_in, x_out):
    E, F = 8, 352
    FT = [(0, 128), (128, 128), (256, 96)]
    N_STEPS = 4 + 3 + 5 + 1 + 15
    with ExitStack() as ctx:
        sb = lambda name, shape, dt=F32: ctx.enter_context(nc.sbuf_tensor("m0_" + name, shape, dt))
        ident = sb("ident", [P, P])
        w1_hi, w1_lo = (sb(f"w1_{s}", [P, E, 2, 2 * F], F32R) for s in ("hi", "lo"))
        w2_hi, w2_lo = (sb(f"w2_{s}", [P, E, 3, D], F32R) for s in ("hi", "lo"))
        rw = sb("rw", [P, 2, E])
        order = sb("order", [P, 4, E])
        eps = sb("eps", [P, 1])
        x = sb("x", [P, 2, 4, D])
        xn = sb("xn", [P, 4, D])
        stats, mv, rs = sb("stats", [P, 4, 6]), sb("mv", [P, 4, 2]), sb("rs", [P, 4, 4])
        xT = sb("xT", [P, 2, T])
        xT_hi, xT_lo = (sb(f"xT_{s}", [P, 2, 2, T], F32R) for s in ("hi", "lo"))
        p = sb("p", [P, 4, E])
        work, small = sb("work", [P, 4, 4, E]), sb("small", [P, 4, 4])
        prob = sb("prob", [P, 2, 4, E])
        raw = sb("raw", [P, 2, 3 * D])
        g = sb("g", [P, 2, T])
        g_hi, g_lo = (sb(f"g_{s_}", [P, 2, 3, T], F32R) for s_ in ("hi", "lo"))
        y_ps = ctx.enter_context(nc.psum_tensor("m0_y_ps", [P, 2, 2, T], F32))
        o_ps = ctx.enter_context(nc.psum_tensor("m0_o_ps", [P, 2, 2, D], F32))
        f_ps = ctx.enter_context(nc.psum_tensor("m0_f_ps", [P, 2, T], F32))

        names = """const_in w_hi w_ready x_stored steps var_ready ln_ready rs_ready xn_ready xT_ps xT_ready xT_hi_ready xT_lo_ready
                   logits z_ready exp_ready prob_ready y_ready silu_ready g_ready g_hi_ready g_lo_ready o_ready acc_done const_set"""
        (const_in, w_hi_s, w_ready, x_stored, steps_s, var_ready, ln_ready, rs_ready, xn_ready, xT_ps, xT_ready, xT_hi_ready, xT_lo_ready,
         logits, z_ready, exp_ready, prob_ready, y_ready, silu_ready, g_ready, g_hi_ready, g_lo_ready, o_ready, acc_done,
         const_set) = (sem("m0_" + q) for q in names.split())
        w_in = [sem(f"m0_w_in{r}") for r in range(2)]
        passed = sem("passed")
        x_loaded = [sem(f"m0_x_loaded{r}") for r in range(2)]

        def pieces(e):
            r3, f3 = F - 2 * P, lambda t, a, b: t[:, e, a:b, :]
            for j in range(3):
                r = (3 * e + j) % 2
                if j < 2:
                    yield r, [(raw[:, r, 0:2 * F], A["m0_w1"][e, j * P:(j + 1) * P], w1_hi[:, e, j, :], w1_lo[:, e, j, :])]
                else:
                    raw_3 = raw[:, r, :].rearrange("p (f c) -> p f c", f=3)
                    yield r, [(raw_3[:, 0:2, :], A["m0_w2"][e, 0:2 * P].rearrange("(k c) f -> c k f", k=2), f3(w2_hi, 0, 2), f3(w2_lo, 0, 2)),
                              (raw_3[0:r3, 2, :], A["m0_w2"][e, 2 * P:F], w2_hi[0:r3, e, 2, :], w2_lo[0:r3, e, 2, :])]

        def low(pool, n, b):
            pool.wait_ge(xT_ready, n + 1)
            pool.wait_ge(xT_hi_ready, n + 1)
            if not isinstance(n, int) or n > 1:
                pool.wait_ge(y_ready, 3 * E * (n - 1))
            pool.tensor_tensor(xT_lo[:, b, :, :], xT[:, :, :], xT_hi[:, b, :, :], ALU.subtract).then_inc(xT_lo_ready, 1)

        def f_ring(e, f):
            return (3 * e + f) % 2

        with nc.Block() as block:

            @block.sync
            def _(sp):
                sp.dma_start(x[:, 0, :, :], x_in[0:T, :].rearrange("(k p) c -> p k c", p=P)).then_inc(x_loaded[0], 16)
                for dst, src in ((ident[:, :], A["ident"]), (rw[:, :, :], A["m0_rw"]), (order[:, :, :], A["order"])):
                    sp.dma_start(dst, src).then_inc(const_in, 16)
                for e in range(E):
                    for j, (r, parts) in enumerate(pieces(e)):
                        wait(sp, w_ready, 3 * e + j - 1)
                        for dst, src, _, _ in parts:
                            sp.dma_start(dst, src).then_inc(w_in[r], 16)
                    if e == 1:
                        sp.dma_start(x[:, 1, :, :], x_in[T:2 * T, :].rearrange("(k p) c -> p k c", p=P)).then_inc(x_loaded[1], 16)

                def store(n, b):
                    sp.wait_ge(acc_done, 2 * E * (n + 1))
                    sp.dma_start(x_out[bass.ds(n * T, T), :].rearrange("(k p) c -> p k c", p=P), x[:, b, :, :]).then_inc(x_stored, 16)

                def slot(n, b, following):
                    if isinstance(n, int) and n < 1:
                        return
                    store(n - 1, 1 - b)
                    sp.wait_ge(x_stored, 16 * n)
                    if following:
                        n1, b1 = following
                        sp.dma_start(x[:, b1, :, :], x_in[bass.ds(n1 * T, T), :].rearrange("(k p) c -> p k c", p=P)).then_inc(x_loaded[b1], 16)

                batch_slots(sp, slot)
                store(NB - 1, 1)
                sp.wait_ge(x_stored, 16 * NB)

            @block.gpsimd
            def _(pool):
                pool.memset(eps[:, :], 1e-5).then_inc(const_set, 1)
                low(pool, 0, 0)
                for e in range(E):
                    for j, (r, parts) in enumerate(pieces(e)):
                        pool.wait_ge(w_hi_s, 3 * e + j + 1)
                        for src, _, hi, lo in parts:
                            last = pool.tensor_tensor(lo, src, hi, ALU.subtract)
                        last.then_inc(w_ready, 1)

                def slot(n, b, following):
                    if following and not (isinstance(n, int) and n < 0):
                        low(pool, *following)

                batch_slots(pool, slot)

            @block.scalar
            def _(act):
                def before(n, part):
                    if part == 0:
                        act.wait_ge(const_set, 1)
                        act.wait_ge(var_ready, n + 1)
                        wait(act, xn_ready, n)
                        act.activation(rs[:, 0, :], mv[:, :, 1], ACT.Ln, bias=eps[:, :]).then_inc(ln_ready, 1)
                        act.wait_ge(ln_ready, n + 1)
                        act.activation(rs[:, 0, :], rs[:, 0, :], ACT.Exp, scale=-0.5).then_inc(rs_ready, 1)
                    if part == 2:
                        act.wait_ge(z_ready, n + 1)
                        act.activation(p[:, :, :], p[:, :, :], ACT.Exp).then_inc(exp_ready, 1)

                def transposed(n, b):
                    act.wait_ge(xT_ps, n + 1)
                    wait(act, xT_lo_ready, n)
                    wait(act, logits, n)
                    if not isinstance(n, int) or n > 1:
                        act.wait_ge(y_ready, 3 * E * (n - 1))
                    act.activation(xT[:, :, :], f_ps[:, :, :], ACT.Copy).then_inc(xT_ready, 1)
                    act.activation(xT_hi[:, b, :, :], f_ps[:, :, :], ACT.Copy).then_inc(xT_hi_ready, 1)

                def upper(q, r, b2, f):
                    rows = FT[f][1]
                    act.wait_ge(g_ready, q + 1)
                    act.activation(g_hi[0:rows, b2, f, :], g[0:rows, r, :], ACT.Copy).then_inc(g_hi_ready, 1)

                def slot(n, b, following):
                    if isinstance(n, int) and n < 0:
                        before(0, 0)
                        transposed(0, 0)
                        for j in range(3):
                            split_hi(0, j)
                        before(0, 2)
                        return
                    for e in range(E):
                        for f in range(3):
                            q = 3 * E * n + 3 * e + f
                            rows = FT[f][1]
                            act.wait_ge(y_ready, q + 1)
                            wait(act, g_lo_ready, q - 1)
                            act.activation(g[0:rows, f_ring(e, f), :], y_ps[0:rows, f_ring(e, f), 0, :], ACT.Silu).then_inc(silu_ready, 1)
                            if f == 0 and not (isinstance(n, int) and n == 0 and e < 2):
                                act.wait_ge(o_ready, 2 * (E * n + e - 1))
                            if f:
                                upper(q - 1, f_ring(e, f - 1), e % 2, f - 1)
                            if isinstance(n, int) and n == 0 and e + 1 < E:
                                split_hi(e + 1, f)
                        upper(q, f_ring(e, 2), e % 2, 2)
                        if following:
                            if e == 2:
                                before(following[0], 0)
                            if e == 4:
                                transposed(*following)
                            if e == 6:
                                before(following[0], 2)

                def split_hi(e, j):
                    r, parts = list(pieces(e))[j]
                    loads = sum(len(list(pieces(0))[q % 3][1]) for q in range(3 * e + j + 1) if q % 2 == r)
                    act.wait_ge(w_in[r], 16 * loads)
                    for src, _, hi, _ in parts:
                        last = act.activation(hi, src, ACT.Copy)
                    last.then_inc(w_hi_s, 1)

                batch_slots(act, slot)

            @block.vector
            def _(dve):
                steps = Steps(dve, steps_s, N_STEPS)
                dve.wait_ge(const_in, 48)

                def before(n, b, part):
                    if part == 0:
                        steps.begin(n)
                        dve.wait_ge(x_loaded[b], 16 * ((n - b) // 2 + 1) if isinstance(n, int) else 8 * (n - b) + 16)
                        wait(dve, var_ready, n)
                        dve_normalise(dve, steps, passed, x[:, b], xn, stats, mv, rs, 1e-5, var_ready, rs_ready, xn_ready, n, 0)
                    if part == 1:
                        wait(dve, xT_ps, n)
                        dve_normalise(dve, steps, passed, x[:, b], xn, stats, mv, rs, 1e-5, var_ready, rs_ready, xn_ready, n, 1)
                    if part == 2:
                        z_in = f_ps[:, 0, 0:4 * E].rearrange("p (k e) -> p k e", k=4)
                        dve.wait_ge(logits, n + 1)
                        steps(dve.tensor_reduce(small[:, 0, :], z_in, AX.X, ALU.max))
                        dve.tensor_tensor(p[:, :, :], z_in, small[:, 0, :].unsqueeze(2).broadcast_to([P, 4, E]), ALU.subtract).then_inc(z_ready, 1)
                    if part == 3:
                        dve.wait_ge(exp_ready, n + 1)
                        mask = dve_top2(dve, steps, p[:, :, :], order[:, :, :], work, small)
                        dve.tensor_tensor(prob[:, b, :, :], p[:, :, :], mask, ALU.mult).then_inc(prob_ready, 1)
                        assert steps.count == N_STEPS, steps.count

                def accumulate(n, b, e):
                    if e == 0:
                        dve.wait_ge(prob_ready, n + 1)
                    for half in range(2):
                        q = 2 * (E * n + e) + half
                        dve.wait_ge(o_ready, q + 1)
                        wait(dve, acc_done, q - 1)
                        for a in range(2):
                            k = 2 * half + a
                            last = dve.scalar_tensor_tensor(x[:, b, k, :], o_ps[:, half, a, :], prob[:, b, k, e:e + 1], x[:, b, k, :], ALU.mult, ALU.add)
                        last.then_inc(acc_done, 1)

                def slot(n, b, following):
                    if isinstance(n, int) and n < 0:
                        for part in range(4):
                            before(0, 0, part)
                        return
                    for e in range(E):
                        for f in range(3):
                            q = 3 * E * n + 3 * e + f
                            rows, r = FT[f][1], f_ring(e, f)
                            dve.wait_ge(silu_ready, q + 1)
                            dve.tensor_tensor(g[0:rows, r, :], g[0:rows, r, :], y_ps[0:rows, r, 1, :], ALU.mult).then_inc(g_ready, 1)
                            dve.wait_ge(g_hi_ready, q + 1)
                            dve.tensor_tensor(g_lo[0:rows, e % 2, f, :], g[0:rows, r, :], g_hi[0:rows, e % 2, f, :], ALU.subtract).then_inc(g_lo_ready, 1)
                        if e:
                            accumulate(n, b, e - 1)
                        elif not (isinstance(n, int) and n == 0):
                            accumulate(n - 1, 1 - b, E - 1)
                        if following and e in (2, 3, 5, 6):
                            before(*following, (2, 3, 5, 6).index(e))

                batch_slots(dve, slot)
                accumulate(NB - 1, 1, E - 1)

            @block.tensor
            def _(pe):
                pe.wait_ge(const_in, 48)

                def transposes(n):
                    pe.wait_ge(xn_ready, n + 1)
                    wait(pe, z_ready, n)
                    for kt in range(2):
                        for k in range(4):
                            last = pe.transpose(f_ps[:, kt, k * P:(k + 1) * P], xn[:, k, kt * P:(kt + 1) * P], ident[:, :])
                    last.then_inc(xT_ps, 1)

                def router(n):
                    pe.wait_ge(xT_hi_ready, n + 1)
                    for k in range(4):
                        for kt in range(2):
                            last = pe.matmul(f_ps[:, 0, k * E:(k + 1) * E], xT[:, kt, k * P:(k + 1) * P], rw[:, kt, :], start=(kt == 0), stop=(kt == 1))
                    last.then_inc(logits, 1)

                def up(n, b, e):
                    for f, (f0, rows) in enumerate(FT):
                        q = 3 * E * n + 3 * e + f
                        wait(pe, g_ready, q - 1)
                        for half in range(2):
                            cols = slice(half * F + f0, half * F + f0 + rows)
                            parts = [(w, xt, kt) for kt in range(2) for w, xt in ((w1_hi, xT_hi), (w1_lo, xT_hi), (w1_hi, xT_lo))]
                            for m, (w, xt, kt) in enumerate(parts):
                                last = pe.matmul(y_ps[0:rows, f_ring(e, f), half, :], w[:, e, kt, cols], xt[:, b, kt, :], start=(m == 0), stop=(m == 5))
                        last.then_inc(y_ready, 1)

                def down(n, e):
                    pe.wait_ge(g_lo_ready, 3 * E * n + 3 * e + 3)
                    for half in range(2):
                        wait(pe, acc_done, 2 * (E * n + e - 1) + half + 1)
                        for a in range(2):
                            tok = slice((2 * half + a) * P, (2 * half + a + 1) * P)
                            parts = [(gg, w, f) for f in range(3) for gg, w in ((g_hi, w2_hi), (g_lo, w2_hi), (g_hi, w2_lo))]
                            for m, (gg, w, f) in enumerate(parts):
                                rows = FT[f][1]
                                last = pe.matmul(o_ps[:, half, a, :], gg[0:rows, e % 2, f, tok], w[0:rows, e, f, :], start=(m == 0), stop=(m == 8))
                        last.then_inc(o_ready, 1)

                def slot(n, b, following):
                    if isinstance(n, int) and n < 0:
                        transposes(0)
                        router(0)
                        return
                    pe.wait_ge(xT_lo_ready, n + 1)
                    for e in range(E):
                        if isinstance(n, int) and n == 0:
                            pe.wait_ge(w_ready, 3 * (e + 1))
                        up(n, b, e)
                        if e:
                            down(n, e - 1)
                        elif not (isinstance(n, int) and n == 0):
                            down(n - 1, E - 1)
                        if following and e == 4:
                            transposes(following[0])
                        if following and e == 5:
                            router(following[0])

                batch_slots(pe, slot)
                down(NB - 1, E - 1)


def moe_linear_phase(nc, sem, A, x_in, x_out):
    E, PAIRS = 8, 4
    N_STEPS = 4 + 3 + 5 + 3 + 15 + 4
    with ExitStack() as ctx:
        sb = lambda name, shape, dt=F32: ctx.enter_context(nc.sbuf_tensor("m1_" + name, shape, dt))
        ident = sb("ident", [P, P])
        w_hi, w_lo = (sb(f"w_{s}", [P, PAIRS, 2, 2 * D], F32R) for s in ("hi", "lo"))
        raw = sb("raw", [P, PAIRS, 2, 2 * D])
        gw = sb("gw", [P, 2, E])
        gb = sb("gb", [P, E])
        eb = sb("eb", [E, D])
        order = sb("order", [P, 4, E])
        eps = sb("eps", [P, 1])
        x = sb("x", [P, 2, 4, D])
        xn = sb("xn", [P, 4, D])
        stats, mv, rs = sb("stats", [P, 4, 6]), sb("mv", [P, 4, 2]), sb("rs", [P, 4, 4])
        xT = sb("xT", [P, 2, T])
        xT_hi, xT_lo = (sb(f"xT_{s}", [P, 2, 2, T], F32R) for s in ("hi", "lo"))
        p = sb("p", [P, 4, E])
        work, small = sb("work", [P, 4, 4, E]), sb("small", [P, 4, 4])
        comb = sb("comb", [P, 2, 4, E])
        combT = sb("combT", [E, 2, T])
        f_ps = ctx.enter_context(nc.psum_tensor("m1_f_ps", [P, 2, T], F32))
        o_ps = ctx.enter_context(nc.psum_tensor("m1_o_ps", [P, 4, 2 * D], F32))
        b_ps = ctx.enter_context(nc.psum_tensor("m1_b_ps", [P, 2, 2 * D], F32))

        names = """const_in w_in w_hi w_ready x_stored steps var_ready ln_ready rs_ready xn_ready xT_ps xT_ready xT_hi_ready xT_lo_ready
                   logits z_ready exp_ready comb_ready combT_ps combT_ready b_ready b_added o_ready acc_done const_set"""
        (const_in, w_in, w_hi_s, w_ready, x_stored, steps_s, var_ready, ln_ready, rs_ready, xn_ready, xT_ps, xT_ready, xT_hi_ready, xT_lo_ready,
         logits, z_ready, exp_ready, comb_ready, combT_ps, combT_ready, b_ready, b_added, o_ready, acc_done, const_set) = (sem("m1_" + q) for q in names.split())
        passed = sem("passed")
        x_loaded = [sem(f"m1_x_loaded{r}") for r in range(2)]
        UNITS = 4 * PAIRS

        def low(pool, n, b):
            pool.wait_ge(xT_ready, n + 1)
            pool.wait_ge(xT_hi_ready, n + 1)
            if not isinstance(n, int) or n > 1:
                pool.wait_ge(o_ready, UNITS * (n - 1))
            pool.tensor_tensor(xT_lo[:, b, :, :], xT[:, :, :], xT_hi[:, b, :, :], ALU.subtract).then_inc(xT_lo_ready, 1)

        with nc.Block() as block:

            @block.sync
            def _(sp):
                sp.dma_start(x[:, 0, :, :], x_in[0:T, :].rearrange("(k p) c -> p k c", p=P)).then_inc(x_loaded[0], 16)
                for dst, src in ((ident[:, :], A["ident"]), (gw[:, :, :], A["m1_gw"]), (gb[:, :], A["m1_gb"]), (eb[:, :], A["m1_eb"]),
                                 (order[:, :, :], A["order"])):
                    sp.dma_start(dst, src).then_inc(const_in, 16)
                for e in range(PAIRS):
                    sp.dma_start(raw[:, e, :, :], A["m1_w"][e].rearrange("(k c) f -> c k f", k=2)).then_inc(w_in, 16)

                def store(n, b):
                    sp.wait_ge(acc_done, UNITS * (n + 1))
                    sp.dma_start(x_out[bass.ds(n * T, T), :].rearrange("(k p) c -> p k c", p=P), x[:, b, :, :]).then_inc(x_stored, 16)

                def slot(n, b, following):
                    if isinstance(n, int) and n < 0:
                        return
                    if not (isinstance(n, int) and n == 0):
                        store(n - 1, 1 - b)
                        sp.wait_ge(x_stored, 16 * n)
                    if following:
                        n1, b1 = following
                        sp.dma_start(x[:, b1, :, :], x_in[bass.ds(n1 * T, T), :].rearrange("(k p) c -> p k c", p=P)).then_inc(x_loaded[b1], 16)

                batch_slots(sp, slot)
                store(NB - 1, 1)
                sp.wait_ge(x_stored, 16 * NB)

            @block.gpsimd
            def _(pool):
                pool.memset(eps[:, :], 1e-5).then_inc(const_set, 1)
                low(pool, 0, 0)
                for e in range(PAIRS):
                    pool.wait_ge(w_hi_s, e + 1)
                    pool.tensor_tensor(w_lo[:, e, :, :], raw[:, e, :, :], w_hi[:, e, :, :], ALU.subtract).then_inc(w_ready, 1)

                def slot(n, b, following):
                    if following and not (isinstance(n, int) and n < 0):
                        low(pool, *following)

                batch_slots(pool, slot)

            @block.scalar
            def _(act):
                act.preload_act_table_set("natural_log_exp_and_others")
                act.wait_ge(const_set, 1)

                def before(n, b, part):
                    if part == 0:
                        act.wait_ge(var_ready, n + 1)
                        wait(act, xn_ready, n)
                        act.activation(rs[:, 0, :], mv[:, :, 1], ACT.Ln, bias=eps[:, :]).then_inc(ln_ready, 1)
                        act.wait_ge(ln_ready, n + 1)
                        act.activation(rs[:, 0, :], rs[:, 0, :], ACT.Exp, scale=-0.5).then_inc(rs_ready, 1)
                    if part == 1:
                        act.wait_ge(xT_ps, n + 1)
                        wait(act, xT_lo_ready, n)
                        wait(act, logits, n)
                        if not isinstance(n, int) or n > 1:
                            act.wait_ge(o_ready, UNITS * (n - 1))
                        act.activation(xT[:, :, :], f_ps[:, :, :], ACT.Copy).then_inc(xT_ready, 1)
                        act.activation(xT_hi[:, b, :, :], f_ps[:, :, :], ACT.Copy).then_inc(xT_hi_ready, 1)
                    if part == 2:
                        act.wait_ge(z_ready, n + 1)
                        act.activation(p[:, :, :], p[:, :, :], ACT.Exp).then_inc(exp_ready, 1)
                    if part == 3:
                        act.wait_ge(combT_ps, n + 1)
                        if not isinstance(n, int) or n > 1:
                            act.wait_ge(b_ready, 2 * (n - 1))
                        act.activation(combT[:, b, :], f_ps[0:E, 0, :], ACT.Copy).then_inc(combT_ready, 1)

                def slot(n, b, following):
                    if isinstance(n, int) and n < 0:
                        for part in range(3):
                            before(0, 0, part)
                        for e in range(PAIRS):
                            if e == 0:
                                act.wait_ge(w_in, 16 * PAIRS)
                            act.activation(w_hi[:, e, :, :], raw[:, e, :, :], ACT.Copy).then_inc(w_hi_s, 1)
                        before(0, 0, 3)
                    elif following:
                        for part in range(4):
                            before(*following, part)

                batch_slots(act, slot)

            @block.vector
            def _(dve):
                steps = Steps(dve, steps_s, N_STEPS)
                dve.wait_ge(const_in, 80)

                def before(n, b, part):
                    if part == 0:
                        steps.begin(n)
                        dve.wait_ge(x_loaded[b], 16 * ((n - b) // 2 + 1) if isinstance(n, int) else 8 * (n - b) + 16)
                        wait(dve, var_ready, n)
                        dve_normalise(dve, steps, passed, x[:, b], xn, stats, mv, rs, 1e-5, var_ready, rs_ready, xn_ready, n, 0)
                    if part == 1:
                        wait(dve, xT_ps, n)
                        dve_normalise(dve, steps, passed, x[:, b], xn, stats, mv, rs, 1e-5, var_ready, rs_ready, xn_ready, n, 1)
                    if part == 2:
                        z_in = f_ps[:, 0, 0:4 * E].rearrange("p (k e) -> p k e", k=4)
                        bc = lambda s: s.unsqueeze(2).broadcast_to([P, 4, E])
                        dve.wait_ge(logits, n + 1)
                        steps(dve.tensor_tensor(p[:, :, :], z_in, gb[:, :].unsqueeze(1).broadcast_to([P, 4, E]), ALU.add))
                        steps(dve.tensor_scalar(p[:, :, :], p[:, :, :], 1e-4, None, ALU.max))
                        steps(dve.tensor_reduce(small[:, 0, :], p[:, :, :], AX.X, ALU.max))
                        dve.tensor_tensor(p[:, :, :], p[:, :, :], bc(small[:, 0, :]), ALU.subtract).then_inc(z_ready, 1)
                    if part == 3:
                        bc = lambda s: s.unsqueeze(2).broadcast_to([P, 4, E])
                        dve.wait_ge(exp_ready, n + 1)
                        mask = dve_top2(dve, steps, p[:, :, :], order[:, :, :], work, small)
                        steps(dve.scalar_tensor_tensor(work[:, 1], p[:, :, :], 0.1, mask, ALU.max, ALU.mult))
                        steps(dve.tensor_reduce(small[:, 0, :], work[:, 1], AX.X, ALU.add))
                        steps(dve.reciprocal(small[:, 1, :], small[:, 0, :]))
                        steps(dve.tensor_tensor(work[:, 1], work[:, 1], bc(small[:, 1, :]), ALU.mult))
                        dve.tensor_scalar(comb[:, b, :, :], work[:, 1], 0.5, None, ALU.mult).then_inc(comb_ready, 1)
                        assert steps.count == N_STEPS, steps.count

                def accumulate(n, b, u):
                    k, e = u // PAIRS, 2 * (u % PAIRS)
                    dve.wait_ge(o_ready, UNITS * n + u + 1)
                    if u % PAIRS == 0 and k % 2 == 0:
                        dve.wait_ge(b_ready, 2 * n + k // 2 + 1)
                        dve.tensor_tensor(x[:, b, k:k + 2, :], b_ps[:, k // 2, :].rearrange("p (a c) -> p a c", a=2), x[:, b, k:k + 2, :],
                                          ALU.add).then_inc(b_added, 1)
                        dve.wait_ge(b_added, 2 * n + k // 2 + 1)
                    else:
                        dve.wait_ge(acc_done, UNITS * n + u)
                    for a in range(2):
                        ins = dve.scalar_tensor_tensor(x[:, b, k, :], o_ps[:, u % 4, a * D:(a + 1) * D], comb[:, b, k, e + a:e + a + 1], x[:, b, k, :],
                                                       ALU.mult, ALU.add)
                        if a == 0:
                            ins.then_inc(half_s, 1)
                            dve.wait_ge(half_s, UNITS * n + u + 1)
                        else:
                            ins.then_inc(acc_done, 1)

                half_s = sem("m1_half_done")

                def slot(n, b, following):
                    if isinstance(n, int) and n < 0:
                        for part in range(4):
                            before(0, 0, part)
                        return
                    dve.wait_ge(comb_ready, n + 1)
                    for u in range(UNITS):
                        accumulate(n, b, u)
                        if following and u in (3, 5, 9, 11):
                            before(*following, (3, 5, 9, 11).index(u))

                batch_slots(dve, slot)

            @block.tensor
            def _(pe):
                pe.wait_ge(const_in, 80)

                def before(n, b, part):
                    if part == 0:
                        pe.wait_ge(xn_ready, n + 1)
                        wait(pe, combT_ready, n)
                        for kt in range(2):
                            for k in range(4):
                                last = pe.transpose(f_ps[:, kt, k * P:(k + 1) * P], xn[:, k, kt * P:(kt + 1) * P], ident[:, :])
                        last.then_inc(xT_ps, 1)
                    if part == 1:
                        pe.wait_ge(xT_hi_ready, n + 1)
                        for k in range(4):
                            for kt in range(2):
                                last = pe.matmul(f_ps[:, 0, k * E:(k + 1) * E], xT[:, kt, k * P:(k + 1) * P], gw[:, kt, :], start=(kt == 0), stop=(kt == 1))
                        last.then_inc(logits, 1)
                    if part == 2:
                        pe.wait_ge(comb_ready, n + 1)
                        for k in range(4):
                            last = pe.transpose(f_ps[0:E, 0, k * P:(k + 1) * P], comb[:, b, k, :], ident[:, :])
                        last.then_inc(combT_ps, 1)

                def slot(n, b, following):
                    if isinstance(n, int) and n < 0:
                        for part in range(3):
                            before(0, 0, part)
                        return
                    pe.wait_ge(xT_lo_ready, n + 1)
                    pe.wait_ge(combT_ready, n + 1)
                    for u in range(UNITS):
                        k, e = u // PAIRS, u % PAIRS
                        tok = slice(k * P, (k + 1) * P)
                        if u % PAIRS == 0 and k % 2 == 0:
                            wait(pe, b_added, 2 * n + k // 2 - 1)
                            for a in range(2):
                                last = pe.matmul(b_ps[:, k // 2, a * D:(a + 1) * D], combT[:, b, (k + a) * P:(k + a + 1) * P], eb[:, :], start=True, stop=True)
                            last.then_inc(b_ready, 1)
                        if isinstance(n, int) and n == 0 and k == 0:
                            pe.wait_ge(w_ready, e + 1)
                        wait(pe, acc_done, UNITS * n + u - 3)
                        parts = [(xt, w, kt) for kt in range(2) for xt, w in ((xT_hi, w_hi), (xT_lo, w_hi), (xT_hi, w_lo))]
                        for m, (xt, w, kt) in enumerate(parts):
                            last = pe.matmul(o_ps[:, u % 4, :], xt[:, b, kt, tok], w[:, e, kt, :], start=(m == 0), stop=(m == 5))
                        last.then_inc(o_ready, 1)
                        if following and u in (8, 10, 14):
                            before(*following, (8, 10, 14).index(u))

                batch_slots(pe, slot)


DI = 2 * D
DS, DTR = 16, 16
ND = DI // P
NP = DS // 2

SCHEDULE = {
    0: [("load", 0), ("final", 3)], 1: [("z", 0), ("z", 1), ("ln", 0)], 2: [("dt", 1)],
    3: [("z", 2), ("z", 3), ("silu_z", 0), ("rsqrt", 0), ("ln", 1)], 4: [("out", 0), ("out", 1)], 5: [("sum", 0), ("rsqrt", 1)], 7: [("ln", 2)],
    8: [("final", 0)], 9: [("dt", 2)], 10: [("tr", 0), ("tr", 1)], 13: [("xi", 0), ("xi", 1)],
    15: [("conv", 0)], 16: [("final", 1), ("conv", 1)], 17: [("xi", 2), ("xi", 3)], 19: [("conv", 2)],
    20: [("conv", 3), ("silu_u", 0), ("split", 0), ("split", 1)], 18: [("dt", 3)], 23: [("ux", 0), ("ux", 1), ("split", 2), ("split", 3)],
    24: [("final", 2)], 26: [("ux", 2), ("ux", 3), ("xd", 0), ("bc", 0), ("bc", 1), ("bc", 2)],
    27: [("bc", 3)], 28: [("dt0", 0), ("bc", 4)], 29: [("bc", 5)], 30: [("bc", 6)], 31: [("bc", 7)],
}
NEXT = ("load", "ln", "rsqrt", "sum", "tr", "xi", "conv", "silu_u", "split", "ux", "xd", "dt0", "bc")
LAST = ("out",)
FILLS = [task for at in sorted(SCHEDULE) for task in SCHEDULE[at] if task[0] in ("out", "z", "dt", "dt0", "tr", "xi", "conv")]


def mamba_phase(nc, sem, A, x_in, x_out):
    with ExitStack() as ctx:
        sb = lambda name, shape, dt=F32: ctx.enter_context(nc.sbuf_tensor("mb_" + name, shape, dt))
        ident = sb("ident", [P, P])
        cols = sb("cols", [P, 4, 9])
        lnc = sb("lnc", [P, 2, 2])
        a_neg = sb("a_neg", [P, ND, DS])
        fix = sb("fix", [P, 3])
        diag = sb("diag", [P, ND, 4, P])
        wi_hi, wi_lo = (sb(f"wi_{s}", [P, 2, 2 * DI], F32R) for s in ("hi", "lo"))
        wo_hi, wo_lo = (sb(f"wo_{s}", [P, ND, D], F32R) for s in ("hi", "lo"))
        wx_hi, wx_lo = (sb(f"wx_{s}", [P, ND, 48], F32R) for s in ("hi", "lo"))
        wdt = sb("wdt", [DTR, DI])
        xin = sb("xin", [P, 4, D])
        res = sb("res", [P, 2, 4, D])
        xn = sb("xn", [P, 4, D])
        stats, mv, rs = sb("stats", [P, 2, 4, 6]), sb("mv", [P, 2, 4, 2]), sb("rs", [P, 2, 4, 4])
        hT_hi, hT_lo = (sb(f"hT_{s}", [P, 2, T], F32R) for s in ("hi", "lo"))
        xi = sb("xi", [P, 2, T + 3])
        u = sb("u", [P, 2, ND, T])
        u_hi, u_lo = (sb(f"u_{s}", [P, 2, T], F32R) for s in ("hi", "lo"))
        z = sb("z", [P, ND, T])
        xd = sb("xd", [DTR + 2 * DS, T])
        ex, lg = (sb(n, [P, T]) for n in ("ex", "lg"))
        dt, dtu = sb("dt", [P, 2, T]), sb("dtu", [P, 2, T])
        bbc, cbc = sb("bbc", [P, DS, T]), sb("cbc", [P, DS, T])
        raw_wi, raw_wo = bbc[:, 0:4, :].rearrange("p (k a) t -> p k (a t)", k=2), bbc[:, 4:6, :].rearrange("p a (b e) -> p (a b) e", b=2)
        raw_wx = bbc[:, 6, 0:ND * 48].rearrange("p (d e) -> p d e", d=ND)
        dbu = sb("dbu", [P, 2, 2, T])
        hc = sb("hc", [P, 2, 2, T])
        y_hi, y_lo = (sb(f"y_{s}", [P, ND, T], F32R) for s in ("hi", "lo"))
        scr = nc.dram_tensor("mb_scr", (2, 2 * DS, T), F32, kind="Internal").ap()
        da_ps = ctx.enter_context(nc.psum_tensor("mb_da_ps", [P, 2, 2, T], F32))
        y_ps = ctx.enter_context(nc.psum_tensor("mb_y_ps", [P, T], F32))
        g_ps = ctx.enter_context(nc.psum_tensor("mb_g_ps", [P, T], F32))
        f_ps = ctx.enter_context(nc.psum_tensor("mb_f_ps", [P, 2, T], F32))

        names = """const_in prep p_bias a_exp x_stored passed_pool ln_done ln_steps var1 rs1 xn1 var2 rs2 xn2 res_sum scr_written x_loaded
                   f_ready hT_hi_ready z_ready u_ready u_hi_ready u_lo_ready xd_ready
                   act_steps ex_ready dt_steps dt_ready dtu_ready da_ready dbu_ready scan_done hc_ready y_ready
                   y_used yg_ready y_hi_ready y_lo_ready ux_done"""
        S = {q: sem("mb_" + q) for q in names.split()}
        S["passed"] = sem("passed")
        f_used = [sem(f"mb_f_used{r}") for r in range(2)]
        bc_loaded = [sem(f"mb_bc_loaded{r}") for r in range(NP)]
        PREP = 4 * ND + 1 + 2 + 6 + 1

        def present(n, kind, i):
            if n == -1:
                return kind in NEXT
            if n == NB:
                return kind in LAST or (kind, i) == ("final", 3)
            if n == 0 and (kind in LAST or (kind, i) == ("final", 3)):
                return False
            return not (n == NB - 1 and kind in NEXT)

        def fill(n, kind, i):
            at = FILLS.index((kind, i))
            bank = at % 2

            def before(m, upto=None):
                here = [j for j, f in enumerate(FILLS[:upto]) if present(m, *f)]
                return sum(j % 2 == bank for j in here), len(here)
            if isinstance(n, int):
                parts = [before(m) for m in range(-1, n)] + [before(n, at)]
                return bank, sum(p[0] for p in parts), sum(p[1] for p in parts) + 1
            parts = [before(-1), before(0), before(1, at)]
            same, every = before(1)
            return bank, n * same + sum(p[0] for p in parts) - same, n * every + sum(p[1] for p in parts) + 1 - every

        def tasks(run, n, b, at):
            for kind, i in SCHEDULE.get(at, []):
                if present(n if isinstance(n, int) else 1, kind, i):
                    back = kind in LAST or (kind, i) == ("final", 3)
                    m, mb = (n + 1, 1 - b) if kind in NEXT else (n - 1, 1 - b) if back else (n, b)
                    run(kind, i, n, m, mb)

        def slots(eng, unit, run, lag=0, end=None):
            every = range(ND * NP)

            def slot(n, b, _):
                first = isinstance(n, int) and n < 0
                for at in every:
                    if not first:
                        unit(n, b, at // NP, at % NP)
                    if at >= lag or first:
                        tasks(run, n, b, at if first else at - lag)
                if first:
                    unit(n, b, ND, 0)
                else:
                    for at in every[ND * NP - lag:]:
                        tasks(run, n, b, at)

            batch_slots(eng, slot)
            if end:
                end()
            for at in every:
                tasks(run, NB, 0, at)

        def count(n, d, p):
            return ND * NP * n + NP * d + p

        def q_ring(p):
            return p % 2

        def used_up(eng, n, kind, i):
            bank, used, _ = fill(n, kind, i)
            eng.wait_ge(f_used[bank], used + 1)

        with nc.Block() as block:

            @block.sync
            def _(sp):
                def load(n):
                    wait(sp, S["res_sum"], n)
                    sp.dma_start(xin[:, :, :], x_in[bass.ds(n * T, T), :].rearrange("(k p) c -> p k c", p=P)).then_inc(S["x_loaded"], 16)

                load(0)
                for dst, src in ((ident[:, :], A["ident"]), (cols[:, :, 0:7], A["mb_cols"]), (lnc[:, :, :], A["mb_ln"]), (a_neg[:, :, :], A["mb_alog"]),
                                 (wdt[:, :], A["mb_wdt"]), (raw_wi, A["mb_wi"].rearrange("(k c) e -> c k e", c=P)),
                                 (raw_wo, A["mb_wo"].rearrange("(k c) e -> c k e", c=P)),
                                 (raw_wx, A["mb_wx"].rearrange("(k c) e -> c k e", c=P))):
                    sp.dma_start(dst, src).then_inc(S["const_in"], 16)

                def run(kind, i, n, m, b):
                    if (kind, i) == ("out", 1):
                        used_up(sp, n, "out", 1)
                        sp.dma_start(x_out[bass.ds(m * T, T), :].rearrange("(k p) c -> p k c", p=P), res[:, b, :, :]).then_inc(S["x_stored"], 16)
                    elif kind == "load" and not (isinstance(n, int) and n < 0):
                        load(m)
                    elif kind == "bc":
                        if i == 0:
                            sp.wait_ge(S["xd_ready"], m + 1)
                            sp.dma_start(scr[b], xd[DTR:, :]).then_inc(S["scr_written"], 16)
                            sp.wait_ge(S["scr_written"], 16 * (m + 1))
                        wait(sp, S["dbu_ready"], count(m, -1, i) + 1)
                        over = lambda row: scr[b, row:row + 2, :].unsqueeze(0).broadcast_to([P, 2, T])
                        sp.dma_start(bbc[:, 2 * i:2 * i + 2, :], over(2 * i)).then_inc(bc_loaded[i], 16)
                        wait(sp, S["hc_ready"], count(m, -1, i) + 1)
                        sp.dma_start(cbc[:, 2 * i:2 * i + 2, :], over(DS + 2 * i)).then_inc(bc_loaded[i], 16)

                slots(sp, lambda *a: None, run)
                sp.wait_ge(S["x_stored"], 16 * NB)

            @block.gpsimd
            def _(pool):
                for q, (dst, value) in enumerate(((fix[:, 0:1], 1e-5), (fix[:, 1:2], 1e-6), (fix[:, 2:3], 1.0), (xi[:, :, 0:3], 0.0))):
                    pool.memset(dst, value).then_inc(S["passed_pool"], 1)

                def unit(n, b, d, p):
                    if d == ND:
                        return
                    q = count(n, d, p)
                    if p == 0:
                        pool.wait_ge(S["dtu_ready"], ND * n + d + 1)
                    if d == 0:
                        pool.wait_ge(bc_loaded[p], 32 * (n + 1))
                    wait(pool, S["scan_done"], q - 1)
                    dtu_2 = dtu[:, d % 2, :].unsqueeze(1).broadcast_to([P, 2, T])
                    pool.tensor_tensor(dbu[:, q_ring(p), :, :], dtu_2, bbc[:, 2 * p:2 * p + 2, :], ALU.mult).then_inc(S["dbu_ready"], 1)

                def run(kind, i, n, m, b):
                    if kind in ("dt", "dt0"):
                        q = ND * m + i
                        pool.wait_ge(S["dt_ready"], q + 1)
                        pool.tensor_tensor(dtu[:, i % 2, :], dt[:, i % 2, :], u[:, b, i, :], ALU.mult).then_inc(S["dtu_ready"], 1)
                    elif kind == "final":
                        pool.wait_ge(S["y_hi_ready"], ND * m + i + 1)
                        pool.tensor_tensor(y_lo[:, i, :], z[:, i, :], y_hi[:, i, :], ALU.subtract).then_inc(S["y_lo_ready"], 1)
                    elif kind == "sum":
                        pool.wait_ge(S["xn1"], m + 1)
                        if not isinstance(n, int) or n > 0:
                            pool.wait_ge(S["x_stored"], 16 * (m - 1))
                        pool.tensor_tensor(res[:, b, :, :], xin[:, :, :], xn[:, :, :], ALU.add).then_inc(S["res_sum"], 1)

                slots(pool, unit, run, lag=3)

            @block.scalar
            def _(act):
                act.preload_act_table_set("natural_log_exp_and_others")
                act.wait_ge(S["const_in"], 16 * 8)
                act.activation(a_neg[:, :, :], a_neg[:, :, :], ACT.Exp).then_inc(S["a_exp"], 1)
                act.wait_ge(S["prep"], PREP)
                act.wait_ge(S["passed_pool"], 4)

                def exps(n, d, p):
                    q = count(n, d, p)
                    if p == 0:
                        act.wait_ge(S["dt_ready"], ND * n + d + 1)
                    wait(act, S["hc_ready"], q - 1)
                    for j in range(2):
                        last = act.activation(da_ps[:, q_ring(p), j, :], dt[:, d % 2, :], ACT.Exp, scale=a_neg[:, d, 2 * p + j:2 * p + j + 1])
                    last.then_inc(S["da_ready"], 1)

                def unit(n, b, d, p):
                    if d == ND:
                        exps(0, 0, 0)
                    elif (d, p) != (ND - 1, NP - 1):
                        exps(n, d + (p + 1) // NP, (p + 1) % NP)
                    elif not (isinstance(n, int) and n == NB - 1):
                        exps(n + 1, 0, 0)

                def run(kind, i, n, m, b):
                    if kind in ("z", "tr", "xi", "conv", "dt", "dt0"):
                        bank, used, ready = fill(n, kind, i)
                    if kind == "rsqrt":
                        var, rsq, xnr = (S["var1"], S["rs1"], S["xn1"]) if i == 0 else (S["var2"], S["rs2"], S["xn2"])
                        act.wait_ge(var, m + 1)
                        wait(act, xnr, m)
                        act.activation(rs[:, i, 0, :], mv[:, i, :, 1], ACT.Ln, bias=fix[:, i:i + 1]).then_inc(S["ln_done"], 1)
                        act.wait_ge(S["ln_done"], 2 * m + i + 1)
                        act.activation(rs[:, i, 0, :], rs[:, i, 0, :], ACT.Exp, scale=-0.5).then_inc(rsq, 1)
                    elif kind == "z":
                        act.wait_ge(S["f_ready"], ready)
                        wait(act, S["y_lo_ready"], ND * (m - 1) + i + 1)
                        act.activation(z[:, i, :], f_ps[:, bank, :], ACT.Identity, bias=cols[:, i, 8:9]).then_inc(f_used[bank], 1)
                    elif kind == "tr":
                        act.wait_ge(S["f_ready"], ready)
                        act.activation(hT_hi[:, i, :], f_ps[:, bank, :], ACT.Copy).then_inc(S["hT_hi_ready"], 1)
                    elif kind == "xi":
                        act.wait_ge(S["f_ready"], ready)
                        act.activation(xi[:, i % 2, 3:], f_ps[:, bank, :], ACT.Identity, bias=cols[:, i, 7:8]).then_inc(f_used[bank], 1)
                    elif kind == "conv":
                        act.wait_ge(S["f_ready"], ready)
                        act.activation(u[:, b, i, :], f_ps[:, bank, :], ACT.Identity, bias=cols[:, i, 4:5]).then_inc(f_used[bank], 1)
                    elif kind == "silu_z":
                        used_up(act, n, "z", 2)
                        used_up(act, n, "z", 3)
                        act.activation(z[:, :, :], z[:, :, :], ACT.Silu).then_inc(S["z_ready"], 1)
                        act.preload_act_table_set("natural_log_exp_and_others")
                    elif kind == "silu_u":
                        used_up(act, n, "conv", 2)
                        used_up(act, n, "conv", 3)
                        act.activation(u[:, b, :, :], u[:, b, :, :], ACT.Silu).then_inc(S["u_ready"], 1)
                        act.preload_act_table_set("natural_log_exp_and_others")
                        act.wait_ge(S["u_ready"], m + 1)
                    elif kind == "split":
                        wait(act, S["ux_done"], ND * m + i - 1)
                        act.activation(u_hi[:, i % 2, :], u[:, b, i, :], ACT.Copy).then_inc(S["u_hi_ready"], 1)
                    elif kind == "xd":
                        act.wait_ge(S["ux_done"], ND * m + ND)
                        wait(act, S["scr_written"], 16 * m)
                        act.activation(xd[:, :], g_ps[0:48, :], ACT.Copy).then_inc(S["xd_ready"], 1)
                    elif kind in ("dt", "dt0"):
                        q = ND * m + i
                        act.wait_ge(S["f_ready"], ready)
                        wait(act, S["dt_ready"], q)
                        act.activation(ex[:, :], f_ps[:, bank, :], ACT.Abs, bias=cols[:, i, 5:6]).then_inc(S["act_steps"], 1)
                        wait(act, S["da_ready"], NP * (q - 1))
                        wait(act, S["dbu_ready"], NP * (q - 1))
                        act.activation(dt[:, i % 2, :], f_ps[:, bank, :], ACT.Relu, bias=cols[:, i, 5:6]).then_inc(f_used[bank], 1)
                        act.wait_ge(S["act_steps"], 2 * q + 1)
                        act.activation(ex[:, :], ex[:, :], ACT.Exp, scale=-1.0).then_inc(S["act_steps"], 1)
                        act.wait_ge(S["act_steps"], 2 * q + 2)
                        act.activation(dtu[:, i % 2, :], ex[:, :], ACT.Identity, bias=fix[:, 2:3])
                        act.activation(lg[:, :], ex[:, :], ACT.Ln, bias=fix[:, 2:3]).then_inc(S["ex_ready"], 1)
                    elif kind == "final":
                        act.wait_ge(S["yg_ready"], ND * m + i + 1)
                        if i == 0 and present(n if isinstance(n, int) else 1, "out", 1):
                            act.wait_ge(S["f_ready"], fill(n, "out", 1)[2])
                        act.activation(y_hi[:, i, :], z[:, i, :], ACT.Copy).then_inc(S["y_hi_ready"], 1)

                slots(act, unit, run, lag=1)

            @block.vector
            def _(dve):
                done = [0]

                def mark(ins):
                    done[0] += 1
                    ins.then_inc(S["prep"], 1)

                def settle():
                    dve.wait_ge(S["prep"], done[0])

                dve.wait_ge(S["const_in"], 16 * 8)
                for d in range(ND):
                    for k in range(4):
                        mark(dve.tensor_scalar(diag[:, d, k, :], ident[:, :], cols[:, d, k:k + 1], None, ALU.mult))
                dve.wait_ge(S["p_bias"], 1)
                mark(dve.tensor_copy(cols[:, :, 7:9], g_ps[:, 0:8].rearrange("p (a d) -> p d a", a=2)))
                for kt in range(2):
                    mark(dve.tensor_scalar(raw_wi[:, kt, :], raw_wi[:, kt, :], lnc[:, kt, 0:1], None, ALU.mult))
                settle()
                for raw, hi, lo in ((raw_wi, wi_hi, wi_lo), (raw_wo, wo_hi, wo_lo), (raw_wx, wx_hi, wx_lo)):
                    mark(dve.tensor_copy(hi[:, :, :], raw))
                    settle()
                    mark(dve.tensor_tensor(lo[:, :, :], raw, hi[:, :, :], ALU.subtract))
                dve.wait_ge(S["a_exp"], 1)
                mark(dve.tensor_scalar(a_neg[:, :, :], a_neg[:, :, :], -1.0, None, ALU.mult))
                settle()
                assert done[0] == PREP, done[0]
                ln_steps = Steps(dve, S["ln_steps"], 2 * 12)

                def unit(n, b, d, p):
                    if d == ND:
                        return
                    q = count(n, d, p)
                    r = q_ring(p)
                    dve.wait_ge(S["da_ready"], q + 1)
                    dve.wait_ge(S["dbu_ready"], q + 1)
                    for j in range(2):
                        last = dve.tensor_tensor_scan(da_ps[:, r, j, :], da_ps[:, r, j, :], dbu[:, r, j, :], 0.0, ALU.mult, ALU.add)
                    last.then_inc(S["scan_done"], 1)
                    if d == 0:
                        dve.wait_ge(bc_loaded[p], 32 * (n + 1))
                    wait(dve, S["y_ready"], q - 1)
                    dve.wait_ge(S["scan_done"], q + 1)
                    dve.tensor_tensor(hc[:, r, :, :], da_ps[:, r, :, :], cbc[:, 2 * p:2 * p + 2, :], ALU.mult).then_inc(S["hc_ready"], 1)
                    if p == 0:
                        if d:
                            final(n, b, d - 1)
                        elif not (isinstance(n, int) and n == 0):
                            final(n - 1, 1 - b, ND - 1)

                def final(n, b, d):
                    q = ND * n + d
                    dve.wait_ge(S["y_ready"], NP * (q + 1))
                    dve.wait_ge(S["z_ready"], n + 1)
                    dve.scalar_tensor_tensor(u[:, b, d, :], u[:, b, d, :], cols[:, d, 6:7], y_ps[:, :], ALU.mult, ALU.add).then_inc(S["y_used"], 1)
                    dve.wait_ge(S["y_used"], q + 1)
                    dve.tensor_tensor(z[:, d, :], u[:, b, d, :], z[:, d, :], ALU.mult).then_inc(S["yg_ready"], 1)

                def run(kind, i, n, m, b):
                    if kind in ("out", "tr"):
                        bank, used, ready = fill(n, kind, i)
                    if kind == "final" and isinstance(n, int) and n == NB:
                        final(m, b, i)
                    if kind == "out":
                        dve.wait_ge(S["f_ready"], ready)
                        r_2 = res[:, b, 2 * i:2 * i + 2, :]
                        dve.wait_ge(S["res_sum"], m + 1)
                        dve.tensor_tensor(r_2, f_ps[:, bank, :].rearrange("p (a c) -> p a c", a=2), r_2, ALU.add).then_inc(f_used[bank], 1)
                    elif kind == "ln":
                        if i == 0:
                            ln_steps.begin(m)
                            dve.wait_ge(S["x_loaded"], 16 * (m + 1))
                            wait(dve, S["var1"], m)
                            wait(dve, S["xn1"], m)
                            dve_normalise(dve, ln_steps, S["passed"], xin, xn, stats[:, 0], mv[:, 0], rs[:, 0], 1e-5, S["var1"], S["rs1"], S["xn1"], m, 0)
                        if i == 1:
                            if not (isinstance(n, int) and n < 0):
                                dve.wait_ge(S["f_ready"], fill(n - 1, "tr", 1)[2])
                            dve_normalise(dve, ln_steps, S["passed"], xin, xn, stats[:, 0], mv[:, 0], rs[:, 0], 1e-5, S["var1"], S["rs1"], S["xn1"], m, 1)
                            wait(dve, S["var2"], m)
                            wait(dve, S["xn2"], m)
                            dve.wait_ge(S["xn1"], m + 1)
                            dve_normalise(dve, ln_steps, S["passed"], xn, xn, stats[:, 1], mv[:, 1], rs[:, 1], 1e-6, S["var2"], S["rs2"], S["xn2"], m, 0)
                        if i == 2:
                            dve.wait_ge(S["res_sum"], m + 1)
                            dve_normalise(dve, ln_steps, S["passed"], xn, xn, stats[:, 1], mv[:, 1], rs[:, 1], 1e-6, S["var2"], S["rs2"], S["xn2"], m, 1)
                            assert ln_steps.count == 24, ln_steps.count
                    elif kind == "tr":
                        dve.wait_ge(S["hT_hi_ready"], 2 * m + i + 1)
                        dve.tensor_tensor(hT_lo[:, i, :], f_ps[:, bank, :], hT_hi[:, i, :], ALU.subtract).then_inc(f_used[bank], 1)
                    elif kind == "split":
                        dve.wait_ge(S["u_hi_ready"], ND * m + i + 1)
                        dve.tensor_tensor(u_lo[:, i % 2, :], u[:, b, i, :], u_hi[:, i % 2, :], ALU.subtract).then_inc(S["u_lo_ready"], 1)
                    elif kind in ("dt", "dt0"):
                        q = ND * m + i
                        dve.wait_ge(S["ex_ready"], q + 1)
                        w1 = dtu[:, i % 2, :]
                        dve.scalar_tensor_tensor(w1, w1, -1.0, ex[:, :], ALU.add, ALU.subtract).then_inc(S["dt_steps"], 1)
                        dve.wait_ge(S["dt_steps"], 2 * q + 1)
                        dve.tensor_tensor(lg[:, :], lg[:, :], w1, ALU.subtract).then_inc(S["dt_steps"], 1)
                        dve.wait_ge(S["dt_steps"], 2 * q + 2)
                        dve.tensor_tensor(dt[:, i % 2, :], dt[:, i % 2, :], lg[:, :], ALU.add).then_inc(S["dt_ready"], 1)

                slots(dve, unit, run, lag=2)

            @block.tensor
            def _(pe):
                pe.wait_ge(S["const_in"], 16 * 8)
                for j in range(8):
                    for kt in range(2):
                        last = pe.matmul(g_ps[:, j:j + 1], raw_wi[:, kt, j * P:(j + 1) * P], lnc[:, kt, 1:2], start=(kt == 0), stop=(kt == 1))
                last.then_inc(S["p_bias"], 1)
                pe.wait_ge(S["prep"], PREP)

                def unit(n, b, d, p):
                    if d == ND:
                        return
                    q = count(n, d, p)
                    if p == 0:
                        wait(pe, S["y_used"], ND * n + d)
                    pe.wait_ge(S["hc_ready"], q + 1)
                    for j in range(2):
                        last = pe.matmul(y_ps[:, :], ident[:, :], hc[:, q_ring(p), j, :], start=(p == 0 and j == 0), stop=(p == NP - 1 and j == 1))
                    last.then_inc(S["y_ready"], 1)

                def run(kind, i, n, m, b):
                    if kind == "ux":
                        q = ND * m + i
                        pe.wait_ge(S["u_lo_ready"], q + 1)
                        if i == 0:
                            wait(pe, S["xd_ready"], m)
                        for k, (w, ux) in enumerate(((wx_hi, u_hi), (wx_lo, u_hi), (wx_hi, u_lo))):
                            last = pe.matmul(g_ps[0:48, :], w[:, i, :], ux[:, i % 2, :], start=(i == 0 and k == 0), stop=(i == ND - 1 and k == 2))
                        last.then_inc(S["ux_done"], 1)
                        return
                    if kind not in ("out", "z", "dt", "dt0", "tr", "xi", "conv"):
                        return
                    bank, used, ready = fill(n, kind, i)
                    out = f_ps[:, bank, :]
                    wait(pe, f_used[bank], used)
                    if kind == "out":
                        pe.wait_ge(S["y_lo_ready"], ND * m + ND)
                        for a in range(2):
                            tok = slice((2 * i + a) * P, (2 * i + a + 1) * P)
                            parts = [(yy, w, d) for d in range(ND) for yy, w in ((y_hi, wo_hi), (y_lo, wo_hi), (y_hi, wo_lo))]
                            for c, (yy, w, d) in enumerate(parts):
                                last = pe.matmul(out[:, a * D:(a + 1) * D], yy[:, d, tok], w[:, d, :], start=(c == 0), stop=(c == 3 * ND - 1))
                    elif kind in ("xi", "z"):
                        if (kind, i) == ("xi", 0):
                            used_up(pe, n, "tr", 0)
                            used_up(pe, n, "tr", 1)
                        e = slice(((kind == "z") * ND + i) * P, ((kind == "z") * ND + i + 1) * P)
                        parts = [(w, h, kt) for kt in range(2) for w, h in ((wi_hi, hT_hi), (wi_lo, hT_hi), (wi_hi, hT_lo))]
                        for c, (w, h, kt) in enumerate(parts):
                            last = pe.matmul(out, w[:, kt, e], h[:, kt, :], start=(c == 0), stop=(c == 5))
                    elif kind == "tr":
                        pe.wait_ge(S["xn2"], m + 1)
                        for a in range(4):
                            last = pe.transpose(out[:, a * P:(a + 1) * P], xn[:, a, i * P:(i + 1) * P], ident[:, :])
                    elif kind == "conv":
                        used_up(pe, n, "xi", i)
                        for c in range(4):
                            last = pe.matmul(out, diag[:, i, c, :], xi[:, i % 2, c:c + T], start=(c == 0), stop=(c == 3))
                    elif kind in ("dt", "dt0"):
                        pe.wait_ge(S["xd_ready"], m + 1)
                        last = pe.matmul(out, wdt[:, i * P:(i + 1) * P], xd[0:DTR, :], start=True, stop=True)
                    last.then_inc(S["f_ready"], 1)

                def behind(n, b, d, p):
                    if d == ND:
                        return
                    if (d, p) != (0, 0):
                        unit(n, b, (d * NP + p - 1) // NP, (p - 1) % NP)
                    elif not (isinstance(n, int) and n == 0):
                        unit(n - 1, 1 - b, ND - 1, NP - 1)

                slots(pe, behind, run, end=lambda: unit(NB - 1, 1, ND - 1, NP - 1))


def four_phases(nc, A, x4):
    x1, x2, x3 = (nc.dram_tensor(f"x{i}", (NB * T, D), F32, kind="Internal").ap() for i in (1, 2, 3))
    with ExitStack() as sems:
        passed = sems.enter_context(nc.semaphore("passed"))
        sem = lambda name: passed if name == "passed" else sems.enter_context(nc.semaphore(name))
        attention_phase(nc, sem, A, x1)
        moe_swiglu_phase(nc, sem, A, x1, x2)
        mamba_phase(nc, sem, A, x2, x3)
        moe_linear_phase(nc, sem, A, x3, x4)


def host_layout(a):
    c = {k: np.ascontiguousarray(np.asarray(v)) for k, v in a.items()}
    rep = lambda row: np.ascontiguousarray(np.broadcast_to(row, (P, row.size)))
    swap = np.arange(D) ^ 1
    col2 = lambda v: v.reshape(2, P).T
    cos, sin = (c[f"L0_attn_{n}"][T] for n in ("cos", "sin"))
    sign = np.where(np.arange(D) % 2 == 0, -1.0, 1.0).astype(np.float32)
    out = {"x": c["L0_attn_x"].reshape(NB * T, D), "ident": np.eye(P, dtype=np.float32)}
    for n in "qk":
        w = c[f"L0_attn_w{n}"].T
        out[f"w{n}T"], out[f"w{n}Ts"] = np.ascontiguousarray(w), np.ascontiguousarray(w[:, swap])
    out["cosb"], out["sinb"], out["signb"] = rep(np.tile(cos, NJ)), rep(np.tile(sin, NJ)), rep(sign)
    bq, bk, bv = (c[f"L0_attn_b{n}"] for n in "qkv")
    out["at_cols"] = np.ascontiguousarray(np.concatenate(
        [col2(bq), col2(bk), col2(bq[swap]), col2(bk[swap])] + [np.tile(v, P // v.size)[:, None] for v in (cos, sin, sign[:P])], axis=1))
    out["wvT"] = np.ascontiguousarray(c["L0_attn_wv"].T)
    out["bvt"] = np.ascontiguousarray(np.repeat(bv.reshape(4, 4, DK).transpose(1, 0, 2).reshape(4, 4 * DK), 32, axis=0))
    wo = np.zeros((4, 32, 4, D), np.float32)
    wo[:, :DK] = c["L0_attn_wo"].T.reshape(4, 4, DK, D).transpose(1, 2, 0, 3)
    out["wo_pad"] = wo.reshape(P, 4, D)
    out["bo_rep"] = rep(c["L0_attn_bo"])
    out["order"] = np.ascontiguousarray(np.broadcast_to(np.arange(8, 0, -1, dtype=np.float32), (P, 4, 8)))
    out["m0_rw"] = np.ascontiguousarray(c["L0_ffn_router_weight"].reshape(2, P, 8).transpose(1, 0, 2))
    out["m1_gw"] = np.ascontiguousarray(c["L1_ffn_gate_W"].reshape(2, P, 8).transpose(1, 0, 2))
    out["m1_gb"], out["m1_eb"] = rep(c["L1_ffn_gate_b"]), c["L1_ffn_expert_b"]
    out["m1_w"] = np.ascontiguousarray(c["L1_ffn_expert_W"].reshape(4, 2, D, D).transpose(0, 2, 1, 3).reshape(4, D, 2 * D))
    m = {k[8:]: v for k, v in c.items() if k.startswith("L1_attn_")}
    inner = [*m["conv_w"][:, 0, :].T, m["conv_b"], m["b_dt"], m["Dp"]]
    out["mb_cols"] = np.ascontiguousarray(np.stack([v.reshape(4, P) for v in inner], 2).transpose(1, 0, 2))
    out["mb_ln"] = np.ascontiguousarray(np.stack([v.reshape(2, P) for v in (m["ln_g"], m["ln_b"])], 2).transpose(1, 0, 2))
    out["mb_alog"] = np.ascontiguousarray(m["A_log"].reshape(4, P, 16).transpose(1, 0, 2))
    out["mb_wdt"], out["mb_wi"], out["mb_wo"] = (np.ascontiguousarray(m[k].T) for k in ("W_dt", "W_in", "W_out"))
    out["mb_wx"] = np.ascontiguousarray(m["W_x"].T)
    out["m0_w1"], out["m0_w2"] = c["L0_ffn_w1"], c["L0_ffn_w2"]
    return out


def kernel(**inputs):
    import concourse.bacc as _bacc
    from concourse.bass_utils import run_bass_kernel_spmd as _run

    arrays = host_layout(inputs)
    nc = _bacc.Bacc("TRN2", target_bir_lowering=False, num_devices=1)
    args = {name: nc.dram_tensor("in_" + name, a.shape, F32, kind="ExternalInput").ap() for name, a in arrays.items()}
    x4 = nc.dram_tensor("x4", (NB * T, D), F32, kind="ExternalOutput").ap()
    four_phases(nc, args, x4)
    r = _run(nc, [{"in_" + name: a for name, a in arrays.items()}], core_ids=[0])
    return r.results[0]["x4"].reshape(NB, T, D)
```

```python
from contextlib import ExitStack

import numpy as np

import concourse.bass as bass
from concourse import mybir

ALU = mybir.AluOpType
ACT = mybir.ActivationFunctionType
AX = mybir.AxisListType
F32 = mybir.dt.float32
F32R = mybir.dt.float32r

P = 128
D = 256
NB, T = 8, 512
NT = NB * T // P
NH = 16
DK = D // NH
NJ = D // DK
SCALE = DK ** -0.5


def wait(eng, sem, value):
    if not isinstance(value, int) or value > 0:
        eng.wait_ge(sem, value)

def attention_phase(nc, all_sems, A, x_out):
    with ExitStack() as ctx:
        sb = lambda name, shape, dt=F32: ctx.enter_context(nc.sbuf_tensor("at_" + name, shape, dt))
        sem = lambda name: all_sems("at_" + name)
        x_in = A["x"]

        ident = sb("ident", [P, P])
        cosb, sinb, signb = (sb(n, [P, D]) for n in ("cosb", "sinb", "signb"))
        cols = sb("cols", [P, 11])
        bqk = sb("bqk", [P, 4])
        wraw = sb("wraw", [P, 2, 2, D])
        wrot = sb("wrot", [P, 2, D])
        w_hi = sb("w_hi", [P, 2, 2, D], F32R)
        w_lo = sb("w_lo", [P, 2, 2, D], F32R)
        wv = sb("wv", [P, 2, D])
        bvt = sb("bvt", [P, 64])
        wo = sb("wo", [P, 4, D])
        bo = sb("bo", [P, D])
        eps = sb("eps", [P, 1])

        xin = sb("xin", [P, 4, D])
        stats = sb("stats", [P, 6])
        mv = sb("mv", [P, 2, 2])
        rs = sb("rs", [P, 2, 4])
        xn = sb("xn", [P, D])
        xT = sb("xT", [P, 2, 2, P])
        xT_hi = sb("xT_hi", [P, 2, P], F32R)
        xT_lo = sb("xT_lo", [P, 2, P], F32R)
        qk = sb("qk", [P, 4, P])
        qk_hi = sb("qk_hi", [P, 4, P], F32R)
        qk_lo = sb("qk_lo", [P, 4, P], F32R)
        qst = sb("qst", [P, 4, NJ, P], F32R)
        kst = sb("kst", [P, 4, NJ, P], F32R)
        vau = sb("vau", [P, 4, 4, 4, 32])
        mx = sb("mx", [P, 2, 16])
        nm = sb("nm", [4, 4, 32, 4])
        nm_hi = sb("nm_hi", [4, 4, 32, 4], F32R)
        nm_lo = sb("nm_lo", [4, 4, 32, 4], F32R)
        probs = sb("probs", [P, 2, 16, 512])
        oc = sb("oc", [P, 512])
        sums = sb("sums", [P, 512])
        rsum = sb("rsum", [P, 2, 512])
        oT = sb("oT", [P, 4, 512])
        xo = sb("xo", [P, 4, D])
        scr = nc.dram_tensor("at_scr", (4, 2, 2 * D, P), F32, kind="Internal").ap()

        s_ps = ctx.enter_context(nc.psum_tensor("at_s_ps", [P, 2, 2, 512], F32))
        t_ps = ctx.enter_context(nc.psum_tensor("at_t_ps", [P, 2, 512], F32))
        o_ps = ctx.enter_context(nc.psum_tensor("at_o_ps", [P, 512], F32))
        f_ps = ctx.enter_context(nc.psum_tensor("at_f_ps", [P, 512], F32))

        w_in, wprep, const_set = sem("w_in"), sem("wprep"), sem("const_set")
        x_loaded = [sem(f"x_loaded{r}") for r in range(4)]
        stats_done, aggr_done = sem("stats_done"), sem("aggr_done")
        ln_done, rsq_done = sem("ln_done"), sem("rsq_done")
        pool_chain = sem("pool_chain")
        xn_ready = sem("xn_ready")
        xT_ps_ready, xT_ready, xT_hi_ready, xT_lo_ready = (sem(n) for n in ("xT_ps_ready", "xT_ready", "xT_hi_ready", "xT_lo_ready"))
        qk_ps_ready, qk_ready, qk_hi_ready, qk_lo_ready = (sem(n) for n in ("qk_ps_ready", "qk_ready", "qk_hi_ready", "qk_lo_ready"))
        scr_written = sem("scr_written")
        stack_ready = [sem(f"stack_ready{r}") for r in range(4)]
        v_ps_ready, v_ready = sem("v_ps_ready"), sem("v_ready")
        s_ready, max_done = sem("s_ready"), sem("max_done")
        mT_ready, nm_made, nm_hi_ready, nm_ready, nm_rows = (sem(n) for n in ("mT_ready", "nm_made", "nm_hi_ready", "nm_ready", "nm_rows"))
        t_ready, exp_done, pv_done = sem("t_ready"), sem("exp_done"), sem("pv_done")
        oc_ready, sums_ready, lsum_done, rsum_ready, oT_ready = (sem(n) for n in ("oc_ready", "sums_ready", "lsum_done", "rsum_ready", "oT_ready"))
        xo_loaded, xo_biased, wo_ready, xo_ready, x_stored = (sem(n) for n in ("xo_loaded", "xo_biased", "wo_ready", "xo_ready", "x_stored"))

        def slots(eng, slot):
            for t in range(-6, 4):
                slot(t // 4, t % 4)
            with eng.Fori(1, NB - 2) as i:
                for g in range(4):
                    slot(i, g)
            for t in range(4 * (NB - 2), NT + 3):
                slot(t // 4, t % 4)

        def tile(i, g, lag):
            q = g + lag
            n = i + q // 4 if q // 4 else i
            t = 4 * n + q % 4
            if isinstance(t, int) and not 0 <= t < NT:
                return None
            return t, q % 4, n

        passed = all_sems("passed")

        def pass_on(eng, t):
            if not isinstance(t, int):
                eng.sem_inc(passed, 1)

        with nc.Block() as block:

            @block.sync
            def _(sp):
                first = [(ident, A["ident"]), (cosb, A["cosb"]), (sinb, A["sinb"]), (signb, A["signb"]),
                         (cols, A["at_cols"]), (wv, A["wvT"].rearrange("(k c) e -> c k e", k=2)),
                         (bvt, A["bvt"]), (wo, A["wo_pad"]), (bo, A["bo_rep"])]
                for dst, src in first:
                    sp.dma_start(dst[tuple(slice(None) for _ in dst.shape)], src).then_inc(w_in, 16)
                for m in range(2):
                    if m:
                        sp.wait_ge(wprep, 5)
                    for v, n in enumerate((("wqT", "wqTs"), ("wkT", "wkTs"))[m]):
                        sp.dma_start(wraw[:, v, :, :], A[n].rearrange("(k c) e -> c k e", k=2)).then_inc(w_in, 16)

                sp.sem_inc(x_stored, 16)

                def slot(i, g):
                    if w := tile(i, g, 6):
                        t, r, n = w
                        wait(sp, xn_ready, t - 3)
                        sp.dma_start(xin[:, r, :], x_in[bass.ds(t * P, P), :].rearrange("(h k) c -> k h c", h=4)).then_inc(x_loaded[r], 16)
                    if w := tile(i, g, 3):
                        t, r, n = w
                        sp.wait_ge(const_set, 6)
                        wait(sp, stack_ready[r], 96 * n)
                        pass_on(sp, t)
                        wait(sp, t_ready, 16 * (t - 3))
                        pass_on(sp, t)
                        for kind, src, ready, rows_q, rows_k in ((0, qk_hi, qk_hi_ready, (0, 32), (0, 16)),
                                                                 (1, qk_lo, qk_lo_ready, (16,), (32,))):
                            sp.wait_ge(ready, t + 1)
                            sp.dma_start(scr[r, kind].rearrange("(a p) t -> p a t", p=P), src[:, :, :].bitcast(F32)).then_inc(scr_written, 16)
                            sp.wait_ge(scr_written, 32 * t + 16 * (kind + 1))
                            for st, rows, col in ((qst, rows_q, 0), (kst, rows_k, D)):
                                for row in rows:
                                    sp.dma_start(st[row:row + 16, r, :, :].bitcast(F32),
                                                 scr[r, kind, col:col + D].rearrange("(j d) t -> d j t", d=DK)).then_inc(stack_ready[r], 16)
                    if w := tile(i, g, 1):
                        t, r, n = w
                        sp.wait_ge(const_set, 6)
                        sp.wait_ge(nm_ready, t + 1)
                        for row, src in ((48, nm_hi), (49, nm_lo)):
                            sp.dma_start(qst[row:row + 1, r, :, :].bitcast(F32).rearrange("o (c j) k -> o c (j k)", c=4),
                                         src[:, :, :, :].bitcast(F32).rearrange("c j k h -> c (j k h)")).then_inc(nm_rows, 16)
                    if g == 2 and (w := tile(i, g, -6)):
                        n = w[2]
                        sp.wait_ge(xo_ready, 2 * (n + 1))
                        sp.dma_start(x_out[bass.ds(n * 4 * P, 4 * P), :].rearrange("(k p) c -> p k c", p=P), xo[:, :, :]).then_inc(x_stored, 16)
                    if g == 1 and (w := tile(i, g, -5)):
                        n = w[2]
                        sp.wait_ge(x_stored, 16 * (n + 1))
                        sp.dma_start(xo[:, :, :], x_in[bass.ds(n * 4 * P, 4 * P), :].rearrange("(k p) c -> p k c", p=P)).then_inc(xo_loaded, 16)

                slots(sp, slot)
                sp.wait_ge(x_stored, 16 * (NB + 1))

            @block.gpsimd
            def _(pool):
                fills = [(eps[:, :], 1e-5), (vau[:, :, :, :, :], 1.0), (qst[:, :, :, :].bitcast(F32), 0.0)]
                fills += [(kst[a:b, :, :, :].bitcast(F32), v) for a, b, v in ((0, 32, 0.0), (32, 64, 1.0), (64, P, 0.0))]
                for n, (dst, value) in enumerate(fills):
                    wait(pool, const_set, n)
                    pool.memset(dst, value).then_inc(const_set, 1)

                def chain(ins, count):
                    ins.then_inc(pool_chain, 1)
                    pool.wait_ge(pool_chain, count)

                def slot(i, g):
                    if w := tile(i, g, 3):
                        t = w[0]
                        pool.wait_ge(qk_hi_ready, t + 1)
                        wait(pool, scr_written, 32 * t)
                        pool.tensor_tensor(qk_lo[:, :, :], qk[:, :, :], qk_hi[:, :, :], ALU.subtract).then_inc(qk_lo_ready, 1)
                    if w := tile(i, g, 1):
                        t = w[0]
                        pool.wait_ge(nm_hi_ready, t + 1)
                        wait(pool, nm_rows, 32 * t)
                        pool.tensor_tensor(nm_lo[:, :, :, :], nm[:, :, :, :], nm_hi[:, :, :, :], ALU.subtract).then_inc(nm_ready, 1)
                    if w := tile(i, g, -2):
                        t, r, n = w
                        pool.wait_ge(rsum_ready, t + 1)
                        if r == 0:
                            wait(pool, wo_ready, 2 * n)
                        pool.tensor_tensor(oT[:, r, :].rearrange("p (k j) -> p j k", j=NJ), oc[:, :].rearrange("p (j k) -> p j k", j=NJ),
                                           rsum[:, 1, :].rearrange("p (j k) -> p j k", j=NJ), ALU.mult).then_inc(oT_ready, 1)
                    if w := tile(i, g, 5):
                        t, r, n = w
                        p = r % 2
                        pool.wait_ge(rsq_done, t + 1)
                        y, v, a, b = rs[:, p, 1:2], mv[:, p, 1:2], rs[:, p, 2:3], rs[:, p, 3:4]
                        chain(pool.tensor_tensor(a, y, y, ALU.mult), 5 * t + 1)
                        chain(pool.tensor_tensor(b, v, eps[:, :], ALU.add), 5 * t + 2)
                        chain(pool.tensor_tensor(a, a, b, ALU.mult), 5 * t + 3)
                        pass_on(pool, t)
                        chain(pool.tensor_scalar(a, a, -0.5, 1.5, ALU.mult, ALU.add), 5 * t + 4)
                        chain(pool.tensor_tensor(y, y, a, ALU.mult), 5 * t + 5)
                    if w := tile(i, g, 4):
                        t = w[0]
                        pool.wait_ge(xT_hi_ready, t + 1)
                        wait(pool, qk_ps_ready, t)
                        pool.tensor_tensor(xT_lo[:, :, :], xT[:, w[1] % 2, :, :], xT_hi[:, :, :], ALU.subtract).then_inc(xT_lo_ready, 1)
                    if g == 1 and (w := tile(i, g, -5)):
                        n = w[2]
                        pool.wait_ge(xo_loaded, 16 * (n + 1))
                        bo_all = bo[:, :].unsqueeze(1).broadcast_to([P, 4, D])
                        pool.tensor_tensor(xo[:, :, :], xo[:, :, :], bo_all, ALU.add).then_inc(xo_biased, 1)

                slots(pool, slot)

            @block.scalar
            def _(act):
                act.preload_act_table_set("natural_log_exp_and_others")
                act.wait_ge(const_set, 6)

                def exp(t, r, k):
                    act.wait_ge(t_ready, 16 * t + k + 1)
                    wait(act, pv_done, 4 * (t - 1))
                    act.activation(probs[:, r % 2, k, :], t_ps[:, k % 2, :], ACT.Exp, scale=SCALE).then_inc(exp_done, 1)

                def slot(i, g):
                    for k in range(16):
                        if w := tile(i, g, 0):
                            exp(w[0], w[1], k)
                        if k == 9 and (w := tile(i, g, 1)):
                            t = w[0]
                            act.wait_ge(mT_ready, t + 1)
                            wait(act, nm_ready, t)
                            wait(act, nm_rows, 32 * t)
                            m_ps = f_ps[0:4, :].rearrange("c (h j k) -> c j k h", h=4, j=4)
                            act.activation(nm[:, :, :, :], m_ps, ACT.Copy, scale=-1.0).then_inc(nm_made, 1)
                            act.activation(nm_hi[:, :, :, :], m_ps, ACT.Copy, scale=-1.0).then_inc(nm_hi_ready, 1)
                        if k == 15 and (w := tile(i, g, -1)):
                            t = w[0]
                            act.wait_ge(pv_done, 4 * t + 4)
                            wait(act, oT_ready, t)
                            act.activation(oc[:, :], o_ps[:, :], ACT.Copy).then_inc(oc_ready, 1)
                        if k == 3 and (w := tile(i, g, -2)):
                            t = w[0]
                            act.wait_ge(sums_ready, t + 1)
                            act.activation(rsum[:, 0, :], sums[:, :], ACT.Ln).then_inc(lsum_done, 1)
                            act.wait_ge(lsum_done, t + 1)
                            act.activation(rsum[:, 1, :], rsum[:, 0, :], ACT.Exp, scale=-1.0).then_inc(rsum_ready, 1)
                        if k == 3 and (w := tile(i, g, 3)):
                            t = w[0]
                            act.wait_ge(qk_ready, t + 1)
                            wait(act, scr_written, 32 * t)
                            act.activation(qk_hi[:, :, :], qk[:, :, :], ACT.Copy).then_inc(qk_hi_ready, 1)
                        if k == 12 and (w := tile(i, g, 5)):
                            t, r, n = w
                            p = r % 2
                            act.wait_ge(aggr_done, t + 1)
                            wait(act, xn_ready, t - 1)
                            act.activation(rs[:, p, 0:1], mv[:, p, 1:2], ACT.Ln, bias=eps[:, :]).then_inc(ln_done, 1)
                            act.wait_ge(ln_done, t + 1)
                            act.activation(rs[:, p, 1:2], rs[:, p, 0:1], ACT.Exp, scale=-0.5).then_inc(rsq_done, 1)
                        if k == 13 and (w := tile(i, g, 4)):
                            t = w[0]
                            act.wait_ge(xT_ps_ready, t + 1)
                            wait(act, xT_lo_ready, t)
                            wait(act, v_ps_ready, t - 1)
                            t_in = f_ps[:, 0:2 * P].rearrange("p (k t) -> p k t", k=2)
                            act.activation(xT[:, w[1] % 2, :, :], t_in, ACT.Copy).then_inc(xT_ready, 1)
                            act.activation(xT_hi[:, :, :], t_in, ACT.Copy).then_inc(xT_hi_ready, 1)

                slots(act, slot)

            @block.vector
            def _(dve):
                done = [0]

                def link(ins):
                    done[0] += 1
                    ins.then_inc(wprep, 1)
                    dve.wait_ge(wprep, done[0])

                dve.wait_ge(w_in, 16 * 11)
                link(dve.tensor_tensor(sinb[:, :], sinb[:, :], signb[:, :], ALU.mult))
                for m in range(2):
                    if m:
                        dve.wait_ge(w_in, 16 * 13)
                    for kt in range(2):
                        link(dve.tensor_tensor(wraw[:, 1, kt, :], wraw[:, 1, kt, :], sinb[:, :], ALU.mult)) if kt == 0 else \
                            dve.tensor_tensor(wraw[:, 1, kt, :], wraw[:, 1, kt, :], sinb[:, :], ALU.mult).then_inc(wprep, 1)
                    done[0] += 1
                    cos2 = cosb[:, :].unsqueeze(1).broadcast_to([P, 2, D])
                    dve.wait_ge(wprep, done[0])
                    if m == 0:
                        link(dve.tensor_tensor(wrot[:, :, :], wraw[:, 0, :, :], cos2, ALU.mult))
                        link(dve.tensor_tensor(wrot[:, :, :], wrot[:, :, :], wraw[:, 1, :, :], ALU.add))
                    else:
                        link(dve.tensor_tensor(wrot[:, :, :], wraw[:, 0, :, :], cos2, ALU.mult))
                        link(dve.tensor_tensor(wrot[:, :, :], wrot[:, :, :], wraw[:, 1, :, :], ALU.add))
                    link(dve.tensor_copy(w_hi[:, m, :, :], wrot[:, :, :]))
                    link(dve.tensor_tensor(w_lo[:, m, :, :], wrot[:, :, :], w_hi[:, m, :, :], ALU.subtract))
                link(dve.tensor_tensor(cols[:, 9:10], cols[:, 9:10], cols[:, 10:11], ALU.mult))
                link(dve.tensor_scalar(cols[:, 4:8], cols[:, 4:8], cols[:, 9:10], None, ALU.mult))
                link(dve.tensor_scalar(bqk[:, :], cols[:, 0:4], cols[:, 8:9], None, ALU.mult))
                link(dve.tensor_tensor(bqk[:, :], bqk[:, :], cols[:, 4:8], ALU.add))
                dve.wait_ge(const_set, 6)

                def max_pair(t, m):
                    dve.wait_ge(s_ready, 8 * t + m + 1)
                    if m == 0:
                        wait(dve, mT_ready, t - 1)
                    h, c = m // 2, 2 * (m % 2)
                    out = mx[:, parity[0], 4 * h + c:4 * h + c + 2]
                    dve.tensor_reduce(out, s_ps[:, m % 2, :, :], AX.X, ALU.max).then_inc(max_done, 1)

                parity = [0]

                def project_out(n, part):
                    dve.wait_ge(xo_biased, n + 1)
                    dve.wait_ge(wo_ready, 2 * n + part + 1)
                    dve.tensor_tensor(xo[:, 2 * part:2 * part + 2, :], f_ps[:, :].rearrange("p (a c) -> p a c", a=2),
                                      xo[:, 2 * part:2 * part + 2, :], ALU.add).then_inc(xo_ready, 1)

                def slot(i, g):
                    ahead = tile(i, g, 2)

                    def mp(m):
                        if ahead:
                            parity[0] = ahead[1] % 2
                            max_pair(ahead[0], m)

                    if w := tile(i, g, -2):
                        t = w[0]
                        dve.wait_ge(oc_ready, t + 1)
                        wait(dve, lsum_done, t)
                        pass_on(dve, t)
                        dve.stream_shuffle(sums[:, :], oc[:, :], [16 + q % 16 for q in range(32)]).then_inc(sums_ready, 1)
                    if g == 2 and (w := tile(i, g, -6)):
                        project_out(w[2], 1)
                    mp(0)
                    if w := tile(i, g, 3):
                        t = w[0]
                        dve.wait_ge(qk_ps_ready, t + 1)
                        wait(dve, qk_lo_ready, t)
                        b_all = bqk[:, :].unsqueeze(2).broadcast_to([P, 4, P])
                        dve.tensor_tensor(qk[:, :, :], f_ps[:, :].rearrange("p (a t) -> p a t", a=4), b_all, ALU.add).then_inc(qk_ready, 1)
                    mp(1)
                    if w := tile(i, g, 2):
                        t, r, n = w
                        dve.wait_ge(v_ps_ready, t + 1)
                        wait(dve, pv_done, 4 * (t - 3))
                        v_in = f_ps[:, 0:256].rearrange("p (h c d) -> p h c d", h=4, d=DK)
                        v_b = bvt[:, :].rearrange("p (c d) -> p c d", d=DK).unsqueeze(1).broadcast_to([P, 4, 4, DK])
                        dve.tensor_tensor(vau[:, r, :, :, 0:DK], v_in, v_b, ALU.add).then_inc(v_ready, 1)
                    mp(2)
                    if w := tile(i, g, 5):
                        t, r, n = w
                        dve.wait_ge(x_loaded[r], 16 * (n + 1))
                        wait(dve, xn_ready, t - 1)
                        wait(dve, aggr_done, t)
                        dve.bn_stats(stats[:, :], xin[:, r, :]).then_inc(stats_done, 1)
                    mp(3)
                    if w := tile(i, g, 5):
                        t, r, n = w
                        dve.wait_ge(stats_done, t + 1)
                        pass_on(dve, t)
                        dve.bn_aggr(mv[:, r % 2, :], stats[:, :]).then_inc(aggr_done, 1)
                    mp(4)
                    mp(5)
                    mp(6)
                    mp(7)
                    if w := tile(i, g, 5):
                        t, r, n = w
                        dve.wait_ge(pool_chain, 5 * t + 5)
                        wait(dve, xT_ps_ready, t)
                        dve.tensor_scalar(xn[:, :], xin[:, r, :], mv[:, r % 2, 0:1], rs[:, r % 2, 1:2],
                                          ALU.subtract, ALU.mult).then_inc(xn_ready, 1)
                    if g == 1 and (w := tile(i, g, -5)):
                        project_out(w[2], 0)

                slots(dve, slot)

            @block.tensor
            def _(pe):
                S_AT = (1, 3, 5, 7, 9, 11, 13, 15)
                PV_AT, QK_AT, V_AT, MT_AT, XT_AT = 15, 2, 4, 8, 11
                pe.wait_ge(w_in, 16 * 13)
                pe.wait_ge(wprep, 17)
                pe.wait_ge(const_set, 6)

                def of_head(stack, r, h, rows, chunk=None):
                    seq = stack[0:rows, r, :, :].rearrange("r j (k h) -> r (j k) h", h=4)
                    return seq[:, :, h] if chunk is None else seq[:, chunk * P:(chunk + 1) * P, h]

                def scores_T(t, r, k):
                    c, h = k // 4, k % 4
                    wait(pe, exp_done, 16 * t + k - 1)
                    pe.matmul(t_ps[:, k % 2, :], of_head(kst, r, h, 64, c), of_head(qst, r, h, 64), start=True, stop=True).then_inc(t_ready, 1)

                def scores(t, r, m):
                    wait(pe, max_done, 8 * t + m - 1)
                    h, c = m // 2, 2 * (m % 2)
                    for a in range(2):
                        last = pe.matmul(s_ps[:, m % 2, a, :], of_head(qst, r, h, 48, c + a), of_head(kst, r, h, 48), start=True, stop=True)
                    last.then_inc(s_ready, 1)

                def values(t, r, c):
                    pe.wait_ge(exp_done, 16 * t + 4 * c + 4)
                    if c == 0:
                        wait(pe, oc_ready, t)
                        pe.wait_ge(v_ready, t + 1)
                    for h in range(4):
                        last = pe.matmul(o_ps[32 * h:32 * h + 32, :], vau[:, r, h, c, :], probs[:, r % 2, 4 * c + h, :],
                                         start=(c == 0), stop=(c == 3))
                    last.then_inc(pv_done, 1)

                def slot(i, g):
                    now, ahead, front = tile(i, g, 0), tile(i, g, 2), tile(i, g, 3)
                    batch = tile(i, g, -4 - g) if g in (1, 2) else None
                    for k in range(16):
                        if now:
                            if k == 0:
                                pe.wait_ge(nm_rows, 32 * (now[0] + 1))
                            scores_T(now[0], now[1], k)
                        if ahead and k in S_AT:
                            if k == S_AT[0]:
                                pe.wait_ge(stack_ready[ahead[1]], 96 * (ahead[2] + 1))
                            scores(ahead[0], ahead[1], S_AT.index(k))
                        if (g, k) in ((1, 14), (2, 0)) and batch:
                            project(i, g - 1, batch[2])
                        if k == QK_AT and front:
                            t = front[0]
                            pe.wait_ge(xT_lo_ready, t + 1)
                            if g == 2 and batch:
                                pe.wait_ge(xo_ready, 2 * (batch[2] + 1))
                            for a in range(4):
                                m, et = a // 2, a % 2
                                parts = [(wt, xt, kt) for kt in range(2) for wt, xt in ((w_hi, xT_hi), (w_lo, xT_hi), (w_hi, xT_lo))]
                                for n3, (wt, xt, kt) in enumerate(parts):
                                    last = pe.matmul(f_ps[:, a * P:(a + 1) * P], wt[:, m, kt, et * P:(et + 1) * P], xt[:, kt, :],
                                                     start=(n3 == 0), stop=(n3 == 5))
                            last.then_inc(qk_ps_ready, 1)
                        if k == PV_AT and (w := tile(i, g, -1)):
                            for c in range(4):
                                values(w[0], w[1], c)
                        if k == V_AT and ahead:
                            t = ahead[0]
                            if front:
                                pe.wait_ge(qk_ready, t + 2)
                            else:
                                pe.wait_ge(xT_hi_ready, NT)
                                pe.wait_ge(nm_hi_ready, t - 1)
                                if batch:
                                    wait(pe, xo_ready, 2 * (batch[2] + g - 1))
                            for h in range(4):
                                for kt in range(2):
                                    for jj in range(4):
                                        wv_j = wv[:, kt, :].rearrange("p (c j d) -> p j c d", c=4, j=4)[:, jj, :, :]
                                        last = pe.matmul(f_ps[32 * jj:32 * jj + 32, 64 * h:64 * h + 64],
                                                         xT[:, ahead[1] % 2, kt, :].rearrange("c (k h) -> c k h", h=4)[:, :, h],
                                                         wv_j, start=(kt == 0), stop=(kt == 1), skip_group_check=True)
                            last.then_inc(v_ps_ready, 1)
                        if k == MT_AT and (w := tile(i, g, 1)):
                            t, r, n = w
                            if ahead:
                                pe.wait_ge(v_ready, ahead[0] + 1)
                            else:
                                pe.wait_ge(v_ready, NT)
                                pe.wait_ge(xT_hi_ready, NT)
                                pe.wait_ge(nm_hi_ready, t)
                                if batch:
                                    wait(pe, xo_ready, 2 * (batch[2] + g - 1))
                            pe.wait_ge(max_done, 8 * t + 8)
                            for h in range(4):
                                last = pe.transpose(f_ps[0:4, h * P:(h + 1) * P], mx[:, r % 2, 4 * h:4 * h + 4], ident[:, :])
                            last.then_inc(mT_ready, 1)
                        if k == XT_AT and (w := tile(i, g, 4)):
                            t = w[0]
                            pe.wait_ge(xn_ready, t + 1)
                            wait(pe, qk_ready, t)
                            wait(pe, v_ready, t - 1)
                            wait(pe, nm_hi_ready, t - 2)
                            for kt in range(2):
                                last = pe.transpose(f_ps[:, kt * P:(kt + 1) * P], xn[:, kt * P:(kt + 1) * P], ident[:, :])
                            last.then_inc(xT_ps_ready, 1)

                def project(i, part, n):
                    if part == 0:
                        pe.wait_ge(oT_ready, 4 * n + 4)
                        if w := tile(i, 1, 4):
                            pe.wait_ge(xT_hi_ready, w[0] + 1)
                        else:
                            pe.wait_ge(xT_hi_ready, NT)
                            pe.wait_ge(nm_hi_ready, min(4 * i + 3, NT))
                    else:
                        pe.wait_ge(xo_ready, 2 * n + 1)
                    for a in range(2):
                        tok = slice((2 * part + a) * P, (2 * part + a + 1) * P)
                        for gg in range(4):
                            last = pe.matmul(f_ps[:, a * D:(a + 1) * D], oT[:, gg, tok], wo[:, gg, :], start=(gg == 0), stop=(gg == 3))
                    last.then_inc(wo_ready, 1)

                slots(pe, slot)


class Steps:
    def __init__(self, eng, sem, per_batch):
        self.eng, self.sem, self.per_batch = eng, sem, per_batch

    def begin(self, n):
        self.base, self.count = n * self.per_batch, 0

    def mark(self, ins):
        ins.then_inc(self.sem, 1)
        self.count += 1

    def settle(self):
        self.eng.wait_ge(self.sem, self.base + self.count)

    def __call__(self, ins):
        self.mark(ins)
        self.settle()


def batch_slots(eng, slot):
    slot(-1, 1, (0, 0))
    slot(0, 0, (1, 1))
    with eng.Fori(0, (NB - 2) // 2) as i:
        slot(2 * i + 1, 1, (2 * i + 2, 0))
        slot(2 * i + 2, 0, (2 * i + 3, 1))
    slot(NB - 1, 1, None)


def dve_normalise(dve, steps, passed, x, xn, stats, mv, rs, eps, var_ready, rs_ready, xn_ready, n, part):
    if part == 0:
        for k in range(4):
            steps.mark(dve.bn_stats(stats[:, k, :], x[:, k, :]))
        for k in range(4):
            if k == 0:
                steps.settle()
                dve.sem_inc(passed, 1)
            ins = dve.bn_aggr(mv[:, k, :], stats[:, k, :])
            steps.mark(ins) if k < 3 else ins.then_inc(var_ready, 1)
    else:
        dve.wait_ge(rs_ready, n + 1)
        y, v, a, b = rs[:, 0, :], mv[:, :, 1], rs[:, 1, :], rs[:, 2, :]
        steps(dve.tensor_tensor(a, y, y, ALU.mult))
        steps(dve.tensor_scalar(b, v, eps, None, ALU.add))
        steps(dve.tensor_tensor(a, a, b, ALU.mult))
        steps(dve.tensor_scalar(a, a, -0.5, 1.5, ALU.mult, ALU.add))
        steps(dve.tensor_tensor(rs[:, 3, :], y, a, ALU.mult))
        for k in range(4):
            last = dve.tensor_scalar(xn[:, k, :], x[:, k, :], mv[:, k, 0:1], rs[:, 3, k:k + 1], ALU.subtract, ALU.mult)
        last.then_inc(xn_ready, 1)


def dve_top2(dve, steps, p, order, work, small, both=True):
    bc = lambda s: s.unsqueeze(2).broadcast_to([P, 4, 8])
    m, m1, c = work[:, 0], work[:, 1], work[:, 2]
    steps(dve.tensor_reduce(small[:, 0, :], p, AX.X, ALU.add))
    steps(dve.reciprocal(small[:, 1, :], small[:, 0, :]))
    steps(dve.tensor_tensor(p, p, bc(small[:, 1, :]), ALU.mult))
    left = p
    for r, mask in enumerate((m, m1)):
        steps(dve.tensor_reduce(small[:, 2, :], left, AX.X, ALU.max))
        steps(dve.tensor_tensor(c, left, bc(small[:, 2, :]), ALU.is_equal))
        steps(dve.tensor_tensor(c, c, order, ALU.mult))
        steps(dve.tensor_reduce(small[:, 3, :], c, AX.X, ALU.max))
        steps(dve.tensor_tensor(mask, c, bc(small[:, 3, :]), ALU.is_equal))
        if r == 0:
            left = work[:, 3]
            steps(dve.scalar_tensor_tensor(left, mask, -2.0, p, ALU.mult, ALU.add))
    if not both:
        return m, m1
    steps(dve.tensor_tensor(m, m, m1, ALU.add))
    return m


def moe_swiglu_phase(nc, sem, A, x_in, x_out):
    E, F = 8, 352
    FT = [(0, 128), (128, 128), (256, 96)]
    SLOTS = 2 * NT + E
    STRIDE = 6
    N_STEPS = 4 + 3 + 5 + 1 + 14 + 1
    with ExitStack() as ctx:
        sb = lambda name, shape, dt=F32: ctx.enter_context(nc.sbuf_tensor("m0_" + name, shape, dt))
        ident = sb("ident", [P, P])
        w1_hi, w1_lo = (sb(f"w1_{s}", [P, E, 2, 2 * F], F32R) for s in ("hi", "lo"))
        w2_hi, w2_lo = (sb(f"w2_{s}", [P, E, 3, D], F32R) for s in ("hi", "lo"))
        rw = sb("rw", [P, 2, E])
        order = sb("order", [P, 4, E])
        tri = sb("tri", [P, 2, P])
        steps_of = sb("steps_of", [P, NT])
        slot_no = sb("slot_no", [1, SLOTS])
        eps = sb("eps", [P, 1])
        x = sb("x", [P, 2, 4, D])
        xn = sb("xn", [P, 2, 4, D])
        stats, mv, rs = sb("stats", [P, 4, 6]), sb("mv", [P, 4, 2]), sb("rs", [P, 4, 4])
        xT = sb("xT", [P, 2, T])
        work, small = sb("work", [P, 4, 4, E]), sb("small", [P, 4, 4])
        route = sb("route", [P, 3, 4, E])
        both = sb("both", [P, 4, E])
        routes = sb("routes", [P, 5, NT, E])
        upto = sb("upto", [P, E, NT])
        cmp = sb("cmp", [P, E, NT])
        ends, starts, ntiles = (sb(q, [P, E]) for q in ("ends", "starts", "ntiles"))
        row = sb("row", [P, NT, E])
        scr2 = sb("scr2", [P, NT, E])
        pos_f, pos = sb("pos_f", [P, NT, 2]), sb("pos", [P, NT, 2], mybir.dt.int32)
        prob = sb("prob", [P, NT, 2])
        expert_f, expert = sb("expert_f", [1, SLOTS]), sb("expert", [1, SLOTS], mybir.dt.int32)
        lcmp = sb("lcmp", [1, SLOTS, E])
        idx = sb("idx", [P, 2, 4, 2], mybir.dt.int32)
        pr = sb("pr", [P, 2, 4, 2])
        raw = sb("raw", [P, 2, 3 * D])
        xs = xn
        xsT_hi, xsT_lo = (sb(f"xsT_{q}", [P, 2, 2, P], F32R) for q in ("hi", "lo"))
        g = sb("g", [P, 2, F])
        gT_hi, gT_lo = (sb(f"gT_{q}", [P, 2, 3, P], F32R) for q in ("hi", "lo"))
        o = sb("o", [P, 2, D])
        rows_b = sb("rows_b", [P, 4, D])
        xs_d = nc.dram_tensor("m0_xs_list", (SLOTS * P, D), F32, kind="Internal").ap()
        o_d = nc.dram_tensor("m0_o_list", (SLOTS * P, D), F32, kind="Internal").ap()
        xn_d = nc.dram_tensor("m0_xn_rows", (NB * T, D), F32, kind="Internal").ap()
        y_ps = ctx.enter_context(nc.psum_tensor("m0_y_ps", [P, 2, 2, 512], F32))
        f_ps = ctx.enter_context(nc.psum_tensor("m0_f_ps", [P, 2, T], F32))
        o_ps = ctx.enter_context(nc.psum_tensor("m0_o_ps", [P, 512], F32))
        r_ps = ctx.enter_context(nc.psum_tensor("m0_r_ps", [P, 512], F32))

        names = """const_in w_hi w_ready steps var_ready ln_ready rs_ready xn_ready xn_stored xT_ps xT_ready logits z_ready
                   exp_ready both_ready ranks routed const_set zeroed gsteps expert_set idx_ready
                   xs_ps hi_ready lo_ready y_ready silu_ready g_ready gT_ps gT_hi_ready gT_lo_ready o_ready o_copied half x_done x_stored"""
        S = {q: sem("m0_" + q) for q in names.split()}
        passed = sem("passed")
        w_in, x_loaded, xs_loaded, o_stored, gathered = ([sem(f"m0_{q}{r}") for r in range(2)] for q in
                                                         ("w_in", "x_loaded", "xs_loaded", "o_stored", "gathered"))
        scattered = [sem(f"m0_scattered{r}") for r in range(2)]
        tiles_loaded = [sem(f"m0_tiles_loaded{r}") for r in range(2)]

        def pieces(e, b):
            r3, one = F - 2 * P, bass.ds(e, 1)
            flat = lambda ap: ap.rearrange("p o f -> p (o f)")
            for j in range(3):
                r = (b + j) % 2
                if j < 2:
                    yield r, [(raw[:, r, 0:2 * F], A["m0_w1"][one, j * P:(j + 1) * P, :].rearrange("o c f -> (o c) f"),
                               flat(w1_hi[:, one, j, :]), flat(w1_lo[:, one, j, :]))]
                else:
                    for_two = lambda w: w[:, one, 0:2, :].rearrange("p o f c -> p (o f c)")
                    yield r, [(raw[:, r, 0:2 * D], A["m0_w2a"][one, :, :].rearrange("o c f -> (o c) f"), for_two(w2_hi), for_two(w2_lo)),
                              (raw[0:r3, r, 2 * D:3 * D], A["m0_w2"][one, 2 * P:F, :].rearrange("o c f -> (o c) f"),
                               flat(w2_hi[0:r3, one, 2, :]), flat(w2_lo[0:r3, one, 2, :]))]

        def parity_count(n, b):
            return 16 * ((n - b) // 2 + 1) if isinstance(n, int) else 8 * (n - b) + 16

        def batches(eng, slot):
            slot(0, 0)
            slot(1, 1)
            with eng.Fori(1, NB // 2) as i:
                slot(2 * i, 0)
                slot(2 * i + 1, 1)

        def ahead_batches(eng, slot):
            slot(0, 0)
            slot(1, 1)
            with eng.Fori(1, NB // 2 - 1) as i:
                slot(2 * i, 0)
                slot(2 * i + 1, 1)
            slot(NB - 2, 0)
            slot(NB - 1, 1)

        def is_int(n):
            return isinstance(n, int)

        zero = rows_b[:, :, :].rearrange("p k c -> p (k c)")

        with nc.Block() as block:

            @block.sync
            def _(sp):
                sp.dma_start(x[:, 0, :, :], x_in[0:T, :].rearrange("(k p) c -> p k c", p=P)).then_inc(x_loaded[0], 16)
                for dst, src in ((ident[:, :], A["ident"]), (rw[:, :, :], A["m0_rw"]), (order[:, :, :], A["order"]), (tri[:, :, :], A["tri"]),
                                 (steps_of[:, :], A["steps_of"]), (slot_no[:, :], A["slot_no"])):
                    sp.dma_start(dst, src).then_inc(S["const_in"], 16)
                sp.dma_start(x[:, 1, :, :], x_in[T:2 * T, :].rearrange("(k p) c -> p k c", p=P)).then_inc(x_loaded[1], 16)

                def slot(n, b):
                    for j, (r, parts) in enumerate(pieces(n, b)):
                        wait(sp, S["w_ready"], 3 * n + j - 1)
                        for dst, src, _, _ in parts:
                            sp.dma_start(dst, src).then_inc(w_in[r], 16)
                    sp.wait_ge(S["xn_ready"], n + 1)
                    sp.dma_start(xn_d[bass.ds(n * T, T), :].rearrange("(k p) c -> p k c", p=P), xn[:, b, :, :]).then_inc(S["xn_stored"], 16)
                    if not is_int(n) or n < NB - 2:
                        sp.dma_start(x[:, b, :, :], x_in[bass.ds(n * T + 2 * T, T), :].rearrange("(k p) c -> p k c", p=P)).then_inc(x_loaded[b], 16)
                    zeros(2 * n)
                    zeros(2 * n + 1)

                def zeros(c):
                    sp.dma_start(xs_d[bass.ds(c * 4 * P, 4 * P), :].rearrange("(p k) c -> p (k c)", k=4), zero).then_inc(S["zeroed"], 16)

                sp.wait_ge(S["const_set"], 2)
                ahead_batches(sp, slot)
                for c in range(2 * NB, SLOTS // 4):
                    zeros(c)
                sp.wait_ge(S["xn_stored"], 16 * NB)
                sp.wait_ge(S["zeroed"], 16 * (SLOTS // 4))

            @block.gpsimd
            def _(pool):
                pool.memset(eps[:, :], 1e-5).then_inc(S["const_set"], 1)
                pool.memset(rows_b[:, :, :], 0.0).then_inc(S["const_set"], 1)

                def slot(n, b):
                    for j, (r, parts) in enumerate(pieces(n, b)):
                        pool.wait_ge(S["w_hi"], 3 * n + j + 1)
                        for src, _, hi, lo in parts:
                            last = pool.tensor_tensor(lo, src, hi, ALU.subtract)
                        last.then_inc(S["w_ready"], 1)

                ahead_batches(pool, slot)

            @block.scalar
            def _(act):
                act.preload_act_table_set("natural_log_exp_and_others")
                act.wait_ge(S["const_set"], 1)

                def split(n, b, j):
                    r, parts = list(pieces(n, b))[j]
                    loads = ((1, 1, 3), (2, 4, 4))[b][j]
                    act.wait_ge(w_in[r], 32 * (n - b) + 16 * loads)
                    for src, _, hi, _ in parts:
                        last = act.activation(hi, src, ACT.Copy)
                    last.then_inc(S["w_hi"], 1)

                def slot(n, b):
                    act.wait_ge(S["var_ready"], n + 1)
                    wait(act, S["xn_ready"], n)
                    act.activation(rs[:, 0, :], mv[:, :, 1], ACT.Ln, bias=eps[:, :]).then_inc(S["ln_ready"], 1)
                    act.wait_ge(S["ln_ready"], n + 1)
                    act.activation(rs[:, 0, :], rs[:, 0, :], ACT.Exp, scale=-0.5).then_inc(S["rs_ready"], 1)
                    split(n, b, 0)
                    act.wait_ge(S["xT_ps"], n + 1)
                    act.activation(xT[:, :, :], f_ps[:, :, :], ACT.Copy).then_inc(S["xT_ready"], 1)
                    split(n, b, 1)
                    act.wait_ge(S["z_ready"], n + 1)
                    act.activation(route[:, 0, :, :], route[:, 0, :, :], ACT.Exp).then_inc(S["exp_ready"], 1)
                    split(n, b, 2)

                ahead_batches(act, slot)

            @block.vector
            def _(dve):
                steps = Steps(dve, S["steps"], N_STEPS)
                dve.wait_ge(S["const_in"], 16 * 6)

                def slot(n, b):
                    steps.begin(n)
                    dve.wait_ge(x_loaded[b], parity_count(n, b))
                    wait(dve, S["var_ready"], n)
                    args = (dve, steps, passed, x[:, b], xn[:, b], stats, mv, rs, 1e-5, S["var_ready"], S["rs_ready"], S["xn_ready"], n)
                    dve_normalise(*args, 0)
                    wait(dve, S["xT_ps"], n)
                    if not is_int(n) or n > 1:
                        dve.wait_ge(S["xn_stored"], 16 * (n - 1))
                    dve_normalise(*args, 1)
                    z_in = f_ps[:, 0, 0:4 * E].rearrange("p (k e) -> p k e", k=4)
                    dve.wait_ge(S["logits"], n + 1)
                    wait(dve, S["routed"], 2 * n)
                    steps(dve.tensor_reduce(small[:, 0, :], z_in, AX.X, ALU.max))
                    dve.tensor_tensor(route[:, 0, :, :], z_in, small[:, 0, :].unsqueeze(2).broadcast_to([P, 4, E]), ALU.subtract).then_inc(S["z_ready"], 1)
                    dve.wait_ge(S["exp_ready"], n + 1)
                    first, second = dve_top2(dve, steps, route[:, 0, :, :], order[:, :, :], work, small, both=False)
                    steps.mark(dve.tensor_copy(route[:, 1, :, :], first))
                    wait(dve, S["ranks"], n)
                    dve.tensor_copy(route[:, 2, :, :], second)
                    dve.tensor_tensor(both[:, :, :], first, second, ALU.add).then_inc(S["both_ready"], 1)
                    assert steps.count == N_STEPS, steps.count
                    dve.wait_ge(S["both_ready"], n + 1)
                    dve.sem_inc(passed, 1)
                    dve.tensor_copy(routes[:, 0:3, bass.ds(4 * n, 4), :], route[:, :, :, :]).then_inc(S["routed"], 1)
                    dve.wait_ge(S["ranks"], n + 1)
                    dve.sem_inc(passed, 1)
                    dve.tensor_copy(routes[:, 3:5, bass.ds(4 * n, 4), :], r_ps[:, 0:8 * E].rearrange("p (a k e) -> p a k e", a=2, k=4)).then_inc(S["routed"], 1)

                ahead_batches(dve, slot)

            @block.tensor
            def _(pe):
                pe.wait_ge(S["const_in"], 16 * 6)

                def slot(n, b):
                    pe.wait_ge(S["xn_ready"], n + 1)
                    wait(pe, S["z_ready"], n)
                    for kt in range(2):
                        for k in range(4):
                            last = pe.transpose(f_ps[:, kt, k * P:(k + 1) * P], xn[:, b, k, kt * P:(kt + 1) * P], ident[:, :])
                    last.then_inc(S["xT_ps"], 1)
                    pe.wait_ge(S["xT_ready"], n + 1)
                    for k in range(4):
                        for kt in range(2):
                            last = pe.matmul(f_ps[:, 0, k * E:(k + 1) * E], xT[:, kt, k * P:(k + 1) * P], rw[:, kt, :], start=(kt == 0), stop=(kt == 1))
                    last.then_inc(S["logits"], 1)
                    pe.wait_ge(S["both_ready"], n + 1)
                    wait(pe, S["routed"], 2 * n)
                    for a in range(2):
                        last = pe.matmul(r_ps[:, a * 4 * E:(a + 1) * 4 * E], tri[:, a, :], both[:, :, :].rearrange("p k e -> p (k e)"), start=True, stop=True)
                    last.then_inc(S["ranks"], 1)

                ahead_batches(pe, slot)

        with nc.Block() as block:

            @block.vector
            def _(dve):
                steps = Steps(dve, S["gsteps"], 0)
                steps.begin(0)
                ones = tri[:, 1, 0:NT]
                for e in range(E):
                    steps.mark(dve.tensor_tensor_scan(upto[:, e, :], ones, routes[:, 4, :, e], 0.0, ALU.mult, ALU.add))
                steps.settle()
                total = upto[:, :, NT - 1:NT].broadcast_to([P, E, NT])
                steps(dve.tensor_tensor(cmp[:, :, :], total, steps_of[:, :].unsqueeze(1).broadcast_to([P, E, NT]), ALU.is_gt))
                steps(dve.tensor_reduce(ntiles[:, :], cmp[:, :, :], AX.X, ALU.add))
                steps(dve.tensor_tensor_scan(ends[:, :], tri[:, 1, 0:E], ntiles[:, :], 0.0, ALU.mult, ALU.add))
                steps(dve.tensor_tensor(starts[:, :], ends[:, :], ntiles[:, :], ALU.subtract))
                steps(dve.tensor_scalar(starts[:, :], starts[:, :], float(P), None, ALU.mult))
                steps(dve.tensor_tensor(row[:, :, :], upto[:, :, :].rearrange("p e t -> p t e"), routes[:, 4, :, :], ALU.subtract))
                steps(dve.tensor_tensor(row[:, :, :], row[:, :, :], routes[:, 3, :, :], ALU.add))
                steps(dve.tensor_tensor(row[:, :, :], row[:, :, :], starts[:, :].unsqueeze(1).broadcast_to([P, NT, E]), ALU.add))
                for c in range(2):
                    for src, dst in ((row[:, :, :], pos_f), (routes[:, 0, :, :], prob)):
                        steps(dve.tensor_tensor(scr2[:, :, :], src, routes[:, 1 + c, :, :], ALU.mult))
                        steps(dve.tensor_reduce(dst[:, :, c], scr2[:, :, :], AX.X, ALU.add))
                steps(dve.tensor_copy(pos[:, :, :], pos_f[:, :, :]))
                steps(dve.tensor_tensor(lcmp[:, :, :], slot_no[:, :].unsqueeze(2).broadcast_to([1, SLOTS, E]),
                                        ends[0:1, :].unsqueeze(1).broadcast_to([1, SLOTS, E]), ALU.is_ge))
                steps(dve.tensor_reduce(expert_f[:, :], lcmp[:, :, :], AX.X, ALU.add))
                steps(dve.tensor_scalar(expert_f[:, :], expert_f[:, :], float(E - 1), None, ALU.min))
                dve.tensor_copy(expert[:, :], expert_f[:, :]).then_inc(S["expert_set"], 1)
                dve.wait_ge(S["expert_set"], 1)

        with nc.Block() as block:

            @block.sync
            def _(sp):
                def slot(n, b):
                    if not is_int(n) or n > 1:
                        sp.wait_ge(scattered[b], 8 * parity_count(n, b) - 128)
                    sp.dma_start(xn[:, b, :, :], xn_d[bass.ds(n * T, T), :].rearrange("(k p) c -> p k c", p=P)).then_inc(xs_loaded[b], 16)

                batches(sp, slot)

            @block.vector
            def _(dve):
                def slot(n, b):
                    if not is_int(n) or n > 1:
                        dve.wait_ge(scattered[b], 8 * parity_count(n, b) - 128)
                        dve.sem_inc(passed, 1)
                    dve.tensor_copy(idx[:, b, :, :], pos[:, bass.ds(4 * n, 4), :]).then_inc(S["idx_ready"], 1)

                batches(dve, slot)

            @block.gpsimd
            def _(pool):
                def slot(n, b):
                    pool.wait_ge(S["idx_ready"], n + 1)
                    pool.wait_ge(xs_loaded[b], parity_count(n, b))
                    if not is_int(n):
                        pool.sem_inc(passed, 1)
                    for k in range(4):
                        for c in range(2):
                            pool.indirect_dma_start(xs_d, bass.IndirectOffsetOnAxis(ap=idx[:, b, k, c:c + 1], axis=0), xn[:, b, k, :], None).then_inc(scattered[b], 16)

                batches(pool, slot)
                for r in range(2):
                    pool.wait_ge(scattered[r], 64 * NB)

        with nc.Block() as block:

            def slots(eng, slot):
                for t in range(-2, 4):
                    slot(t, t % 2)
                with eng.Fori(0, (SLOTS - 6) // STRIDE) as i:
                    for k in range(STRIDE):
                        slot(STRIDE * i + 4 + k, k % 2, k)
                for t in range(SLOTS - 2, SLOTS + 2):
                    slot(t, t % 2)

            def tile(t, lag):
                t = t + lag
                return None if is_int(t) and not 0 <= t < SLOTS else t

            def gT_in(a, b):
                part = f_ps[:, 1, a * P:b * P]
                return part.rearrange("p (f t) -> p f t", f=2) if b - a == 2 else part[0:96]

            def uses(t, r):
                return 16 * ((t - r) // 2 + 1) if is_int(t) else 8 * (t - r) + 16

            assert (SLOTS - 6) % STRIDE == 0 and STRIDE % 2 == 0

            @block.sync
            def _(sp):
                def slot(t, r, k=None):
                    if (q := tile(t, 2)) is not None:
                        wait(sp, S["xs_ps"], q - 1)
                        sp.dma_start(xs[:, 0, r, :], xs_d[bass.ds(q * P, P), :]).then_inc(tiles_loaded[r], 16)
                    if (q := tile(t, -2)) is not None:
                        sp.wait_ge(S["o_copied"], q + 1)
                        sp.dma_start(o_d[bass.ds(q * P, P), :], o[:, r, :]).then_inc(o_stored[r], 16)

                slots(sp, slot)
                for r in range(2):
                    sp.wait_ge(o_stored[r], 16 * (SLOTS // 2))

            @block.scalar
            def _(act):
                def slot(t, r, k=None):
                    if (q := tile(t, 1)) is not None:
                        act.wait_ge(S["xs_ps"], q + 1)
                        wait(act, S["y_ready"], q - 1)
                        act.activation(xsT_hi[:, 1 - r, :, :], f_ps[:, 0, 0:2 * P].rearrange("p (k t) -> p k t", k=2), ACT.Copy).then_inc(S["hi_ready"], 1)
                    if (q := tile(t, 0)) is not None:
                        act.wait_ge(S["y_ready"], q + 1)
                        wait(act, S["gT_ps"], q - 1)
                        act.activation(g[:, r, :], y_ps[:, r, 0, 0:F], ACT.Silu).then_inc(S["silu_ready"], 1)
                    if (q := tile(t, -1)) is not None:
                        act.wait_ge(S["gT_ps"], q + 1)
                        wait(act, S["o_ready"], q - 1)
                        act.activation(gT_hi[:, 1 - r, 0:2, :], gT_in(0, 2), ACT.Copy)
                        act.activation(gT_hi[0:96, 1 - r, 2, :], gT_in(2, 3), ACT.Copy).then_inc(S["gT_hi_ready"], 1)

                slots(act, slot)

            @block.vector
            def _(dve):
                def slot(t, r, k=None):
                    if (q := tile(t, 1)) is not None:
                        dve.wait_ge(S["hi_ready"], q + 1)
                        dve.tensor_tensor(xsT_lo[:, 1 - r, :, :], f_ps[:, 0, 0:2 * P].rearrange("p (k t) -> p k t", k=2), xsT_hi[:, 1 - r, :, :],
                                          ALU.subtract).then_inc(S["lo_ready"], 1)
                    if (q := tile(t, 0)) is not None:
                        dve.wait_ge(S["silu_ready"], q + 1)
                        dve.tensor_tensor(g[:, r, :], g[:, r, :], y_ps[:, r, 1, 0:F], ALU.mult).then_inc(S["g_ready"], 1)
                    if (q := tile(t, -1)) is not None:
                        dve.wait_ge(S["gT_hi_ready"], q + 1)
                        dve.tensor_tensor(gT_lo[:, 1 - r, 0:2, :], gT_in(0, 2), gT_hi[:, 1 - r, 0:2, :], ALU.subtract)
                        dve.tensor_tensor(gT_lo[0:96, 1 - r, 2, :], gT_in(2, 3), gT_hi[0:96, 1 - r, 2, :], ALU.subtract).then_inc(S["gT_lo_ready"], 1)
                    if (q := tile(t, -2)) is not None:
                        dve.wait_ge(S["o_ready"], q + 1)
                        if not is_int(q) or q > 1:
                            dve.wait_ge(o_stored[r], uses(q - 2, r))
                        dve.tensor_copy(o[:, r, :], o_ps[:, 0:D]).then_inc(S["o_copied"], 1)

                slots(dve, slot)

            @block.tensor
            def _(pe):
                known = {}

                def expert_of(q):
                    pe.sem_inc(passed, 1)
                    return pe.value_load(expert[0:1, bass.ds(q, 1)], min_val=0, max_val=E - 1)

                def slot(t, r, k=None):
                    now = None if tile(t, 0) is None else expert_of(tile(t, 0))
                    before = None if tile(t, -2) is None else known[k - 2] if k and k > 1 else expert_of(tile(t, -2))
                    known[k] = now
                    if (q := tile(t, 1)) is not None:
                        pe.wait_ge(tiles_loaded[1 - r], uses(q, 1 - r))
                        wait(pe, S["lo_ready"], q)
                        for kt in range(2):
                            last = pe.transpose(f_ps[:, 0, kt * P:(kt + 1) * P], xs[:, 0, 1 - r, kt * P:(kt + 1) * P], ident[:, :])
                        last.then_inc(S["xs_ps"], 1)
                    if (q := tile(t, 0)) is not None:
                        pe.wait_ge(S["lo_ready"], q + 1)
                        wait(pe, S["g_ready"], q - 1)
                        e = now
                        for half in range(2):
                            parts = [(xt, w, kt) for kt in range(2) for xt, w in ((xsT_hi, w1_hi), (xsT_lo, w1_hi), (xsT_hi, w1_lo))]
                            for m, (xt, w, kt) in enumerate(parts):
                                rhs = w[:, bass.ds(e, 1), kt, half * F:(half + 1) * F].rearrange("p o f -> p (o f)")
                                last = pe.matmul(y_ps[:, r, half, 0:F], xt[:, r, kt, :], rhs, start=(m == 0), stop=(m == 5))
                        last.then_inc(S["y_ready"], 1)
                    if (q := tile(t, -1)) is not None:
                        pe.wait_ge(S["g_ready"], q + 1)
                        wait(pe, S["gT_lo_ready"], q)
                        for f, (f0, rows) in enumerate(FT):
                            last = pe.transpose(f_ps[0:rows, 1, f * P:(f + 1) * P], g[:, 1 - r, f0:f0 + rows], ident[:, :])
                        last.then_inc(S["gT_ps"], 1)
                    if (q := tile(t, -2)) is not None:
                        pe.wait_ge(S["gT_lo_ready"], q + 1)
                        wait(pe, S["o_copied"], q)
                        e = before
                        parts = [(gg, w, f) for f in range(3) for gg, w in ((gT_hi, w2_hi), (gT_lo, w2_hi), (gT_hi, w2_lo))]
                        for m, (gg, w, f) in enumerate(parts):
                            rows = FT[f][1]
                            rhs = w[0:rows, bass.ds(e, 1), f, :].rearrange("p o f -> p (o f)")
                            last = pe.matmul(o_ps[:, 0:D], gg[0:rows, r, f, :], rhs, start=(m == 0), stop=(m == 8))
                        last.then_inc(S["o_ready"], 1)

                slots(pe, slot)

        with nc.Block() as block:
            rows_in = [[xn[:, 0], xn[:, 1]], [xT[:, :, :].rearrange("p k (a c) -> p (k a) c", a=2), rows_b]]

            @block.sync
            def _(sp):
                def slot(n, b):
                    if not is_int(n) or n > 1:
                        sp.wait_ge(S["x_stored"], 16 * (n - 1))
                    sp.dma_start(x[:, b, :, :], x_in[bass.ds(n * T, T), :].rearrange("(k p) c -> p k c", p=P)).then_inc(tiles_loaded[b], 16)
                    if not is_int(n) or n > 0:
                        store(n - 1, 1 - b)

                def store(n, b):
                    sp.wait_ge(S["x_done"], n + 1)
                    sp.dma_start(x_out[bass.ds(n * T, T), :].rearrange("(k p) c -> p k c", p=P), x[:, b, :, :]).then_inc(S["x_stored"], 16)

                batches(sp, slot)
                store(NB - 1, 1)
                sp.wait_ge(S["x_stored"], 16 * NB)

            @block.gpsimd
            def _(pool):
                def slot(n, b):
                    pool.wait_ge(S["idx_ready"], NB + n + 1)
                    if not is_int(n) or n > 1:
                        pool.wait_ge(S["x_done"], n - 1)
                    if not is_int(n):
                        pool.sem_inc(passed, 1)
                    for k in range(4):
                        for c in range(2):
                            pool.indirect_dma_start(rows_in[b][c][:, k, :], None, o_d,
                                                    bass.IndirectOffsetOnAxis(ap=idx[:, b, k, c:c + 1], axis=0)).then_inc(gathered[b], 16)

                batches(pool, slot)

            @block.vector
            def _(dve):
                def index(n, b):
                    if not is_int(n) or n > 1:
                        dve.wait_ge(S["x_done"], n - 1)
                        dve.wait_ge(gathered[b], 8 * parity_count(n, b) - 128)
                        dve.sem_inc(passed, 1)
                    dve.tensor_copy(pr[:, b, :, :], prob[:, bass.ds(4 * n, 4), :])
                    dve.tensor_copy(idx[:, b, :, :], pos[:, bass.ds(4 * n, 4), :]).then_inc(S["idx_ready"], 1)

                def add(n, b):
                    dve.wait_ge(tiles_loaded[b], 16 * (SLOTS // 2) + parity_count(n, b))
                    dve.wait_ge(gathered[b], 8 * parity_count(n, b))
                    dve.wait_ge(S["idx_ready"], NB + n + 1)
                    for c in range(2):
                        for k in range(4):
                            ins = dve.scalar_tensor_tensor(x[:, b, k, :], rows_in[b][c][:, k, :], pr[:, b, k, c:c + 1], x[:, b, k, :], ALU.mult, ALU.add)
                        if c == 0:
                            ins.then_inc(S["half"], 1)
                            dve.wait_ge(S["half"], n + 1)
                    ins.then_inc(S["x_done"], 1)

                def slot(n, b):
                    index(n, b)
                    if not is_int(n) or n > 0:
                        add(n - 1, 1 - b)

                batches(dve, slot)
                add(NB - 1, 1)


def moe_linear_phase(nc, sem, A, x_in, x_out):
    E, PAIRS = 8, 4
    DVE_AT, ACT_AT, PE_AT, LOW_AT = (3, 5, 10, 11), (4, 9, 11, 15), (9, 11, 15), 10
    N_STEPS = 4 + 3 + 5 + 3 + 15 + 4
    with ExitStack() as ctx:
        sb = lambda name, shape, dt=F32: ctx.enter_context(nc.sbuf_tensor("m1_" + name, shape, dt))
        ident = sb("ident", [P, P])
        w_hi, w_lo = (sb(f"w_{s}", [P, PAIRS, 2, 2 * D], F32R) for s in ("hi", "lo"))
        raw = sb("raw", [P, PAIRS, 2, 2 * D])
        gw = sb("gw", [P, 2, E])
        gb = sb("gb", [P, E])
        eb = sb("eb", [E, D])
        order = sb("order", [P, 4, E])
        eps = sb("eps", [P, 1])
        x = sb("x", [P, 2, 4, D])
        xn = sb("xn", [P, 4, D])
        stats, mv, rs = sb("stats", [P, 4, 6]), sb("mv", [P, 4, 2]), sb("rs", [P, 4, 4])
        xT = sb("xT", [P, 2, T])
        xT_hi, xT_lo = (sb(f"xT_{s}", [P, 2, 2, T], F32R) for s in ("hi", "lo"))
        p = sb("p", [P, 4, E])
        work, small = sb("work", [P, 4, 4, E]), sb("small", [P, 4, 4])
        comb = sb("comb", [P, 2, 4, E])
        combT = sb("combT", [E, 2, T])
        odd = sb("odd", [P, 4, D])
        odd_in = sb("odd_in", [P, PAIRS - 1, D])
        f_ps = ctx.enter_context(nc.psum_tensor("m1_f_ps", [P, 2, T], F32))
        o_ps = ctx.enter_context(nc.psum_tensor("m1_o_ps", [P, 4, 2 * D], F32))
        b_ps = ctx.enter_context(nc.psum_tensor("m1_b_ps", [P, 2, 2 * D], F32))

        names = """const_in w_in w_hi w_ready x_stored steps var_ready ln_ready rs_ready xn_ready xT_ps xT_ready xT_hi_ready xT_lo_ready
                   logits z_ready exp_ready comb_ready combT_ps combT_ready b_ready b_added o_ready acc_done const_set"""
        (const_in, w_in, w_hi_s, w_ready, x_stored, steps_s, var_ready, ln_ready, rs_ready, xn_ready, xT_ps, xT_ready, xT_hi_ready, xT_lo_ready,
         logits, z_ready, exp_ready, comb_ready, combT_ps, combT_ready, b_ready, b_added, o_ready, acc_done, const_set) = (sem("m1_" + q) for q in names.split())
        passed = sem("passed")
        odd_done, odd_added, tile_done = (sem("m1_" + q) for q in ("odd_done", "odd_added", "tile_done"))
        x_loaded = [sem(f"m1_x_loaded{r}") for r in range(2)]
        UNITS = 4 * PAIRS

        def low(pool, n, b):
            pool.wait_ge(xT_ready, n + 1)
            pool.wait_ge(xT_hi_ready, n + 1)
            if not isinstance(n, int) or n > 1:
                pool.wait_ge(o_ready, UNITS * (n - 1))
            pool.tensor_tensor(xT_lo[:, b, :, :], xT[:, :, :], xT_hi[:, b, :, :], ALU.subtract).then_inc(xT_lo_ready, 1)

        with nc.Block() as block:

            @block.sync
            def _(sp):
                sp.dma_start(x[:, 0, :, :], x_in[0:T, :].rearrange("(k p) c -> p k c", p=P)).then_inc(x_loaded[0], 16)
                for dst, src in ((ident[:, :], A["ident"]), (gw[:, :, :], A["m1_gw"]), (gb[:, :], A["m1_gb"]), (eb[:, :], A["m1_eb"]),
                                 (order[:, :, :], A["order"])):
                    sp.dma_start(dst, src).then_inc(const_in, 16)
                for e in range(PAIRS):
                    sp.dma_start(raw[:, e, :, :], A["m1_w"][e].rearrange("(k c) f -> c k f", k=2)).then_inc(w_in, 16)

                def store(n, b):
                    sp.wait_ge(tile_done, 4 * (n + 1))
                    sp.dma_start(x_out[bass.ds(n * T, T), :].rearrange("(k p) c -> p k c", p=P), x[:, b, :, :]).then_inc(x_stored, 16)

                def slot(n, b, following):
                    if isinstance(n, int) and n < 0:
                        return
                    if not (isinstance(n, int) and n == 0):
                        store(n - 1, 1 - b)
                        sp.wait_ge(x_stored, 16 * n)
                    if following:
                        n1, b1 = following
                        sp.dma_start(x[:, b1, :, :], x_in[bass.ds(n1 * T, T), :].rearrange("(k p) c -> p k c", p=P)).then_inc(x_loaded[b1], 16)

                batch_slots(sp, slot)
                store(NB - 1, 1)
                sp.wait_ge(x_stored, 16 * NB)

            @block.gpsimd
            def _(pool):
                pool.memset(eps[:, :], 1e-5).then_inc(const_set, 1)
                low(pool, 0, 0)
                for e in range(PAIRS):
                    pool.wait_ge(w_hi_s, e + 1)
                    pool.tensor_tensor(w_lo[:, e, :, :], raw[:, e, :, :], w_hi[:, e, :, :], ALU.subtract).then_inc(w_ready, 1)

                def add_odd(n, b, u):
                    k, e = u // PAIRS, u % PAIRS
                    for j in (e - 1, e):
                        if j > 0:
                            q = 4 * (PAIRS - 1) * n + (PAIRS - 1) * k + j - 1
                            pool.wait_ge(odd_done, UNITS * n + PAIRS * k + j + 1)
                            wait(pool, odd_added, q)
                            pool.tensor_tensor(odd[:, k, :], odd[:, k, :], odd_in[:, j - 1, :], ALU.add).then_inc(odd_added, 1)
                    if e == PAIRS - 1:
                        pool.wait_ge(odd_added, q + 1)
                        pool.wait_ge(acc_done, UNITS // 2 * n + 2 * (k + 1))
                        pool.tensor_tensor(x[:, b, k, :], x[:, b, k, :], odd[:, k, :], ALU.add).then_inc(tile_done, 1)

                def slot(n, b, following):
                    if isinstance(n, int) and n < 0:
                        return
                    for u in range(UNITS):
                        if u % 2:
                            add_odd(n, b, u)
                        if following and u == LOW_AT:
                            low(pool, *following)

                batch_slots(pool, slot)

            @block.scalar
            def _(act):
                act.preload_act_table_set("natural_log_exp_and_others")
                act.wait_ge(const_set, 1)

                def before(n, b, part):
                    if part == 0:
                        act.wait_ge(var_ready, n + 1)
                        wait(act, xn_ready, n)
                        act.activation(rs[:, 0, :], mv[:, :, 1], ACT.Ln, bias=eps[:, :]).then_inc(ln_ready, 1)
                        act.wait_ge(ln_ready, n + 1)
                        act.activation(rs[:, 0, :], rs[:, 0, :], ACT.Exp, scale=-0.5).then_inc(rs_ready, 1)
                    if part == 1:
                        act.wait_ge(xT_ps, n + 1)
                        wait(act, xT_lo_ready, n)
                        wait(act, logits, n)
                        if not isinstance(n, int) or n > 1:
                            act.wait_ge(o_ready, UNITS * (n - 1))
                        act.activation(xT[:, :, :], f_ps[:, :, :], ACT.Copy).then_inc(xT_ready, 1)
                        act.activation(xT_hi[:, b, :, :], f_ps[:, :, :], ACT.Copy).then_inc(xT_hi_ready, 1)
                    if part == 2:
                        act.wait_ge(z_ready, n + 1)
                        act.activation(p[:, :, :], p[:, :, :], ACT.Exp).then_inc(exp_ready, 1)
                    if part == 3:
                        act.wait_ge(combT_ps, n + 1)
                        if not isinstance(n, int) or n > 1:
                            act.wait_ge(b_ready, 2 * (n - 1))
                        act.activation(combT[:, b, :], f_ps[0:E, 0, :], ACT.Copy).then_inc(combT_ready, 1)

                def weigh_odd(n, b, u):
                    k, e = u // PAIRS, u % PAIRS
                    act.wait_ge(o_ready, UNITS * n + u + 1)
                    for a in range(2):
                        j = e - 1 + a
                        if j == 0:
                            wait(act, tile_done, 4 * (n - 1) + k + 1)
                            dst = odd[:, k, :]
                        else:
                            wait(act, odd_added, 4 * (PAIRS - 1) * n + (PAIRS - 1) * (k - 1) + j)
                            dst = odd_in[:, j - 1, :]
                        act.activation(dst, o_ps[:, u % 4, a * D:(a + 1) * D], ACT.Identity,
                                       scale=comb[:, b, k, 2 * e + a:2 * e + a + 1]).then_inc(odd_done, 1)

                def slot(n, b, following):
                    if isinstance(n, int) and n < 0:
                        for part in range(3):
                            before(0, 0, part)
                        for e in range(PAIRS):
                            if e == 0:
                                act.wait_ge(w_in, 16 * PAIRS)
                            act.activation(w_hi[:, e, :, :], raw[:, e, :, :], ACT.Copy).then_inc(w_hi_s, 1)
                        before(0, 0, 3)
                        return
                    act.wait_ge(comb_ready, n + 1)
                    for u in range(UNITS):
                        if u % 2:
                            weigh_odd(n, b, u)
                        if following and u in ACT_AT:
                            before(*following, ACT_AT.index(u))

                batch_slots(act, slot)

            @block.vector
            def _(dve):
                steps = Steps(dve, steps_s, N_STEPS)
                dve.wait_ge(const_in, 80)

                def before(n, b, part):
                    if part == 0:
                        steps.begin(n)
                        dve.wait_ge(x_loaded[b], 16 * ((n - b) // 2 + 1) if isinstance(n, int) else 8 * (n - b) + 16)
                        wait(dve, var_ready, n)
                        dve_normalise(dve, steps, passed, x[:, b], xn, stats, mv, rs, 1e-5, var_ready, rs_ready, xn_ready, n, 0)
                    if part == 1:
                        wait(dve, xT_ps, n)
                        dve_normalise(dve, steps, passed, x[:, b], xn, stats, mv, rs, 1e-5, var_ready, rs_ready, xn_ready, n, 1)
                    if part == 2:
                        z_in = f_ps[:, 0, 0:4 * E].rearrange("p (k e) -> p k e", k=4)
                        bc = lambda s: s.unsqueeze(2).broadcast_to([P, 4, E])
                        dve.wait_ge(logits, n + 1)
                        steps(dve.tensor_tensor(p[:, :, :], z_in, gb[:, :].unsqueeze(1).broadcast_to([P, 4, E]), ALU.add))
                        steps(dve.tensor_scalar(p[:, :, :], p[:, :, :], 1e-4, None, ALU.max))
                        steps(dve.tensor_reduce(small[:, 0, :], p[:, :, :], AX.X, ALU.max))
                        dve.tensor_tensor(p[:, :, :], p[:, :, :], bc(small[:, 0, :]), ALU.subtract).then_inc(z_ready, 1)
                    if part == 3:
                        bc = lambda s: s.unsqueeze(2).broadcast_to([P, 4, E])
                        dve.wait_ge(exp_ready, n + 1)
                        wait(dve, odd_done, UNITS * (n - 1))
                        mask = dve_top2(dve, steps, p[:, :, :], order[:, :, :], work, small)
                        steps(dve.scalar_tensor_tensor(work[:, 1], p[:, :, :], 0.1, mask, ALU.max, ALU.mult))
                        steps(dve.tensor_reduce(small[:, 0, :], work[:, 1], AX.X, ALU.add))
                        steps(dve.reciprocal(small[:, 1, :], small[:, 0, :]))
                        steps(dve.tensor_tensor(work[:, 1], work[:, 1], bc(small[:, 1, :]), ALU.mult))
                        dve.tensor_scalar(comb[:, b, :, :], work[:, 1], 0.5, None, ALU.mult).then_inc(comb_ready, 1)
                        assert steps.count == N_STEPS, steps.count

                def accumulate(n, b, u):
                    k, e = u // PAIRS, 2 * (u % PAIRS)
                    q = UNITS // 2 * n + u // 2
                    dve.wait_ge(o_ready, UNITS * n + u + 1)
                    if u % PAIRS == 0 and k % 2 == 0:
                        dve.wait_ge(b_ready, 2 * n + k // 2 + 1)
                        dve.tensor_tensor(x[:, b, k:k + 2, :], b_ps[:, k // 2, :].rearrange("p (a c) -> p a c", a=2), x[:, b, k:k + 2, :],
                                          ALU.add).then_inc(b_added, 1)
                        dve.wait_ge(b_added, 2 * n + k // 2 + 1)
                    else:
                        dve.wait_ge(acc_done, q)
                    for a in range(2):
                        ins = dve.scalar_tensor_tensor(x[:, b, k, :], o_ps[:, u % 4, a * D:(a + 1) * D], comb[:, b, k, e + a:e + a + 1], x[:, b, k, :],
                                                       ALU.mult, ALU.add)
                        if a == 0:
                            ins.then_inc(half_s, 1)
                            dve.wait_ge(half_s, q + 1)
                        else:
                            ins.then_inc(acc_done, 1)

                half_s = sem("m1_half_done")

                def slot(n, b, following):
                    if isinstance(n, int) and n < 0:
                        for part in range(4):
                            before(0, 0, part)
                        return
                    dve.wait_ge(comb_ready, n + 1)
                    for u in range(UNITS):
                        if u % 2 == 0:
                            accumulate(n, b, u)
                        if following and u in DVE_AT:
                            before(*following, DVE_AT.index(u))

                batch_slots(dve, slot)

            @block.tensor
            def _(pe):
                pe.wait_ge(const_in, 80)

                def before(n, b, part):
                    if part == 0:
                        pe.wait_ge(xn_ready, n + 1)
                        wait(pe, combT_ready, n)
                        for kt in range(2):
                            for k in range(4):
                                last = pe.transpose(f_ps[:, kt, k * P:(k + 1) * P], xn[:, k, kt * P:(kt + 1) * P], ident[:, :])
                        last.then_inc(xT_ps, 1)
                    if part == 1:
                        pe.wait_ge(xT_hi_ready, n + 1)
                        for k in range(4):
                            for kt in range(2):
                                last = pe.matmul(f_ps[:, 0, k * E:(k + 1) * E], xT[:, kt, k * P:(k + 1) * P], gw[:, kt, :], start=(kt == 0), stop=(kt == 1))
                        last.then_inc(logits, 1)
                    if part == 2:
                        pe.wait_ge(comb_ready, n + 1)
                        for k in range(4):
                            last = pe.transpose(f_ps[0:E, 0, k * P:(k + 1) * P], comb[:, b, k, :], ident[:, :])
                        last.then_inc(combT_ps, 1)

                def slot(n, b, following):
                    if isinstance(n, int) and n < 0:
                        for part in range(3):
                            before(0, 0, part)
                        return
                    pe.wait_ge(xT_lo_ready, n + 1)
                    pe.wait_ge(combT_ready, n + 1)
                    for u in range(UNITS):
                        k, e = u // PAIRS, u % PAIRS
                        tok = slice(k * P, (k + 1) * P)
                        if u % PAIRS == 0 and k % 2 == 0:
                            wait(pe, b_added, 2 * n + k // 2 - 1)
                            for a in range(2):
                                last = pe.matmul(b_ps[:, k // 2, a * D:(a + 1) * D], combT[:, b, (k + a) * P:(k + a + 1) * P], eb[:, :], start=True, stop=True)
                            last.then_inc(b_ready, 1)
                        if isinstance(n, int) and n == 0 and k == 0:
                            pe.wait_ge(w_ready, e + 1)
                        if u % 2:
                            wait(pe, odd_done, UNITS * n + u - 3)
                        else:
                            wait(pe, acc_done, UNITS // 2 * n + u // 2 - 1)
                        parts = [(xt, w, kt) for kt in range(2) for xt, w in ((xT_hi, w_hi), (xT_lo, w_hi), (xT_hi, w_lo))]
                        for m, (xt, w, kt) in enumerate(parts):
                            last = pe.matmul(o_ps[:, u % 4, :], xt[:, b, kt, tok], w[:, e, kt, :], start=(m == 0), stop=(m == 5))
                        last.then_inc(o_ready, 1)
                        if following and u in PE_AT:
                            before(*following, PE_AT.index(u))

                batch_slots(pe, slot)


DI = 2 * D
DS, DTR = 16, 16
ND = DI // P
NP = DS // 2

SCHEDULE = {
    0: [("load", 0), ("final", 3)], 1: [("z", 0), ("z", 1), ("ln", 0)], 2: [("dt", 1)],
    3: [("z", 2), ("z", 3), ("silu_z", 0), ("rsqrt", 0), ("ln", 1)], 4: [("out", 0), ("out", 1)], 5: [("sum", 0), ("rsqrt", 1)], 7: [("ln", 2)],
    8: [("final", 0)], 9: [("dt", 2)], 10: [("tr", 0), ("tr", 1)], 13: [("xi", 0), ("xi", 1)],
    15: [("conv", 0)], 16: [("final", 1), ("conv", 1)], 17: [("xi", 2), ("xi", 3)], 19: [("conv", 2)],
    20: [("conv", 3), ("silu_u", 0), ("split", 0), ("split", 1)], 18: [("dt", 3)], 23: [("ux", 0), ("ux", 1), ("split", 2), ("split", 3)],
    24: [("final", 2)], 26: [("ux", 2), ("ux", 3), ("xd", 0), ("bc", 0), ("bc", 1), ("bc", 2)],
    27: [("bc", 3)], 28: [("dt0", 0), ("bc", 4)], 29: [("bc", 5)], 30: [("bc", 6)], 31: [("bc", 7)],
}
NEXT = ("load", "ln", "rsqrt", "sum", "tr", "xi", "conv", "silu_u", "split", "ux", "xd", "dt0", "bc")
LAST = ("out",)
FILLS = [task for at in sorted(SCHEDULE) for task in SCHEDULE[at] if task[0] in ("out", "z", "dt", "dt0", "tr", "xi", "conv")]


def mamba_phase(nc, sem, A, x_in, x_out):
    with ExitStack() as ctx:
        sb = lambda name, shape, dt=F32: ctx.enter_context(nc.sbuf_tensor("mb_" + name, shape, dt))
        ident = sb("ident", [P, P])
        cols = sb("cols", [P, 4, 9])
        lnc = sb("lnc", [P, 2, 2])
        a_neg = sb("a_neg", [P, ND, DS])
        fix = sb("fix", [P, 3])
        diag = sb("diag", [P, ND, 4, P])
        wi_hi, wi_lo = (sb(f"wi_{s}", [P, 2, 2 * DI], F32R) for s in ("hi", "lo"))
        wo_hi, wo_lo = (sb(f"wo_{s}", [P, ND, D], F32R) for s in ("hi", "lo"))
        wx_hi, wx_lo = (sb(f"wx_{s}", [P, ND, 48], F32R) for s in ("hi", "lo"))
        wdt = sb("wdt", [DTR, DI])
        xin = sb("xin", [P, 4, D])
        res = sb("res", [P, 2, 4, D])
        xn = sb("xn", [P, 4, D])
        stats, mv, rs = sb("stats", [P, 2, 4, 6]), sb("mv", [P, 2, 4, 2]), sb("rs", [P, 2, 4, 4])
        hT_hi, hT_lo = (sb(f"hT_{s}", [P, 2, T], F32R) for s in ("hi", "lo"))
        xi = sb("xi", [P, 2, T + 3])
        u = sb("u", [P, 2, ND, T])
        u_hi, u_lo = (sb(f"u_{s}", [P, 2, T], F32R) for s in ("hi", "lo"))
        z = sb("z", [P, ND, T])
        xd = sb("xd", [DTR + 2 * DS, T])
        ex, lg = (sb(n, [P, T]) for n in ("ex", "lg"))
        dt, dtu = sb("dt", [P, 2, T]), sb("dtu", [P, 2, T])
        bbc, cbc = sb("bbc", [P, DS, T]), sb("cbc", [P, DS, T])
        raw_wi, raw_wo = bbc[:, 0:4, :].rearrange("p (k a) t -> p k (a t)", k=2), bbc[:, 4:6, :].rearrange("p a (b e) -> p (a b) e", b=2)
        raw_wx = bbc[:, 6, 0:ND * 48].rearrange("p (d e) -> p d e", d=ND)
        dbu = sb("dbu", [P, 2, 2, T])
        hc = sb("hc", [P, 2, 2, T])
        y_hi, y_lo = (sb(f"y_{s}", [P, ND, T], F32R) for s in ("hi", "lo"))
        scr = nc.dram_tensor("mb_scr", (2, 2 * DS, T), F32, kind="Internal").ap()
        da_ps = ctx.enter_context(nc.psum_tensor("mb_da_ps", [P, 2, 2, T], F32))
        y_ps = ctx.enter_context(nc.psum_tensor("mb_y_ps", [P, T], F32))
        g_ps = ctx.enter_context(nc.psum_tensor("mb_g_ps", [P, T], F32))
        f_ps = ctx.enter_context(nc.psum_tensor("mb_f_ps", [P, 2, T], F32))

        names = """const_in prep diag_set wi_scaled w_hi_done w_lo_done p_bias a_exp x_stored passed_pool ln_done ln_steps var1 rs1 xn1 var2 rs2 xn2 res_sum scr_written x_loaded
                   f_ready hT_hi_ready z_ready u_ready u_hi_ready u_lo_ready xd_ready
                   act_steps ex_ready dt_steps dt_ready dtu_ready da_ready dbu_ready scan_done hc_ready y_ready
                   y_used yg_ready y_hi_ready y_lo_ready ux_done"""
        S = {q: sem("mb_" + q) for q in names.split()}
        S["passed"] = sem("passed")
        f_used = [sem(f"mb_f_used{r}") for r in range(2)]
        bc_loaded = [sem(f"mb_bc_loaded{r}") for r in range(NP)]
        weights = ((raw_wi, wi_hi, wi_lo), (raw_wo, wo_hi, wo_lo), (raw_wx, wx_hi, wx_lo))

        def present(n, kind, i):
            if n == -1:
                return kind in NEXT
            if n == NB:
                return kind in LAST or (kind, i) == ("final", 3)
            if n == 0 and (kind in LAST or (kind, i) == ("final", 3)):
                return False
            return not (n == NB - 1 and kind in NEXT)

        def fill(n, kind, i):
            at = FILLS.index((kind, i))
            bank = at % 2

            def before(m, upto=None):
                here = [j for j, f in enumerate(FILLS[:upto]) if present(m, *f)]
                return sum(j % 2 == bank for j in here), len(here)
            if isinstance(n, int):
                parts = [before(m) for m in range(-1, n)] + [before(n, at)]
                return bank, sum(p[0] for p in parts), sum(p[1] for p in parts) + 1
            parts = [before(-1), before(0), before(1, at)]
            same, every = before(1)
            return bank, n * same + sum(p[0] for p in parts) - same, n * every + sum(p[1] for p in parts) + 1 - every

        def tasks(run, n, b, at):
            for kind, i in SCHEDULE.get(at, []):
                if present(n if isinstance(n, int) else 1, kind, i):
                    back = kind in LAST or (kind, i) == ("final", 3)
                    m, mb = (n + 1, 1 - b) if kind in NEXT else (n - 1, 1 - b) if back else (n, b)
                    run(kind, i, n, m, mb)

        def slots(eng, unit, run, lag=0, end=None):
            every = range(ND * NP)

            def slot(n, b, _):
                first = isinstance(n, int) and n < 0
                for at in every:
                    if not first:
                        unit(n, b, at // NP, at % NP)
                    if at >= lag or first:
                        tasks(run, n, b, at if first else at - lag)
                if first:
                    unit(n, b, ND, 0)
                else:
                    for at in every[ND * NP - lag:]:
                        tasks(run, n, b, at)

            batch_slots(eng, slot)
            if end:
                end()
            for at in every:
                tasks(run, NB, 0, at)

        def count(n, d, p):
            return ND * NP * n + NP * d + p

        def q_ring(p):
            return p % 2

        def used_up(eng, n, kind, i):
            bank, used, _ = fill(n, kind, i)
            eng.wait_ge(f_used[bank], used + 1)

        with nc.Block() as block:

            @block.sync
            def _(sp):
                def load(n):
                    wait(sp, S["res_sum"], n)
                    sp.dma_start(xin[:, :, :], x_in[bass.ds(n * T, T), :].rearrange("(k p) c -> p k c", p=P)).then_inc(S["x_loaded"], 16)

                load(0)
                for dst, src in ((ident[:, :], A["ident"]), (cols[:, :, 0:7], A["mb_cols"]), (lnc[:, :, :], A["mb_ln"]), (a_neg[:, :, :], A["mb_alog"]),
                                 (wdt[:, :], A["mb_wdt"]), (raw_wi, A["mb_wi"].rearrange("(k c) e -> c k e", c=P)),
                                 (raw_wo, A["mb_wo"].rearrange("(k c) e -> c k e", c=P)),
                                 (raw_wx, A["mb_wx"].rearrange("(k c) e -> c k e", c=P))):
                    sp.dma_start(dst, src).then_inc(S["const_in"], 16)

                def run(kind, i, n, m, b):
                    if (kind, i) == ("out", 1):
                        used_up(sp, n, "out", 1)
                        sp.dma_start(x_out[bass.ds(m * T, T), :].rearrange("(k p) c -> p k c", p=P), res[:, b, :, :]).then_inc(S["x_stored"], 16)
                    elif kind == "load" and not (isinstance(n, int) and n < 0):
                        load(m)
                    elif kind == "bc":
                        if i == 0:
                            sp.wait_ge(S["xd_ready"], m + 1)
                            sp.dma_start(scr[b], xd[DTR:, :]).then_inc(S["scr_written"], 16)
                            sp.wait_ge(S["scr_written"], 16 * (m + 1))
                        wait(sp, S["dbu_ready"], count(m, -1, i) + 1)
                        over = lambda row: scr[b, row:row + 2, :].unsqueeze(0).broadcast_to([P, 2, T])
                        sp.dma_start(bbc[:, 2 * i:2 * i + 2, :], over(2 * i)).then_inc(bc_loaded[i], 16)
                        wait(sp, S["hc_ready"], count(m, -1, i) + 1)
                        sp.dma_start(cbc[:, 2 * i:2 * i + 2, :], over(DS + 2 * i)).then_inc(bc_loaded[i], 16)

                slots(sp, lambda *a: None, run)
                sp.wait_ge(S["x_stored"], 16 * NB)

            @block.gpsimd
            def _(pool):
                for q, (dst, value) in enumerate(((fix[:, 0:1], 1e-5), (fix[:, 1:2], 1e-6), (fix[:, 2:3], 1.0), (xi[:, :, 0:3], 0.0))):
                    pool.memset(dst, value).then_inc(S["passed_pool"], 1)
                for j, (raw, hi, lo) in enumerate(weights):
                    pool.wait_ge(S["w_hi_done"], j + 1)
                    pool.tensor_tensor(lo[:, :, :], raw, hi[:, :, :], ALU.subtract).then_inc(S["w_lo_done"], 1)

                def unit(n, b, d, p):
                    if d == ND:
                        return
                    q = count(n, d, p)
                    if p == 0:
                        pool.wait_ge(S["dtu_ready"], ND * n + d + 1)
                    if d == 0:
                        pool.wait_ge(bc_loaded[p], 32 * (n + 1))
                    wait(pool, S["scan_done"], q - 1)
                    dtu_2 = dtu[:, d % 2, :].unsqueeze(1).broadcast_to([P, 2, T])
                    pool.tensor_tensor(dbu[:, q_ring(p), :, :], dtu_2, bbc[:, 2 * p:2 * p + 2, :], ALU.mult).then_inc(S["dbu_ready"], 1)

                def run(kind, i, n, m, b):
                    if kind in ("dt", "dt0"):
                        q = ND * m + i
                        pool.wait_ge(S["dt_ready"], q + 1)
                        pool.tensor_tensor(dtu[:, i % 2, :], dt[:, i % 2, :], u[:, b, i, :], ALU.mult).then_inc(S["dtu_ready"], 1)
                    elif kind == "final":
                        pool.wait_ge(S["y_hi_ready"], ND * m + i + 1)
                        pool.tensor_tensor(y_lo[:, i, :], z[:, i, :], y_hi[:, i, :], ALU.subtract).then_inc(S["y_lo_ready"], 1)
                    elif kind == "sum":
                        pool.wait_ge(S["xn1"], m + 1)
                        if not isinstance(n, int) or n > 0:
                            pool.wait_ge(S["x_stored"], 16 * (m - 1))
                        pool.tensor_tensor(res[:, b, :, :], xin[:, :, :], xn[:, :, :], ALU.add).then_inc(S["res_sum"], 1)

                slots(pool, unit, run, lag=3)

            @block.scalar
            def _(act):
                act.preload_act_table_set("natural_log_exp_and_others")
                act.wait_ge(S["const_in"], 16 * 8)
                act.activation(a_neg[:, :, :], a_neg[:, :, :], ACT.Exp).then_inc(S["a_exp"], 1)
                act.wait_ge(S["wi_scaled"], 2)
                for raw, hi, _ in weights:
                    act.activation(hi[:, :, :], raw, ACT.Copy).then_inc(S["w_hi_done"], 1)
                act.wait_ge(S["prep"], 2)
                act.wait_ge(S["passed_pool"], 4)

                def exps(n, d, p):
                    q = count(n, d, p)
                    if p == 0:
                        act.wait_ge(S["dt_ready"], ND * n + d + 1)
                    wait(act, S["hc_ready"], q - 1)
                    for j in range(2):
                        last = act.activation(da_ps[:, q_ring(p), j, :], dt[:, d % 2, :], ACT.Exp, scale=a_neg[:, d, 2 * p + j:2 * p + j + 1])
                    last.then_inc(S["da_ready"], 1)

                def unit(n, b, d, p):
                    if d == ND:
                        exps(0, 0, 0)
                    elif (d, p) != (ND - 1, NP - 1):
                        exps(n, d + (p + 1) // NP, (p + 1) % NP)
                    elif not (isinstance(n, int) and n == NB - 1):
                        exps(n + 1, 0, 0)

                def run(kind, i, n, m, b):
                    if kind in ("z", "tr", "xi", "conv", "dt", "dt0"):
                        bank, used, ready = fill(n, kind, i)
                    if kind == "rsqrt":
                        var, rsq, xnr = (S["var1"], S["rs1"], S["xn1"]) if i == 0 else (S["var2"], S["rs2"], S["xn2"])
                        act.wait_ge(var, m + 1)
                        wait(act, xnr, m)
                        act.activation(rs[:, i, 0, :], mv[:, i, :, 1], ACT.Ln, bias=fix[:, i:i + 1]).then_inc(S["ln_done"], 1)
                        act.wait_ge(S["ln_done"], 2 * m + i + 1)
                        act.activation(rs[:, i, 0, :], rs[:, i, 0, :], ACT.Exp, scale=-0.5).then_inc(rsq, 1)
                    elif kind == "z":
                        act.wait_ge(S["f_ready"], ready)
                        wait(act, S["y_lo_ready"], ND * (m - 1) + i + 1)
                        act.activation(z[:, i, :], f_ps[:, bank, :], ACT.Identity, bias=cols[:, i, 8:9]).then_inc(f_used[bank], 1)
                    elif kind == "tr":
                        act.wait_ge(S["f_ready"], ready)
                        act.activation(hT_hi[:, i, :], f_ps[:, bank, :], ACT.Copy).then_inc(S["hT_hi_ready"], 1)
                    elif kind == "xi":
                        act.wait_ge(S["f_ready"], ready)
                        act.activation(xi[:, i % 2, 3:], f_ps[:, bank, :], ACT.Identity, bias=cols[:, i, 7:8]).then_inc(f_used[bank], 1)
                    elif kind == "conv":
                        act.wait_ge(S["f_ready"], ready)
                        act.activation(u[:, b, i, :], f_ps[:, bank, :], ACT.Identity, bias=cols[:, i, 4:5]).then_inc(f_used[bank], 1)
                    elif kind == "silu_z":
                        used_up(act, n, "z", 2)
                        used_up(act, n, "z", 3)
                        act.activation(z[:, :, :], z[:, :, :], ACT.Silu).then_inc(S["z_ready"], 1)
                        act.preload_act_table_set("natural_log_exp_and_others")
                    elif kind == "silu_u":
                        used_up(act, n, "conv", 2)
                        used_up(act, n, "conv", 3)
                        act.activation(u[:, b, :, :], u[:, b, :, :], ACT.Silu).then_inc(S["u_ready"], 1)
                        act.preload_act_table_set("natural_log_exp_and_others")
                        act.wait_ge(S["u_ready"], m + 1)
                    elif kind == "split":
                        wait(act, S["ux_done"], ND * m + i - 1)
                        act.activation(u_hi[:, i % 2, :], u[:, b, i, :], ACT.Copy).then_inc(S["u_hi_ready"], 1)
                    elif kind == "xd":
                        act.wait_ge(S["ux_done"], ND * m + ND)
                        wait(act, S["scr_written"], 16 * m)
                        act.activation(xd[:, :], g_ps[0:48, :], ACT.Copy).then_inc(S["xd_ready"], 1)
                    elif kind in ("dt", "dt0"):
                        q = ND * m + i
                        act.wait_ge(S["f_ready"], ready)
                        wait(act, S["dt_ready"], q)
                        act.activation(ex[:, :], f_ps[:, bank, :], ACT.Abs, bias=cols[:, i, 5:6]).then_inc(S["act_steps"], 1)
                        wait(act, S["da_ready"], NP * (q - 1))
                        wait(act, S["dbu_ready"], NP * (q - 1))
                        act.activation(dt[:, i % 2, :], f_ps[:, bank, :], ACT.Relu, bias=cols[:, i, 5:6]).then_inc(f_used[bank], 1)
                        act.wait_ge(S["act_steps"], 2 * q + 1)
                        act.activation(ex[:, :], ex[:, :], ACT.Exp, scale=-1.0).then_inc(S["act_steps"], 1)
                        act.wait_ge(S["act_steps"], 2 * q + 2)
                        act.activation(dtu[:, i % 2, :], ex[:, :], ACT.Identity, bias=fix[:, 2:3])
                        act.activation(lg[:, :], ex[:, :], ACT.Ln, bias=fix[:, 2:3]).then_inc(S["ex_ready"], 1)
                    elif kind == "final":
                        act.wait_ge(S["yg_ready"], ND * m + i + 1)
                        if i == 0 and present(n if isinstance(n, int) else 1, "out", 1):
                            act.wait_ge(S["f_ready"], fill(n, "out", 1)[2])
                        act.activation(y_hi[:, i, :], z[:, i, :], ACT.Copy).then_inc(S["y_hi_ready"], 1)

                slots(act, unit, run, lag=1)

            @block.vector
            def _(dve):
                dve.wait_ge(S["const_in"], 16 * 8)
                dve.wait_ge(S["p_bias"], 1)
                dve.tensor_copy(cols[:, :, 7:9], g_ps[:, 0:8].rearrange("p (a d) -> p d a", a=2)).then_inc(S["prep"], 1)
                for kt in range(2):
                    dve.tensor_scalar(raw_wi[:, kt, :], raw_wi[:, kt, :], lnc[:, kt, 0:1], None, ALU.mult).then_inc(S["wi_scaled"], 1)
                for d in range(ND):
                    for k in range(4):
                        dve.tensor_scalar(diag[:, d, k, :], ident[:, :], cols[:, d, k:k + 1], None, ALU.mult).then_inc(S["diag_set"], 1)
                dve.wait_ge(S["a_exp"], 1)
                dve.tensor_scalar(a_neg[:, :, :], a_neg[:, :, :], -1.0, None, ALU.mult).then_inc(S["prep"], 1)
                ln_steps = Steps(dve, S["ln_steps"], 2 * 12)

                def unit(n, b, d, p):
                    if d == ND:
                        return
                    q = count(n, d, p)
                    r = q_ring(p)
                    dve.wait_ge(S["da_ready"], q + 1)
                    dve.wait_ge(S["dbu_ready"], q + 1)
                    for j in range(2):
                        last = dve.tensor_tensor_scan(da_ps[:, r, j, :], da_ps[:, r, j, :], dbu[:, r, j, :], 0.0, ALU.mult, ALU.add)
                    last.then_inc(S["scan_done"], 1)
                    if d == 0:
                        dve.wait_ge(bc_loaded[p], 32 * (n + 1))
                    wait(dve, S["y_ready"], q - 1)
                    dve.wait_ge(S["scan_done"], q + 1)
                    dve.tensor_tensor(hc[:, r, :, :], da_ps[:, r, :, :], cbc[:, 2 * p:2 * p + 2, :], ALU.mult).then_inc(S["hc_ready"], 1)
                    if p == 0:
                        if d:
                            final(n, b, d - 1)
                        elif not (isinstance(n, int) and n == 0):
                            final(n - 1, 1 - b, ND - 1)

                def final(n, b, d):
                    q = ND * n + d
                    dve.wait_ge(S["y_ready"], NP * (q + 1))
                    dve.wait_ge(S["z_ready"], n + 1)
                    dve.scalar_tensor_tensor(u[:, b, d, :], u[:, b, d, :], cols[:, d, 6:7], y_ps[:, :], ALU.mult, ALU.add).then_inc(S["y_used"], 1)
                    dve.wait_ge(S["y_used"], q + 1)
                    dve.tensor_tensor(z[:, d, :], u[:, b, d, :], z[:, d, :], ALU.mult).then_inc(S["yg_ready"], 1)

                def run(kind, i, n, m, b):
                    if kind in ("out", "tr"):
                        bank, used, ready = fill(n, kind, i)
                    if kind == "final" and isinstance(n, int) and n == NB:
                        final(m, b, i)
                    if kind == "out":
                        dve.wait_ge(S["f_ready"], ready)
                        r_2 = res[:, b, 2 * i:2 * i + 2, :]
                        dve.wait_ge(S["res_sum"], m + 1)
                        dve.tensor_tensor(r_2, f_ps[:, bank, :].rearrange("p (a c) -> p a c", a=2), r_2, ALU.add).then_inc(f_used[bank], 1)
                    elif kind == "ln":
                        if i == 0:
                            ln_steps.begin(m)
                            dve.wait_ge(S["x_loaded"], 16 * (m + 1))
                            wait(dve, S["var1"], m)
                            wait(dve, S["xn1"], m)
                            dve_normalise(dve, ln_steps, S["passed"], xin, xn, stats[:, 0], mv[:, 0], rs[:, 0], 1e-5, S["var1"], S["rs1"], S["xn1"], m, 0)
                        if i == 1:
                            if not (isinstance(n, int) and n < 0):
                                dve.wait_ge(S["f_ready"], fill(n - 1, "tr", 1)[2])
                            dve_normalise(dve, ln_steps, S["passed"], xin, xn, stats[:, 0], mv[:, 0], rs[:, 0], 1e-5, S["var1"], S["rs1"], S["xn1"], m, 1)
                            wait(dve, S["var2"], m)
                            wait(dve, S["xn2"], m)
                            dve.wait_ge(S["xn1"], m + 1)
                            dve_normalise(dve, ln_steps, S["passed"], xn, xn, stats[:, 1], mv[:, 1], rs[:, 1], 1e-6, S["var2"], S["rs2"], S["xn2"], m, 0)
                        if i == 2:
                            dve.wait_ge(S["res_sum"], m + 1)
                            dve_normalise(dve, ln_steps, S["passed"], xn, xn, stats[:, 1], mv[:, 1], rs[:, 1], 1e-6, S["var2"], S["rs2"], S["xn2"], m, 1)
                            assert ln_steps.count == 24, ln_steps.count
                    elif kind == "tr":
                        dve.wait_ge(S["hT_hi_ready"], 2 * m + i + 1)
                        dve.tensor_tensor(hT_lo[:, i, :], f_ps[:, bank, :], hT_hi[:, i, :], ALU.subtract).then_inc(f_used[bank], 1)
                    elif kind == "split":
                        dve.wait_ge(S["u_hi_ready"], ND * m + i + 1)
                        dve.tensor_tensor(u_lo[:, i % 2, :], u[:, b, i, :], u_hi[:, i % 2, :], ALU.subtract).then_inc(S["u_lo_ready"], 1)
                    elif kind in ("dt", "dt0"):
                        q = ND * m + i
                        dve.wait_ge(S["ex_ready"], q + 1)
                        w1 = dtu[:, i % 2, :]
                        dve.scalar_tensor_tensor(w1, w1, -1.0, ex[:, :], ALU.add, ALU.subtract).then_inc(S["dt_steps"], 1)
                        dve.wait_ge(S["dt_steps"], 2 * q + 1)
                        dve.tensor_tensor(lg[:, :], lg[:, :], w1, ALU.subtract).then_inc(S["dt_steps"], 1)
                        dve.wait_ge(S["dt_steps"], 2 * q + 2)
                        dve.tensor_tensor(dt[:, i % 2, :], dt[:, i % 2, :], lg[:, :], ALU.add).then_inc(S["dt_ready"], 1)

                slots(dve, unit, run, lag=2)

            @block.tensor
            def _(pe):
                pe.wait_ge(S["const_in"], 16 * 8)
                for j in range(8):
                    for kt in range(2):
                        last = pe.matmul(g_ps[:, j:j + 1], raw_wi[:, kt, j * P:(j + 1) * P], lnc[:, kt, 1:2], start=(kt == 0), stop=(kt == 1))
                last.then_inc(S["p_bias"], 1)
                pe.wait_ge(S["diag_set"], 4 * ND)
                pe.wait_ge(S["w_lo_done"], 3)
                pe.wait_ge(S["prep"], 1)

                def unit(n, b, d, p):
                    if d == ND:
                        return
                    q = count(n, d, p)
                    if p == 0:
                        wait(pe, S["y_used"], ND * n + d)
                    pe.wait_ge(S["hc_ready"], q + 1)
                    for j in range(2):
                        last = pe.matmul(y_ps[:, :], ident[:, :], hc[:, q_ring(p), j, :], start=(p == 0 and j == 0), stop=(p == NP - 1 and j == 1))
                    last.then_inc(S["y_ready"], 1)

                def run(kind, i, n, m, b):
                    if kind == "ux":
                        q = ND * m + i
                        pe.wait_ge(S["u_lo_ready"], q + 1)
                        if i == 0:
                            wait(pe, S["xd_ready"], m)
                        for k, (w, ux) in enumerate(((wx_hi, u_hi), (wx_lo, u_hi), (wx_hi, u_lo))):
                            last = pe.matmul(g_ps[0:48, :], w[:, i, :], ux[:, i % 2, :], start=(i == 0 and k == 0), stop=(i == ND - 1 and k == 2))
                        last.then_inc(S["ux_done"], 1)
                        return
                    if kind not in ("out", "z", "dt", "dt0", "tr", "xi", "conv"):
                        return
                    bank, used, ready = fill(n, kind, i)
                    out = f_ps[:, bank, :]
                    wait(pe, f_used[bank], used)
                    if kind == "out":
                        pe.wait_ge(S["y_lo_ready"], ND * m + ND)
                        for a in range(2):
                            tok = slice((2 * i + a) * P, (2 * i + a + 1) * P)
                            parts = [(yy, w, d) for d in range(ND) for yy, w in ((y_hi, wo_hi), (y_lo, wo_hi), (y_hi, wo_lo))]
                            for c, (yy, w, d) in enumerate(parts):
                                last = pe.matmul(out[:, a * D:(a + 1) * D], yy[:, d, tok], w[:, d, :], start=(c == 0), stop=(c == 3 * ND - 1))
                    elif kind in ("xi", "z"):
                        if (kind, i) == ("xi", 0):
                            used_up(pe, n, "tr", 0)
                            used_up(pe, n, "tr", 1)
                        e = slice(((kind == "z") * ND + i) * P, ((kind == "z") * ND + i + 1) * P)
                        parts = [(w, h, kt) for kt in range(2) for w, h in ((wi_hi, hT_hi), (wi_lo, hT_hi), (wi_hi, hT_lo))]
                        for c, (w, h, kt) in enumerate(parts):
                            last = pe.matmul(out, w[:, kt, e], h[:, kt, :], start=(c == 0), stop=(c == 5))
                    elif kind == "tr":
                        pe.wait_ge(S["xn2"], m + 1)
                        for a in range(4):
                            last = pe.transpose(out[:, a * P:(a + 1) * P], xn[:, a, i * P:(i + 1) * P], ident[:, :])
                    elif kind == "conv":
                        used_up(pe, n, "xi", i)
                        for c in range(4):
                            last = pe.matmul(out, diag[:, i, c, :], xi[:, i % 2, c:c + T], start=(c == 0), stop=(c == 3))
                    elif kind in ("dt", "dt0"):
                        pe.wait_ge(S["xd_ready"], m + 1)
                        last = pe.matmul(out, wdt[:, i * P:(i + 1) * P], xd[0:DTR, :], start=True, stop=True)
                    last.then_inc(S["f_ready"], 1)

                def behind(n, b, d, p):
                    if d == ND:
                        return
                    if (d, p) != (0, 0):
                        unit(n, b, (d * NP + p - 1) // NP, (p - 1) % NP)
                    elif not (isinstance(n, int) and n == 0):
                        unit(n - 1, 1 - b, ND - 1, NP - 1)

                slots(pe, behind, run, end=lambda: unit(NB - 1, 1, ND - 1, NP - 1))


def four_phases(nc, A, x4):
    x1, x2, x3 = (nc.dram_tensor(f"x{i}", (NB * T, D), F32, kind="Internal").ap() for i in (1, 2, 3))
    passed = nc.alloc_semaphore(name="passed")
    phases = ((attention_phase, (x1,)), (moe_swiglu_phase, (x1, x2)), (mamba_phase, (x2, x3)), (moe_linear_phase, (x3, x4)))
    for phase, ends in phases:
        used = []

        def sem(name):
            if name == "passed":
                return passed
            used.append(nc.alloc_semaphore(name=name))
            return used[-1]

        phase(nc, sem, A, *ends)
        if phase is not moe_linear_phase:
            nc.all_engine_barrier()
            nc.clear_and_free_semaphores(used)
            nc.all_engine_barrier()


def host_layout(a):
    c = {k: np.ascontiguousarray(np.asarray(v)) for k, v in a.items()}
    rep = lambda row: np.ascontiguousarray(np.broadcast_to(row, (P, row.size)))
    swap = np.arange(D) ^ 1
    col2 = lambda v: v.reshape(2, P).T
    cos, sin = (c[f"L0_attn_{n}"][T] for n in ("cos", "sin"))
    sign = np.where(np.arange(D) % 2 == 0, -1.0, 1.0).astype(np.float32)
    out = {"x": c["L0_attn_x"].reshape(NB * T, D), "ident": np.eye(P, dtype=np.float32)}
    for n in "qk":
        w = c[f"L0_attn_w{n}"].T
        out[f"w{n}T"], out[f"w{n}Ts"] = np.ascontiguousarray(w), np.ascontiguousarray(w[:, swap])
    out["cosb"], out["sinb"], out["signb"] = rep(np.tile(cos, NJ)), rep(np.tile(sin, NJ)), rep(sign)
    bq, bk, bv = (c[f"L0_attn_b{n}"] for n in "qkv")
    out["at_cols"] = np.ascontiguousarray(np.concatenate(
        [col2(bq), col2(bk), col2(bq[swap]), col2(bk[swap])] + [np.tile(v, P // v.size)[:, None] for v in (cos, sin, sign[:P])], axis=1))
    out["wvT"] = np.ascontiguousarray(c["L0_attn_wv"].T)
    out["bvt"] = np.ascontiguousarray(np.repeat(bv.reshape(4, 4, DK).transpose(1, 0, 2).reshape(4, 4 * DK), 32, axis=0))
    wo = np.zeros((4, 32, 4, D), np.float32)
    wo[:, :DK] = c["L0_attn_wo"].T.reshape(4, 4, DK, D).transpose(1, 2, 0, 3)
    out["wo_pad"] = wo.reshape(P, 4, D)
    out["bo_rep"] = rep(c["L0_attn_bo"])
    out["order"] = np.ascontiguousarray(np.broadcast_to(np.arange(8, 0, -1, dtype=np.float32), (P, 4, 8)))
    ones = np.ones((P, P), np.float32)
    out["tri"] = np.ascontiguousarray(np.stack([np.triu(ones, 1), ones], 1))
    out["steps_of"], out["slot_no"] = rep(P * np.arange(NT, dtype=np.float32)), np.arange(2 * NT + 8, dtype=np.float32)[None]
    out["m0_rw"] = np.ascontiguousarray(c["L0_ffn_router_weight"].reshape(2, P, 8).transpose(1, 0, 2))
    out["m1_gw"] = np.ascontiguousarray(c["L1_ffn_gate_W"].reshape(2, P, 8).transpose(1, 0, 2))
    out["m1_gb"], out["m1_eb"] = rep(c["L1_ffn_gate_b"]), c["L1_ffn_expert_b"]
    out["m1_w"] = np.ascontiguousarray(c["L1_ffn_expert_W"].reshape(4, 2, D, D).transpose(0, 2, 1, 3).reshape(4, D, 2 * D))
    m = {k[8:]: v for k, v in c.items() if k.startswith("L1_attn_")}
    inner = [*m["conv_w"][:, 0, :].T, m["conv_b"], m["b_dt"], m["Dp"]]
    out["mb_cols"] = np.ascontiguousarray(np.stack([v.reshape(4, P) for v in inner], 2).transpose(1, 0, 2))
    out["mb_ln"] = np.ascontiguousarray(np.stack([v.reshape(2, P) for v in (m["ln_g"], m["ln_b"])], 2).transpose(1, 0, 2))
    out["mb_alog"] = np.ascontiguousarray(m["A_log"].reshape(4, P, 16).transpose(1, 0, 2))
    out["mb_wdt"], out["mb_wi"], out["mb_wo"] = (np.ascontiguousarray(m[k].T) for k in ("W_dt", "W_in", "W_out"))
    out["mb_wx"] = np.ascontiguousarray(m["W_x"].T)
    out["m0_w2a"] = np.ascontiguousarray(c["L0_ffn_w2"][:, :2 * P].reshape(8, 2, P, D).transpose(0, 2, 1, 3).reshape(8, P, 2 * D))
    out["m0_w1"], out["m0_w2"] = c["L0_ffn_w1"], c["L0_ffn_w2"]
    return out


def kernel(**inputs):
    import concourse.bacc as _bacc
    from concourse.bass_utils import run_bass_kernel_spmd as _run

    arrays = host_layout(inputs)
    nc = _bacc.Bacc("TRN2", target_bir_lowering=False, num_devices=1)
    args = {name: nc.dram_tensor("in_" + name, a.shape, F32, kind="ExternalInput").ap() for name, a in arrays.items()}
    x4 = nc.dram_tensor("x4", (NB * T, D), F32, kind="ExternalOutput").ap()
    four_phases(nc, args, x4)
    r = _run(nc, [{"in_" + name: a for name, a in arrays.items()}], core_ids=[0])
    return r.results[0]["x4"].reshape(NB, T, D)
```
